# Optimizing a Trainium2 kernel written in Bass

```python
import numpy as np
import jax
import jax.numpy as jnp

def _softmax(x, axis=-1):
    return jax.nn.softmax(x, axis=axis)

def _gelu(x):
    return jax.nn.gelu(x, approximate=True)

def _silu(x):
    return jax.nn.silu(x)

def _sigmoid(x):
    return jax.nn.sigmoid(x)

def _layernorm(x, axis=-1, eps=1e-05):
    m = jnp.mean(x, axis=axis, keepdims=True)
    v = jnp.var(x, axis=axis, keepdims=True)
    return (x - m) / jnp.sqrt(v + eps)

def _scatter_add(tgt, idx, src, axis=0):
    return tgt.at[idx].add(src)

def _segment_sum(src, seg, n):
    return jax.ops.segment_sum(src, seg, n)
kernel_name = 'mk_decoder_postln_d1_seqx_r8_10f5de'

def setup_inputs(seed: int=0):
    np.random.seed(seed)
    _w = jnp.asarray

    def _rec_inputs():
        import jax
        import jax.numpy as jnp
        _rk = jax.random.key(seed)
        x = 2.818e-05 + 1 * jax.random.normal(jax.random.fold_in(_rk, 1), (16, 128, 128), jnp.float32)
        _lenS = 128 - jax.random.randint(jax.random.fold_in(_rk, 7), (16,), 0, max(1, 128 // 4) + 1, jnp.int32)
        _lenS2 = 77 - jax.random.randint(jax.random.fold_in(_rk, 8), (16,), 0, max(1, 77 // 4) + 1, jnp.int32)
        _ctx_1024P = jax.random.normal(jax.random.fold_in(_rk, 11), (16, 16, 128), jnp.float32)
        _ctx_1024c = jax.random.dirichlet(jax.random.fold_in(_rk, 511), 0.3 * jnp.ones((16,), jnp.float32), (16, 77))
        _ctx_1024t = jnp.einsum('bsk,bkd->bsd', _ctx_1024c, _ctx_1024P)
        _ctx_1024t = _ctx_1024t * jax.lax.rsqrt(jnp.mean(jnp.square(_ctx_1024t)) + 1e-12) * 0.953939
        ctx_1024 = -0.000392918 + 0.999932 * (_ctx_1024t + 0.3 * jax.random.normal(jax.random.fold_in(_rk, 611), (16, 77, 128), jnp.float32))
        return (x, ctx_1024)
    x, ctx_1024 = _rec_inputs()

    def _L0_attn_setup():
        import jax, jax.numpy as jnp
        import numpy as np
        import math
        N_HEAD = 8

        def _rope(x):
            D = x.shape[-1]
            S = x.shape[-2]
            inv_freq = 1.0 / 10000.0 ** (jnp.arange(0, D, 2, dtype=jnp.float32) / D)
            t = jnp.arange(S, dtype=jnp.float32)
            freqs = jnp.repeat(t[:, None] * inv_freq[None, :], 2, axis=-1)
            cos = jnp.cos(freqs).astype(x.dtype)
            sin = jnp.sin(freqs).astype(x.dtype)
            xp = x.reshape(*x.shape[:-1], D // 2, 2)
            rot = jnp.stack((-xp[..., 1], xp[..., 0]), axis=-1).reshape(x.shape)
            return x * cos + rot * sin

        def _row_linear(x, Wo):
            B, S, P = x.shape
            E = Wo.shape[0]
            x = jnp.swapaxes(x, 1, 2).reshape(B, S, P)
            x = jnp.einsum('bsp,ep->bse', x, Wo)
            x = x.reshape(B, E, -1)
            return jnp.swapaxes(x, 1, 2)
        key = jax.random.key(seed)
        k0, k1, k2, k3, k4 = jax.random.split(key, 5)
        B, S, E, P = (4, 256, 128, 128)
        std = 1.0 / math.sqrt(E)
        return {'emb': jax.random.normal(k0, (B, S, E), dtype=jnp.float32), 'W1': jax.random.normal(k1, (P, E), dtype=jnp.float32) * std, 'W2': jax.random.normal(k2, (P, E), dtype=jnp.float32) * std, 'W3': jax.random.normal(k3, (P, E), dtype=jnp.float32) * std, 'Wo': jax.random.normal(k4, (E, P), dtype=jnp.float32) * std}
    _L0_attn_all = _L0_attn_setup()
    _L0_attn_in = {k: v for k, v in _L0_attn_all.items() if k in ('W1', 'W2', 'W3', 'Wo')}
    del _L0_attn_all

    def _L0_xattn_setup():
        import jax, jax.numpy as jnp
        import numpy as np
        B, L, D = (8, 256, 128)
        key = jax.random.key(seed)
        k1, k2, k3 = jax.random.split(key, 3)
        enc_outputs = jax.random.normal(k1, (B, L, D), dtype=jnp.float32)
        x = jax.random.normal(k2, (B, L, D), dtype=jnp.float32)
        Wq = jax.random.normal(k3, (D, D), dtype=jnp.float32) * (1.0 / np.sqrt(D))
        return {'enc_outputs': enc_outputs, 'x': x, 'Wq': Wq}
    _L0_xattn_all = _L0_xattn_setup()
    _L0_xattn_in = {k: v for k, v in _L0_xattn_all.items() if k in ('Wq',)}
    del _L0_xattn_all

    def _L0_ffn_setup():
        import jax, jax.numpy as jnp
        import numpy as np
        B, S, H = (2, 256, 128)
        E, I = (8, 512)
        TOP_K = 2
        W_SCALE = 0.02
        key = jax.random.key(seed)
        k1, k2, k3, k4, k5 = jax.random.split(key, 5)
        return {'hidden_states': jax.random.normal(k1, (B, S, H), dtype=jnp.float32), 'gate_w': jax.random.normal(k2, (H, E), dtype=jnp.float32) * W_SCALE, 'w1s': jax.random.normal(k3, (E, H, I), dtype=jnp.float32) * W_SCALE, 'w2s': jax.random.normal(k4, (E, I, H), dtype=jnp.float32) * W_SCALE, 'w3s': jax.random.normal(k5, (E, H, I), dtype=jnp.float32) * W_SCALE}
    _L0_ffn_all = _L0_ffn_setup()
    _L0_ffn_in = {k: v for k, v in _L0_ffn_all.items() if k in ('gate_w', 'w1s', 'w2s', 'w3s')}
    del _L0_ffn_all
    return {'x': x, 'ctx_1024': ctx_1024, 'L0_attn_W1': _L0_attn_in['W1'], 'L0_attn_W2': _L0_attn_in['W2'], 'L0_attn_W3': _L0_attn_in['W3'], 'L0_attn_Wo': _L0_attn_in['Wo'], 'L0_xattn_Wq': _L0_xattn_in['Wq'], 'L0_ffn_gate_w': _L0_ffn_in['gate_w'], 'L0_ffn_w1s': _L0_ffn_in['w1s'], 'L0_ffn_w2s': _L0_ffn_in['w2s'], 'L0_ffn_w3s': _L0_ffn_in['w3s']}

def reference(x, ctx_1024, L0_attn_W1, L0_attn_W2, L0_attn_W3, L0_attn_Wo, L0_xattn_Wq, L0_ffn_gate_w, L0_ffn_w1s, L0_ffn_w2s, L0_ffn_w3s):
    import jax
    import jax.numpy as jnp

    def _L0_attn_ref(emb, W1, W2, W3, Wo):
        import jax, jax.numpy as jnp
        import numpy as np
        import math
        N_HEAD = 8

        def _rope(x):
            D = x.shape[-1]
            S = x.shape[-2]
            inv_freq = 1.0 / 10000.0 ** (jnp.arange(0, D, 2, dtype=jnp.float32) / D)
            t = jnp.arange(S, dtype=jnp.float32)
            freqs = jnp.repeat(t[:, None] * inv_freq[None, :], 2, axis=-1)
            cos = jnp.cos(freqs).astype(x.dtype)
            sin = jnp.sin(freqs).astype(x.dtype)
            xp = x.reshape(*x.shape[:-1], D // 2, 2)
            rot = jnp.stack((-xp[..., 1], xp[..., 0]), axis=-1).reshape(x.shape)
            return x * cos + rot * sin

        def _row_linear(x, Wo):
            B, S, P = x.shape
            E = Wo.shape[0]
            x = jnp.swapaxes(x, 1, 2).reshape(B, S, P)
            x = jnp.einsum('bsp,ep->bse', x, Wo)
            x = x.reshape(B, E, -1)
            return jnp.swapaxes(x, 1, 2)
        B, S, E = emb.shape
        P = W1.shape[0]
        H = N_HEAD
        D = P // H
        q = jnp.einsum('bse,pe->bsp', emb, W1).reshape(B, H, S, D)
        k = jnp.einsum('bse,pe->bsp', emb, W2).reshape(B, H, S, D)
        v = jnp.einsum('bse,pe->bsp', emb, W3).reshape(B, H, S, D)
        q = _rope(q)
        k = _rope(k)
        scores = jnp.einsum('bhqd,bhkd->bhqk', q, k).astype(jnp.float32) / math.sqrt(H)
        attn = jax.nn.softmax(scores, axis=-1).astype(v.dtype)
        out = jnp.einsum('bhqk,bhkd->bhqd', attn, v)
        out = jnp.swapaxes(out, 1, 2).reshape(B, S, P)
        return _row_linear(out, Wo)

    def _L0_xattn_ref(enc_outputs, x, Wq):
        import jax, jax.numpy as jnp
        import numpy as np
        B, L, D = (8, 256, 128)
        d_k = x.shape[-1]
        q = jnp.einsum('bld,hd->blh', x, Wq)
        k = jnp.einsum('bld,hd->blh', enc_outputs, Wq)
        v = k
        scores = jnp.einsum('bqh,bkh->bqk', q, k) / jnp.sqrt(jnp.float32(d_k))
        Lq, Lk = (scores.shape[1], scores.shape[2])
        causal = jnp.tril(jnp.ones((Lq, Lk), dtype=bool))
        scores = jnp.where(causal, scores, -jnp.inf)
        attn = jax.nn.softmax(scores, axis=-1)
        return jnp.einsum('bqk,bkh->bqh', attn, v)

    def _L0_ffn_ref(hidden_states, gate_w, w1s, w2s, w3s):
        import jax, jax.numpy as jnp
        import numpy as np
        B, S, H = (2, 256, 128)
        E, I = (8, 512)
        TOP_K = 2
        W_SCALE = 0.02
        b, s, h = hidden_states.shape
        x = hidden_states.reshape(-1, h)
        logits = x @ gate_w
        probs = jax.nn.softmax(logits.astype(jnp.float32), axis=-1)
        rw, sel = jax.lax.top_k(probs, TOP_K)
        rw = rw / jnp.sum(rw, axis=-1, keepdims=True)
        comb = jnp.sum(jax.nn.one_hot(sel, E, dtype=x.dtype) * rw[..., None].astype(x.dtype), axis=1)
        out = jnp.zeros_like(x)
        for e in range(E):
            inter = jax.nn.silu(x @ w1s[e]) * (x @ w3s[e])
            out = out + comb[:, e:e + 1] * (inter @ w2s[e])
        return out.reshape(b, s, h)
    x = _layernorm(x + _L0_attn_ref(x, L0_attn_W1, L0_attn_W2, L0_attn_W3, L0_attn_Wo), axis=-1)
    x = _layernorm(x + _L0_xattn_ref(ctx_1024, x, L0_xattn_Wq), axis=-1)
    x = _layernorm(x + _L0_ffn_ref(x, L0_ffn_gate_w, L0_ffn_w1s, L0_ffn_w2s, L0_ffn_w3s), axis=-1)
    return x

_drawn_inputs = setup_inputs


def setup_inputs(seed=0):
    import zlib

    import numpy as np

    out = dict(_drawn_inputs(seed))
    spreads = {}
    factors = {'L0_ffn_gate_w': 7.805, 'L0_ffn_w1s': 6.884, 'L0_ffn_w2s': 6.836, 'L0_ffn_w3s': 6.805}
    for name, (base, spread) in spreads.items():
        noise = np.random.default_rng([zlib.crc32(name.encode()), seed]).standard_normal(out[name].shape)
        drawn = base * np.exp(spread * noise) if base else spread * noise
        out[name] = jnp.asarray(drawn.astype(out[name].dtype))
    for name, factor in factors.items():
        out[name] = (out[name] * factor).astype(out[name].dtype)
    return out
```

```python
from contextlib import ExitStack

import numpy as np
import concourse.bass as bass
from concourse import mybir

F32 = mybir.dt.float32
BF16, F16 = mybir.dt.bfloat16, mybir.dt.float16
I32, U32 = mybir.dt.int32, mybir.dt.uint32
ALU = mybir.AluOpType
ACT = mybir.ActivationFunctionType
AXIS_X = mybir.AxisListType.X

B, S, E = 16, 128, 128
H, D = 8, 16
TL = S // H
L = 77
NE, I = 8, 512
C = I // 128
PAIRS = B // 2
EPS = 1e-5
EITHER_AT = 8
MASKED = -1e30
ROWS = B * S
SLOTS = 2 * ROWS // 128 + NE - 1
EXPERT_TILES = ROWS // 128
Y_ROWS = 2 * ROWS + SLOTS * 128
COLUMNS = {"cos": TL, "sin": TL, "ident": 128, "before": 128, "same_before": 128, "same": NE, "lower": NE * NE,
           "tile_rows": EXPERT_TILES, "iota": 128, "token": B, "spare": SLOTS}
CONST_COLS = sum(COLUMNS.values())


def shape_constants():
    cos, sin = rope_tables()
    row, col = np.arange(128)[:, None], np.arange(128)[None, :]
    e = np.arange(NE)
    parts = {
        "cos": cos, "sin": sin, "ident": row == col,
        "before": row < col,
        "same_before": (row // NE < col // NE) & (row % NE == col % NE),
        "same": row % NE == e[None, :],
        "lower": np.tile((e[None, :] < e[:, None]).reshape(1, -1), (128, 1)),
        "tile_rows": np.tile(128 * np.arange(EXPERT_TILES)[None, :], (128, 1)),
        "iota": np.tile(col, (128, 1)),
        "token": 128 * np.arange(B)[None, :] + row + 1,
        "spare": 2 * ROWS + 1 + 128 * np.arange(SLOTS)[None, :] + row,
    }
    return np.concatenate([parts[n].astype(np.float32) for n in COLUMNS], axis=1)


def rope_tables():
    inv = (1.0 / np.float32(10000.0) ** (np.arange(0, D, 2, dtype=np.float32) / np.float32(D))).astype(np.float32)
    pos = (np.arange(TL)[None, :] * H + np.arange(H)[:, None]).astype(np.float32)
    ang = pos[:, None, :] * np.repeat(inv, 2)[None, :, None]
    ang = ang.astype(np.float32).reshape(H * D, TL)
    return np.cos(ang), np.sin(ang)


def build(nc, x, ctx_in, w_q, w_k, w_v, w_o, w_x, gate_w, w1s, w2s, w3s, consts, out):
    with ExitStack() as ctx:
        def sb(name, shape, dt=F32):
            return ctx.enter_context(nc.sbuf_tensor(name, shape, dt))

        def sem(name):
            return ctx.enter_context(nc.semaphore(name))

        def two(make, name, *a):
            return [make(f"{name}{n}", *a) for n in range(2)]

        qk_dram = nc.dram_tensor("qk_dram", (2, H, D, 2 * 2 * S), F32, kind="Internal").ap()
        v_dram = nc.dram_tensor("v_dram", (2, 2, S, E), F32, kind="Internal").ap()
        y_dram = nc.dram_tensor("y_dram", (Y_ROWS, E), F32, kind="Internal").ap()
        x2_dram = nc.dram_tensor("x2_dram", (B, S, E), F32, kind="Internal").ap()

        const = sb("const", [128, CONST_COLS])
        table, at = {}, 0
        for name, width in COLUMNS.items():
            table[name] = const[:, at:at + width]
            at += width
        rope_cos, rope_sin, ident = table["cos"], table["sin"], table["ident"]
        ident16 = sb("ident16", [128, 128], BF16)
        mask16 = sb("mask16", [128, 2, L], BF16)
        exponent = sb("exponent", [128, 2])
        w_nat = sb("w_nat", [128, 5, 128])
        w_proj = sb("w_proj", [128, 5, 128])
        wo_rows = sb("wo_rows", [128, H, TL])
        wo_t = sb("wo_t", [128, 128])
        wx_t = sb("wx_t", [128, 128])
        wx_gram = sb("wx_gram", [128, 128])
        gate = sb("gate", [128, NE])
        c_rows = two(sb, "c_rows", [L, 4, 128])
        c_t = two(sb, "c_t", [128, 4 * L])
        xk_all = sb("xk_all", [L, B, 128])
        xkk_all = sb("xkk_all", [128, B * L])
        x_all = sb("x_all", [128, B, 128])
        xs = two(sb, "xs", [128, 2, 128])
        x_t = two(sb, "x_t", [128, 256])
        cos_part = two(sb, "cos_part", [128, 512])
        sin_part = two(sb, "sin_part", [128, 512])
        qk_sb = two(sb, "qk_sb", [128, 512])
        qk_t = two(sb, "qk_t", [32 + D, H, 2, S])
        q_t = two(sb, "q_t", [32 + D, H, H, TL])
        v_sb = two(sb, "v_sb", [128, 2, 128])
        v_h = two(sb, "v_h", [128, 2, H, 2 * D])
        top = two(sb, "top", [128, 4])
        s_sb = two(sb, "s_sb", [128, 4, 128])
        e_sb = two(sb, "e_sb", [128, 4, 128])
        e_t = two(sb, "e_t", [128, 4, 128])
        av_sb = two(sb, "av_sb", [128, 128])
        o_rcp = sb("o_rcp", [128, H])
        o_sb = two(sb, "o_sb", [128, 128])
        res1 = sb("res1", [128, 2, 128])
        var1, less1, shift1, var2, less2, shift2 = [sb(name, [128, 2]) for name in ("var1", "less1", "shift1", "var2", "less2", "shift2")]
        stats1, mv1, rstd1 = sb("stats1", [128, 2, 6]), sb("mv1", [128, 2, 2]), sb("rstd1", [128, 2])
        x1 = two(sb, "x1", [128, 2, 128])
        x1_t = sb("x1_t", [128, 256])
        xtop, xsum, xrcp = sb("xtop", [128, 2]), sb("xsum", [128, 2]), sb("xrcp", [128, 2])
        xs_sb = sb("xs_sb", [128, 2, L])
        xe_sb = sb("xe_sb", [128, 2, L])
        xe_t = sb("xe_t", [L, 256])
        res2 = sb("res2", [128, 2, 128])
        stats2, mv2, rstd2 = sb("stats2", [128, 2, 6]), sb("mv2", [128, 2, 2]), sb("rstd2", [128, 2])
        x2 = two(sb, "x2", [128, 2, 128])
        x2_t = sb("x2_t", [128, 256])
        logits = sb("logits", [128, B, NE])
        ones = sb("ones", [128, 128])
        l_top, l_less, prob, p_sum = sb("l_top", [128, B]), sb("l_less", [128, B, NE]), sb("prob", [128, B, NE]), sb("p_sum", [128, B])
        above, tied, rank = sb("above", [128, B, NE, NE]), sb("tied", [128, B, NE, NE]), sb("rank", [128, B, NE])
        chosen = [sb(name, [128, B, NE]) for name in ("first_choice", "second_choice")]
        either = sb("either", [128, B, NE])
        totals = sb("totals", [128, 128])
        more_rows, tiles, tiles_before = sb("more_rows", [128, NE, EXPERT_TILES]), sb("tiles", [128, NE]), sb("tiles_before", [128, NE, NE])
        start, start_rows, tile_end = sb("start", [128, NE]), sb("start_rows", [128, NE]), sb("tile_end", [128, NE])
        past, expert_f, expert_of = sb("past", [128, SLOTS, NE]), sb("expert_f", [128, SLOTS]), sb("expert_of", [128, SLOTS], I32)
        place, product = sb("place", [128, B, NE]), [sb(f"product{n}", [128, B, NE]) for n in range(4)]
        dest, dest_i = sb("dest", [128, 2, B]), sb("dest_i", [128, 2, B], I32)
        dest_tile_i, dest_row_i = sb("dest_tile_i", [128, 2, B], I32), sb("dest_row_i", [128, 2, B], I32)
        dest_tile, dest_row = sb("dest_tile", [128, 2, B]), sb("dest_row", [128, 2, B])
        share, share_sum = sb("share", [128, 2, B]), sb("share_sum", [128, B])
        row_is = sb("row_is", [128, 4, 128], F16)
        tile_is = sb("tile_is", [128, 4, SLOTS], F16)
        taken, is_second, is_empty = sb("taken", [128, 2, SLOTS]), sb("is_second", [128, SLOTS]), sb("is_empty", [128, SLOTS])
        number, number_in, number_out = sb("number", [128, SLOTS]), sb("number_in", [128, SLOTS]), sb("number_out", [128, SLOTS])
        from_row, to_row = sb("from_row", [128, SLOTS], U32), sb("to_row", [128, SLOTS], U32)
        from_now, to_now = two(sb, "from_now", [128, 1], U32), two(sb, "to_now", [128, 1], U32)
        w1_sb, w3_sb = sb("w1_sb", [128, NE, I]), sb("w3_sb", [128, NE, I])
        w2_sb = sb("w2_sb", [128, NE, C, 128])
        xg = two(sb, "xg", [128, 128])
        xg_t = two(sb, "xg_t", [128, 128])
        gated, inner = two(sb, "gated", [128, I]), two(sb, "inner", [128, I])
        inner_t = two(sb, "inner_t", [128, C, 128])
        y_sb = two(sb, "y_sb", [128, 128])
        y_rows = two(sb, "y_rows", [128, 2, 2, 128])
        x2_rows = two(sb, "x2_rows", [128, 2, 128])
        res3 = two(sb, "res3", [128, 2, 128])
        stats3, mv3 = two(sb, "stats3", [128, 2, 6]), two(sb, "mv3", [128, 2, 2])
        less3 = two(sb, "less3", [128, 2])
        var3, rstd3, shift3 = two(sb, "var3", [128, 2]), two(sb, "rstd3", [128, 2]), two(sb, "shift3", [128, 2])
        out_rows = two(sb, "out_rows", [128, 2, 128])

        bank = [ctx.enter_context(nc.psum_tensor(f"bank{n}", [128, 512], F32)) for n in range(8)]
        SCORE = bank[0:2]
        TURN = bank[2:4]
        PROJ, PROJ_ROT, MIX, OUTS = bank[4:8]
        MIX_A, MIX_B = MIX[:, 0:256], MIX[:, 256:512]
        AV = OUTS[:, 0:128]
        AV_T = [PROJ[:, 256:512], PROJ_ROT[:, 256:512]]
        Y = [PROJ[:, 0:128], PROJ_ROT[:, 0:128]]
        LOGITS = PROJ[:, 128:128 + 2 * NE]
        TOTAL, PLACE, COUNT, TABLE = bank[0][:, 0:128], bank[1][:, 0:128], bank[2][:, 0:NE], bank[3][:, 0:2 * SLOTS]
        HID1, HID3, INNER_T, XG_T, Y_SLOT = bank[0:2], bank[2:4], bank[4:6], bank[6][:, 0:128], bank[7][:, 0:128]

        pool_step1, pool_step2 = sem("pool_step1"), sem("pool_step2")
        const_in, w_in, gate_in = sem("const_in"), sem("w_in"), sem("gate_in")
        consts_made, ones_made, wo_ordered = sem("consts_made"), sem("ones_made"), sem("wo_ordered")
        w_turned, w_copied = sem("w_turned"), sem("w_copied")
        c_in = two(sem, "c_in")
        c_turned, c_copied, c_made, c_kept = sem("c_turned"), sem("c_copied"), sem("c_made"), sem("c_kept")
        x_all_in, x_in = sem("x_all_in"), two(sem, "x_in")
        xt_ps, xt_sb = sem("xt_ps"), sem("xt_sb")
        qk_ps, v_ps, rope_parts, roped, v_rows = sem("qk_ps"), sem("v_ps"), sem("rope_parts"), sem("roped"), sem("v_rows")
        qk_stored, qk_placed, q_ordered = two(sem, "qk_stored"), two(sem, "qk_placed"), sem("q_ordered")
        v_stored, v_placed = two(sem, "v_stored"), two(sem, "v_placed")
        score_ps, top_found, score_sub, exped = sem("score_ps"), sem("top_found"), sem("score_sub"), sem("exped")
        et_ps, et_sb, av_ps, rcp_made, o_made = sem("et_ps"), sem("et_sb"), sem("av_ps"), sem("rcp_made"), sem("o_made")
        av_copied, avt_ps = sem("av_copied"), sem("avt_ps")
        y_ps, y_added, stats1_made, mv1_made, rstd1_made, x1_made = (
            sem("y_ps"), sem("y_added"), sem("stats1_made"), sem("mv1_made"), sem("rstd1_made"), sem("x1_made"))
        x1t_ps, x1t_sb, xscore_ps, xtop_found, xscore_sub = sem("x1t_ps"), sem("x1t_sb"), sem("xscore_ps"), sem("xtop_found"), sem("xscore_sub")
        xexped, xet_ps, xet_sb, xo_ps, xsum_step = sem("xexped"), sem("xet_ps"), sem("xet_sb"), sem("xo_ps"), sem("xsum_step")
        res2_made, stats2_made, mv2_made, rstd2_made, x2_made = (
            sem("res2_made"), sem("stats2_made"), sem("mv2_made"), sem("rstd2_made"), sem("x2_made"))
        x2t_ps, x2t_sb, logit_ps, logit_sb = sem("x2t_ps"), sem("x2t_sb"), sem("logit_ps"), sem("logit_sb")
        x2_stored = two(sem, "x2_stored")
        route_step, route_exp, total_ps, totals_sb, place_ps = sem("route_step"), sem("route_exp"), sem("total_ps"), sem("totals_sb"), sem("place_ps")
        hot_made, hot_used, table_ps, lists_made, ones_set = sem("hot_made"), sem("hot_used"), sem("table_ps"), sem("lists_made"), sem("ones_set")
        experts_in, from_copied, to_copied = sem("experts_in"), sem("from_copied"), sem("to_copied")
        gathered, scattered = two(sem, "gathered"), two(sem, "scattered")
        xgt_ps, xgt_sb, hid1_ps, hid3_ps, gated_made, inner_made = (
            sem("xgt_ps"), sem("xgt_sb"), sem("hid1_ps"), sem("hid3_ps"), sem("gated_made"), sem("inner_made"))
        innert_ps, innert_sb, yslot_ps, yslot_sb = sem("innert_ps"), sem("innert_sb"), sem("yslot_ps"), sem("yslot_sb")
        rows_in = two(sem, "rows_in")
        weighed, res3_made, stats3_made, mv3_made, pool_step3, rstd3_made, out_made = (
            sem("weighed"), sem("res3_made"), sem("stats3_made"), sem("mv3_made"), sem("pool_step3"), sem("rstd3_made"), sem("out_made"))
        out_stored = two(sem, "out_stored")

        waits_met = {e.engine: sem(f"waits_met_{n}") for n, e in enumerate((nc.sync, nc.vector, nc.gpsimd))}

        def wait_alone(engine, semaphore, value):
            engine.wait_ge(semaphore, value)
            engine.sem_inc(waits_met[engine.engine], 1)

        block = ctx.enter_context(nc.Block())

        @block.sync
        def _(sp):
            sp.dma_start(const[:, :], consts).then_inc(const_in, 16)
            for n, w in enumerate((w_q, w_k, w_v, w_o, w_x)):
                sp.dma_start(w_nat[:, n, :], w).then_inc(w_in, 16)

            def load_context(u, slot):
                sp.dma_start(c_rows[slot][:, :, :], ctx_in[bass.ds(4 * u, 4)].rearrange("b l e -> l b e")).then_inc(c_in[slot], 16)

            def load_x_all():
                sp.dma_start(x_all[:, :, :], x.rearrange("b t e -> t b e")).then_inc(x_all_in, 16)

            def load_x(n, slot):
                sp.dma_start(xs[slot][:, :, :], x[bass.ds(2 * n, 2)].rearrange("b t e -> t b e")).then_inc(x_in[slot], 16)

            load_context(0, 0)
            load_x(0, 0)
            load_context(1, 1)
            sp.dma_start(gate[:, :], gate_w).then_inc(gate_in, 16)
            load_x(1, 1)
            load_x_all()
            for u in range(2, 4):
                sp.wait_ge(c_turned, u - 1)
                load_context(u, u % 2)

            def rearrange(n, slot, k):
                wait_alone(sp, roped, n + 1)
                if k >= 1:
                    wait_alone(sp, qk_placed[slot], 32 * k)
                sp.dma_start(qk_dram[slot].rearrange("j d t -> (j d) t"), qk_sb[slot][:, :]).then_inc(qk_stored[slot], 16)
                wait_alone(sp, v_rows, n + 1)
                if k >= 1:
                    wait_alone(sp, v_placed[slot], 16 * H * k)
                sp.dma_start(v_dram[slot].rearrange("b t c -> t b c"), v_sb[slot][:, :, :]).then_inc(v_stored[slot], 16)
                wait_alone(sp, qk_stored[slot], 16 * k + 16)
                if k >= 1:
                    wait_alone(sp, score_ps, 4 * (n - 1))
                else:
                    wait_alone(sp, ones_made, 4)
                for b in range(2):
                    sp.dma_start(qk_t[slot][32 * b:32 * b + D, :, :, :].rearrange("d j w t -> d j (w t)"),
                                 qk_dram[slot][:, :, b * 256:(b + 1) * 256].rearrange("j d t -> d j t")).then_inc(qk_placed[slot], 16)
                wait_alone(sp, v_stored[slot], 16 * k + 16)
                if k >= 1:
                    wait_alone(sp, av_ps, 4 * (n - 1))
                for j in range(H):
                    sp.dma_start(v_h[slot][j * TL:(j + 1) * TL, :, :, 0:D],
                                 v_dram[slot][:, :, j * D:(j + 1) * D].rearrange("b (h t) d -> t b h d", h=H)).then_inc(v_placed[slot], 16)

            def store_x2(u, slot):
                wait_alone(sp, x2_made, 2 * u + 2)
                sp.dma_start(x2_dram[bass.ds(2 * u, 2)].rearrange("b t e -> t b e"), x2[slot][:, :, :]).then_inc(x2_stored[slot], 16)

            rearrange(0, 0, 0)
            sp.dma_start(w1_sb[:, :, :], w1s.rearrange("e h i -> h e i")).then_inc(experts_in, 16)
            sp.dma_start(w3_sb[:, :, :], w3s.rearrange("e h i -> h e i")).then_inc(experts_in, 16)
            sp.dma_start(w2_sb[:, :, :, :], w2s.rearrange("e (c p) h -> p e c h", c=C)).then_inc(experts_in, 16)

            def pair(u, slot, k, age, has_next, has_after):
                if has_after:
                    wait_alone(sp, xt_ps, u + 1)
                    load_x(u + 2, slot)
                if age >= 2:
                    store_x2(u - 2, slot)
                if has_next:
                    rearrange(u + 1, 1 - slot, k + slot)

            pair(0, 0, 0, 0, True, True)
            pair(1, 1, 0, 1, True, True)
            with sp.Fori(0, 2) as i:
                pair(2 * i + 2, 0, i + 1, 2, True, True)
                pair(2 * i + 3, 1, i + 1, 3, True, True)
            pair(6, 0, 3, 6, True, False)
            pair(7, 1, 3, 7, False, False)
            store_x2(6, 0)
            store_x2(7, 1)
            sp.wait_ge(x2_stored[0], 16 * 4)
            sp.wait_ge(x2_stored[1], 16 * 4)
            def load_rows(u, slot, k):
                if k is not None:
                    wait_alone(sp, res3_made, 2 * (u - 1))
                for choice in range(2):
                    sp.dma_start(y_rows[slot][:, choice, :, :], y_dram[bass.ds(2 * S * u + choice * ROWS, 2 * S), :].rearrange("(b t) e -> t b e", b=2))\
                      .then_inc(rows_in[slot], 16)
                sp.dma_start(x2_rows[slot][:, :, :], x2_dram[bass.ds(2 * u, 2)].rearrange("b t e -> t b e")).then_inc(rows_in[slot], 16)

            def store_rows(u, slot):
                wait_alone(sp, out_made, 2 * u + 2)
                sp.dma_start(out[bass.ds(2 * u, 2)].rearrange("b t e -> t b e"), out_rows[slot][:, :, :]).then_inc(out_stored[slot], 16)

            sp.wait_ge(scattered[0], 16 * ((SLOTS + 1) // 2))
            sp.wait_ge(scattered[1], 16 * (SLOTS // 2))
            load_rows(0, 0, None)
            load_rows(1, 1, None)
            with sp.Fori(0, PAIRS // 2 - 1) as i:
                for slot in range(2):
                    load_rows(2 * i + 2 + slot, slot, 0)
                    store_rows(2 * i + slot, slot)
            store_rows(PAIRS - 2, 0)
            store_rows(PAIRS - 1, 1)
            sp.wait_ge(out_stored[0], 16 * PAIRS // 2)
            sp.wait_ge(out_stored[1], 16 * PAIRS // 2)

        @block.tensor
        def _(pe):
            pe.wait_ge(const_in, 16)
            pe.wait_ge(w_in, 80)
            for n in range(3):
                mm = pe.transpose(TURN[0][:, n * 128:(n + 1) * 128], w_nat[:, n, :], ident)
            pe.wait_ge(wo_ordered, 1)
            pe.transpose(TURN[1][:, 0:128], wo_rows[:, :, :].rearrange("e j t -> e (j t)"), ident)
            pe.transpose(TURN[1][:, 128:256], w_nat[:, 4, :], ident)
            pe.matmul(TURN[1][:, 256:384], w_nat[:, 4, :], w_nat[:, 4, :], start=True, stop=True).then_inc(w_turned, 1)
            pe.wait_ge(w_copied, 2)

            def context(u, slot, m):
                pe.wait_ge(c_in[slot], 16 * m + 16)
                for b in range(4):
                    mm = pe.transpose(SCORE[slot][:, b * L:(b + 1) * L], c_rows[slot][:, b, :], ident[0:L, 0:L])
                mm.then_inc(c_turned, 1)
                pe.wait_ge(c_copied, u + 1)
                if u >= 1:
                    pe.wait_ge(c_kept, 2 * u)
                for b in range(4):
                    pe.matmul(TURN[0][0:L, b * 128:(b + 1) * 128], c_t[slot][:, b * L:(b + 1) * L], wx_t[:, :], start=True, stop=True)
                pe.matmul(TURN[1][:, 0:4 * L], wx_gram[:, :], c_t[slot][:, :], start=True, stop=True).then_inc(c_made, 1)

            for u in range(4):
                context(u, u % 2, u // 2)
            pe.wait_ge(c_kept, 8)

            def turn_x(n, slot, k, first):
                if first:
                    if n >= 1:
                        pe.wait_ge(v_rows, n)
                else:
                    pe.wait_ge(res2_made, 2 * (n - 2))
                pe.wait_ge(x_in[slot], 16 * k + 16)
                for b in range(2):
                    mm = pe.transpose(MIX_A[:, b * 128:(b + 1) * 128], xs[slot][:, b, :], ident)
                mm.then_inc(xt_ps, 1)

            def project_qk(n, slot, age):
                pe.wait_ge(xt_sb, n + 1)
                if age >= 1:
                    pe.wait_ge(y_added, 2 * (n - 1))
                if age >= 3:
                    pe.wait_ge(logit_sb, n - 3)
                for to, w in ((PROJ[:, 0:256], 0), (PROJ[:, 256:512], 2), (PROJ_ROT[:, 0:256], 1), (PROJ_ROT[:, 256:512], 3)):
                    mm = pe.matmul(to, w_proj[:, w, :], x_t[slot][:, :], start=True, stop=True)
                mm.then_inc(qk_ps, 1)

            def project_v(n, slot):
                for b in range(2):
                    mm = pe.matmul(MIX_B[:, b * 128:(b + 1) * 128], x_t[slot][:, b * 128:(b + 1) * 128], w_proj[:, 4, :], start=True, stop=True)
                mm.then_inc(v_ps, 1)

            def scores(u, slot, k, g, first):
                G = 4 * u + g
                if g == 0:
                    pe.wait_ge(qk_placed[slot], 32 * k + 32)
                    pe.wait_ge(q_ordered, u + 1)
                if not (first and g < 2):
                    pe.wait_ge(score_sub, G - 1)
                for h in range(4):
                    head, rows = (g % 2) * 4 + h, slice(32 * (g // 2), 32 * (g // 2) + D)
                    mm = pe.matmul(SCORE[g % 2][:, h * 128:(h + 1) * 128], q_t[slot][rows, head, :, :].rearrange("d j t -> d (j t)"),
                                   qk_t[slot][rows, :, 1, head * TL:(head + 1) * TL], start=True, stop=True)
                mm.then_inc(score_ps, 1)

            def turn_e(u, g, first):
                G = 4 * u + g
                pe.wait_ge(exped, G + 1)
                if not (first and g < 2):
                    pe.wait_ge(et_sb, G - 1)
                for h in range(4):
                    mm = pe.transpose(TURN[g % 2][:, h * 128:(h + 1) * 128], e_sb[g % 2][:, h, :], ident)
                mm.then_inc(et_ps, 1)

            def times_v(u, slot, k, g, first):
                G, b = 4 * u + g, g // 2
                if g == 0:
                    pe.wait_ge(v_placed[slot], 16 * H * (k + 1))
                pe.wait_ge(et_sb, G + 1)
                if not (first and g == 0):
                    pe.wait_ge(av_copied, G)
                for h in range(4):
                    mm = pe.matmul(AV[32 * h:32 * (h + 1), :], v_h[slot][:, b, (g % 2) * 4 + h, :], e_t[g % 2][:, h, :], start=True, stop=True)
                mm.then_inc(av_ps, 1)

            def turn_av(u, g, projected=None, last=False):
                G = 4 * u + g
                if g == 0:
                    pe.wait_ge(rope_parts, 2 * projected)
                    if last:
                        pe.wait_ge(y_added, 2 * u)
                        pe.wait_ge(logit_sb, u - 2)
                pe.wait_ge(av_copied, G + 1)
                pe.transpose(AV_T[g // 2][:, 128 * (g % 2):128 * (g % 2 + 1)], av_sb[g % 2][:, :], ident).then_inc(avt_ps, 1)

            def mix_rows(u, b):
                pe.wait_ge(o_made, 2 * u + b + 1)
                pe.matmul(Y[b], wo_t[:, :], o_sb[b][:, :], start=True, stop=True).then_inc(y_ps, 1)

            def cross_turn(u, slot, rows_of_v, turned):
                pe.wait_ge(v_rows, rows_of_v)
                if turned is not None:
                    pe.wait_ge(x2t_sb, turned)
                pe.wait_ge(x1_made, 2 * u + 2)
                for b in range(2):
                    mm = pe.transpose(MIX_A[:, b * 128:(b + 1) * 128], x1[slot][:, b, :], ident)
                mm.then_inc(x1t_ps, 1)

            def cross_scores(u):
                pe.wait_ge(x1t_sb, u + 1)
                for b in range(2):
                    to = MIX_B[:, b * L:(b + 1) * L]
                    pe.matmul(to, x1_t[:, b * 128:(b + 1) * 128], xkk_all[:, bass.ds((2 * u + b) * L, L)], start=True, stop=False)
                    mm = pe.matmul(to, ident16[:, :], mask16[:, b, :], start=False, stop=True)
                mm.then_inc(xscore_ps, 1)

            def cross_turn_e(u):
                pe.wait_ge(xexped, u + 1)
                for b in range(2):
                    mm = pe.transpose(MIX_A[0:L, b * 128:(b + 1) * 128], xe_sb[:, b, :], ident)
                mm.then_inc(xet_ps, 1)

            def cross_times_v(u):
                pe.wait_ge(xet_sb, u + 1)
                for b in range(2):
                    mm = pe.matmul(MIX_B[:, b * 128:(b + 1) * 128], xe_t[:, b * 128:(b + 1) * 128],
                                   xk_all[:, bass.ds(2 * u + b, 1), :].rearrange("l b e -> l (b e)"), start=True, stop=True)
                mm.then_inc(xo_ps, 1)

            def turn_x2(u, slot, rows_of_v, last=False):
                pe.wait_ge(v_rows, rows_of_v)
                if last:
                    pe.wait_ge(res2_made, 2 * u + 2)
                pe.wait_ge(x2_made, 2 * u + 2)
                for b in range(2):
                    mm = pe.transpose(MIX_A[:, b * 128:(b + 1) * 128], x2[slot][:, b, :], ident)
                mm.then_inc(x2t_ps, 1)

            def route(u, rows_added):
                pe.wait_ge(x2t_sb, u + 1)
                pe.wait_ge(y_added, rows_added)
                for b in range(2):
                    mm = pe.matmul(LOGITS[:, b * NE:(b + 1) * NE], x2_t[:, b * 128:(b + 1) * 128], gate[:, :], start=True, stop=True)
                mm.then_inc(logit_ps, 1)

            turn_x(0, 0, 0, True)
            project_qk(0, 0, 0)
            project_v(0, 0)
            pe.wait_ge(gate_in, 16)

            def pair(u, slot, k, age, has_next):
                first = age == 0
                scores(u, slot, k, 0, first)
                if age >= 1:
                    turn_av(u - 1, 3)
                if has_next:
                    turn_x(u + 1, 1 - slot, k + slot, age < 2)
                scores(u, slot, k, 1, first)
                if age >= 1:
                    mix_rows(u - 1, 1)
                if has_next:
                    project_qk(u + 1, 1 - slot, age)
                turn_e(u, 0, first)
                if has_next:
                    project_v(u + 1, 1 - slot)
                if age >= 2:
                    turn_x2(u - 2, slot, u + 2 if has_next else u + 1, not has_next)
                scores(u, slot, k, 2, first)
                if age >= 1:
                    cross_turn(u - 1, 1 - slot, u + 2 if has_next else u + 1, None if age < 2 else u - 1)
                turn_e(u, 1, first)
                times_v(u, slot, k, 0, first)
                if age >= 1:
                    cross_scores(u - 1)
                scores(u, slot, k, 3, first)
                turn_e(u, 2, first)
                turn_av(u, 0, u + 2 if has_next else u + 1, not has_next)
                times_v(u, slot, k, 1, first)
                if age >= 1:
                    cross_turn_e(u - 1)
                turn_e(u, 3, first)
                turn_av(u, 1)
                times_v(u, slot, k, 2, first)
                if age >= 1:
                    cross_times_v(u - 1)
                mix_rows(u, 0)
                turn_av(u, 2)
                times_v(u, slot, k, 3, first)
                if age >= 2:
                    route(u - 2, 2 * u + 1)

            pair(0, 0, 0, 0, True)
            pair(1, 1, 0, 1, True)
            with pe.Fori(0, 2) as i:
                pair(2 * i + 2, 0, i + 1, 2, True)
                pair(2 * i + 3, 1, i + 1, 3, True)
            pair(6, 0, 3, 6, True)
            pair(7, 1, 3, 7, False)
            turn_av(7, 3)
            mix_rows(7, 1)
            turn_x2(6, 0, 8, True)
            cross_turn(7, 1, 8, 7)
            cross_scores(7)
            cross_turn_e(7)
            cross_times_v(7)
            route(6, 2 * PAIRS)
            turn_x2(7, 1, 8, True)
            pe.wait_ge(logit_sb, PAIRS - 1)
            route(7, 2 * PAIRS)

            pe.wait_ge(ones_set, 1)
            pe.wait_ge(route_step, EITHER_AT)
            chosen_cols = either[:, :, :].rearrange("t b e -> t (b e)")
            pe.matmul(TOTAL, chosen_cols, ones[:, :], start=True, stop=True).then_inc(total_ps, 1)
            pe.matmul(PLACE, table["before"], chosen_cols, start=True, stop=False)
            pe.wait_ge(totals_sb, 1)
            pe.matmul(PLACE, totals[:, :], table["same_before"], start=False, stop=True)
            pe.matmul(COUNT, totals[:, :], table["same"], start=True, stop=True).then_inc(place_ps, 1)
            for choice in range(2):
                for b in range(B):
                    n = choice * B + b
                    pe.wait_ge(hot_made, 2 * n + 2)
                    mm = pe.matmul(TABLE[:, choice * SLOTS:(choice + 1) * SLOTS], row_is[:, n % 4, :], tile_is[:, n % 4, :],
                                   start=(b == 0), stop=(b == B - 1))
                    mm.then_inc(hot_used, 1)

            def turn_rows(s, slot, k):
                pe.wait_ge(gathered[slot], 16 * k + 16)
                pe.transpose(XG_T, xg[slot][:, :], ident).then_inc(xgt_ps, 1)

            def hidden(s, slot, expert, to, w_sb, done, first):
                mm = pe.matmul(to[slot][:, :], xg_t[slot][:, :], w_sb[:, bass.ds(expert, 1), :].rearrange("h a i -> h (a i)"), start=True, stop=True)
                mm.then_inc(done, 1)

            def down(s, slot, expert, first):
                pe.wait_ge(innert_sb, s + 1)
                if not first:
                    pe.wait_ge(yslot_sb, s)
                for c in range(C):
                    mm = pe.matmul(Y_SLOT, inner_t[slot][:, c, :], w2_sb[:, bass.ds(expert, 1), c, :].rearrange("i a h -> i (a h)"),
                                   start=(c == 0), stop=(c == C - 1))
                mm.then_inc(yslot_ps, 1)

            def turn_inner(s, slot, first):
                pe.wait_ge(inner_made, s + 1)
                if not first:
                    pe.wait_ge(innert_sb, s - 1)
                for c in range(C):
                    mm = pe.transpose(INNER_T[slot][:, c * 128:(c + 1) * 128], inner[slot][:, c * 128:(c + 1) * 128], ident)
                mm.then_inc(innert_ps, 1)

            def tile(s, slot, k, age, has_next):
                expert = pe.value_load(expert_of[0:1, bass.ds(s, 1)], min_val=0, max_val=NE - 1)
                pe.wait_ge(xgt_sb, s + 1)
                if age >= 2:
                    pe.wait_ge(gated_made, s - 1)
                hidden(s, slot, expert, HID1, w1_sb, hid1_ps, age < 2)
                if has_next:
                    turn_rows(s + 1, 1 - slot, k + slot)
                if age >= 2:
                    pe.wait_ge(inner_made, s - 1)
                hidden(s, slot, expert, HID3, w3_sb, hid3_ps, age < 2)
                if age >= 1:
                    before = pe.value_load(expert_of[0:1, bass.ds(s - 1, 1)], min_val=0, max_val=NE - 1)
                    down(s - 1, 1 - slot, before, age < 2)
                turn_inner(s, slot, age < 2)

            pe.wait_ge(lists_made, 1)
            pe.wait_ge(experts_in, 48)
            turn_rows(0, 0, 0)
            tile(0, 0, 0, 0, True)
            tile(1, 1, 0, 1, True)
            with pe.Fori(0, (SLOTS - 3) // 2) as i:
                tile(2 * i + 2, 0, i + 1, 2, True)
                tile(2 * i + 3, 1, i + 1, 3, True)
            tile(SLOTS - 1, 0, (SLOTS - 1) // 2, 2, False)
            down(SLOTS - 1, 0, pe.value_load(expert_of[0:1, SLOTS - 1:SLOTS], min_val=0, max_val=NE - 1), False)

        @block.scalar
        def _(act):
            act.wait_ge(w_turned, 1)
            act.copy(wo_t[:, :], TURN[1][:, 0:128])
            act.copy(wx_t[:, :], TURN[1][:, 128:256])
            act.copy(wx_gram[:, :], TURN[1][:, 256:384]).then_inc(w_copied, 1)

            def context(u, slot):
                act.wait_ge(c_turned, u + 1)
                act.copy(c_t[slot][:, :], SCORE[slot][:, 0:4 * L]).then_inc(c_copied, 1)
                act.wait_ge(c_made, u + 1)
                act.copy(xk_all[:, bass.ds(4 * u, 4), :], TURN[0][0:L, :].rearrange("l (b e) -> l b e", b=4)).then_inc(c_kept, 1)

            for u in range(4):
                context(u, u % 2)

            def copy_x_t(n, slot):
                act.wait_ge(xt_ps, n + 1)
                act.copy(x_t[slot][:, :], MIX_A).then_inc(xt_sb, 1)

            def copy_v(n, slot, k):
                act.wait_ge(v_ps, n + 1)
                if k is not None:
                    act.wait_ge(v_stored[slot], 16 * k)
                act.copy(v_sb[slot][:, :, :], MIX_B.rearrange("t (b c) -> t b c", b=2)).then_inc(v_rows, 1)

            def exp(u, g, first):
                G = 4 * u + g
                act.wait_ge(score_sub, G + 1)
                if not (first and g < 2):
                    act.wait_ge(et_ps, G - 1)
                act.activation(e_sb[g % 2][:, :, :], s_sb[g % 2][:, :, :], ACT.Exp, scale=float(H) ** -0.5).then_inc(exped, 1)

            def copy_e_t(u, g, first):
                G = 4 * u + g
                act.wait_ge(et_ps, G + 1)
                if not (first and g < 2):
                    act.wait_ge(av_ps, G - 1)
                act.copy(e_t[g % 2][:, :, :], TURN[g % 2][:, :].rearrange("k (h q) -> k h q", h=4)).then_inc(et_sb, 1)

            def cross_copy_x1(u):
                act.wait_ge(x1t_ps, u + 1)
                act.copy(x1_t[:, :], MIX_A).then_inc(x1t_sb, 1)

            def cross_exp(u):
                act.wait_ge(xscore_sub, u + 1)
                act.activation(xe_sb[:, :, :], xs_sb[:, :, :], ACT.Exp, scale=float(E) ** -0.5).then_inc(xexped, 1)

            def cross_copy_e(u):
                act.wait_ge(xet_ps, u + 1)
                act.copy(xe_t[:, :], MIX_A[0:L, :]).then_inc(xet_sb, 1)

            def normalise1(u, slot, b, first):
                N = 2 * u + b
                act.wait_ge(rstd1_made, N + 1)
                if not first:
                    act.wait_ge(x1t_ps, u - 1)
                    act.wait_ge(res2_made, 2 * (u - 1))
                act.activation(x1[slot][:, b, :], res1[:, b, :], ACT.Identity, bias=shift1[:, b:b + 1], scale=rstd1[:, b:b + 1]).then_inc(x1_made, 1)

            def normalise2(u, slot, k, first):
                act.wait_ge(rstd2_made, u + 1)
                if not first:
                    act.wait_ge(x2_stored[slot], 16 * k)
                    act.wait_ge(x2t_ps, u - 1)
                for b in range(2):
                    act.activation(x2[slot][:, b, :], res2[:, b, :], ACT.Identity, bias=shift2[:, b:b + 1], scale=rstd2[:, b:b + 1]).then_inc(x2_made, 1)

            def copy_x2_t(u):
                act.wait_ge(x2t_ps, u + 1)
                act.copy(x2_t[:, :], MIX_A).then_inc(x2t_sb, 1)

            def order_q(n, slot, k):
                act.wait_ge(qk_placed[slot], 32 * k + 32)
                act.copy(q_t[slot][:, :, :, :], qk_t[slot][:, :, 0, :].rearrange("d j (h t) -> d h j t", h=H)).then_inc(q_ordered, 1)

            copy_x_t(0, 0)
            copy_v(0, 0, None)
            order_q(0, 0, 0)

            def copy_av(u, g, first):
                G = 4 * u + g
                act.wait_ge(av_ps, G + 1)
                if not (first and g < 2):
                    act.wait_ge(avt_ps, G - 1)
                act.copy(av_sb[g % 2][:, :], AV).then_inc(av_copied, 1)

            def pair(u, slot, k, age, has_next):
                first = age == 0
                exp(u, 0, first)
                if has_next:
                    copy_x_t(u + 1, 1 - slot)
                if age >= 1:
                    normalise1(u - 1, 1 - slot, 0, age < 3)
                if age >= 2:
                    normalise2(u - 2, slot, k - 1, age < 4)
                exp(u, 1, first)
                copy_e_t(u, 0, first)
                if age >= 1:
                    normalise1(u - 1, 1 - slot, 1, age < 3)
                if has_next:
                    copy_v(u + 1, 1 - slot, None if first else k + slot)
                if age >= 2:
                    copy_x2_t(u - 2)
                exp(u, 2, first)
                if age >= 1:
                    cross_copy_x1(u - 1)
                copy_e_t(u, 1, first)
                copy_av(u, 0, first)
                if age >= 1:
                    cross_exp(u - 1)
                exp(u, 3, first)
                copy_e_t(u, 2, first)
                copy_av(u, 1, first)
                if age >= 1:
                    cross_copy_e(u - 1)
                copy_e_t(u, 3, first)
                copy_av(u, 2, first)
                copy_av(u, 3, first)
                if has_next:
                    order_q(u + 1, 1 - slot, k + slot)

            for u in range(4):
                pair(u, u % 2, u // 2, u, True)
            with act.Fori(0, 1) as i:
                pair(2 * i + 4, 0, i + 2, 4, True)
                pair(2 * i + 5, 1, i + 2, 5, True)
            pair(6, 0, 3, 6, True)
            pair(7, 1, 3, 7, False)
            normalise1(7, 1, 0, False)
            normalise2(6, 0, 3, False)
            copy_x2_t(6)
            normalise1(7, 1, 1, False)
            cross_copy_x1(7)
            cross_exp(7)
            cross_copy_e(7)
            normalise2(7, 1, 3, False)
            copy_x2_t(7)

            act.wait_ge(route_step, 2)
            act.activation(prob[:, :, :], l_less[:, :, :], ACT.Exp).then_inc(route_exp, 1)
            act.wait_ge(total_ps, 1)
            act.copy(totals[:, :], TOTAL).then_inc(totals_sb, 1)

            def copy_rows(s, slot):
                act.wait_ge(xgt_ps, s + 1)
                act.copy(xg_t[slot][:, :], XG_T).then_inc(xgt_sb, 1)

            def tile(s, slot, age, has_next):
                act.wait_ge(hid1_ps, s + 1)
                if age >= 2:
                    act.wait_ge(inner_made, s - 1)
                act.activation(gated[slot][:, :], HID1[slot][:, :], ACT.Silu).then_inc(gated_made, 1)
                if has_next:
                    copy_rows(s + 1, 1 - slot)
                act.wait_ge(innert_ps, s + 1)
                if age >= 2:
                    act.wait_ge(yslot_ps, s - 1)
                act.copy(inner_t[slot][:, :, :], INNER_T[slot][:, :].rearrange("i (c t) -> i c t", c=C)).then_inc(innert_sb, 1)

            copy_rows(0, 0)
            tile(0, 0, 0, True)
            tile(1, 1, 1, True)
            with act.Fori(0, (SLOTS - 3) // 2) as i:
                tile(2 * i + 2, 0, 2, True)
                tile(2 * i + 3, 1, 3, True)
            tile(SLOTS - 1, 0, 2, False)

            def normalise3(u, slot, stored):
                act.wait_ge(rstd3_made, u + 1)
                if stored is not None:
                    act.wait_ge(out_stored[slot], stored)
                for b in range(2):
                    act.activation(out_rows[slot][:, b, :], res3[slot][:, b, :], ACT.Identity, bias=shift3[slot][:, b:b + 1],
                                   scale=rstd3[slot][:, b:b + 1]).then_inc(out_made, 1)

            normalise3(0, 0, None)
            normalise3(1, 1, None)
            with act.Fori(0, PAIRS // 2 - 1) as i:
                for slot in range(2):
                    normalise3(2 * i + 2 + slot, slot, 16 * (i + 1))

        @block.vector
        def _(dve):
            dve.wait_ge(w_in, 80)
            dve.tensor_copy(wo_rows[:, :, :], w_nat[:, 3, :].rearrange("e (t j) -> e j t", j=H)).then_inc(wo_ordered, 1)
            dve.wait_ge(w_turned, 1)
            for w, n in ((0, 0), (2, 1), (4, 2)):
                dve.tensor_copy(w_proj[:, w, :], TURN[0][:, n * 128:(n + 1) * 128])
            for w, n in ((1, 0), (3, 1)):
                pairs_of = w_proj[:, w, :].rearrange("e (i two) -> e i two", two=2)
                turned = TURN[0][:, n * 128:(n + 1) * 128].rearrange("e (i two) -> e i two", two=2)
                dve.tensor_scalar(pairs_of[:, :, 0:1], turned[:, :, 1:2], -1.0, None, ALU.mult)
                last = dve.tensor_copy(pairs_of[:, :, 1:2], turned[:, :, 0:1])
            last.then_inc(w_copied, 1)
            for slot in range(2):
                dve.memset(v_h[slot][:, :, :, D + 1:], 0.0)
                dve.memset(v_h[slot][:, :, :, D:D + 1], 1.0).then_inc(ones_made, 1)
                dve.memset(qk_t[slot][:, :, :, :], 0.0).then_inc(ones_made, 1)
            for u in range(4):
                dve.wait_ge(c_made, u + 1)
                dve.tensor_copy(xkk_all[:, 4 * L * u:4 * L * (u + 1)], TURN[1][:, 0:4 * L]).then_inc(c_kept, 1)

            def rope_products(n, slot, first):
                dve.wait_ge(qk_ps, n + 1)
                if not first:
                    dve.wait_ge(roped, n - 1)
                for part, ps, table in ((cos_part, PROJ, rope_cos), (sin_part, PROJ_ROT, rope_sin)):
                    dve.tensor_tensor(part[slot][:, :].rearrange("c (h t) -> c h t", t=TL), ps[:, :].rearrange("c (h t) -> c h t", t=TL),
                                      table.rearrange("c (o t) -> c o t", o=1).to_broadcast([128, 512 // TL, TL]), ALU.mult).then_inc(rope_parts, 1)

            def maximum(u, g, first):
                G = 4 * u + g
                s = SCORE[g % 2][:, :].rearrange("q (h k) -> q h k", h=4)
                dve.wait_ge(score_ps, G + 1)
                dve.tensor_reduce(top[g % 2][:, :], s, AXIS_X, ALU.max).then_inc(top_found, 1)
                dve.wait_ge(top_found, G + 1)
                if not (first and g < 2):
                    dve.wait_ge(exped, G - 1)
                dve.tensor_tensor(s_sb[g % 2][:, :, :], s, top[g % 2][:, :].rearrange("q (h o) -> q h o", o=1).to_broadcast([128, 4, 128]),
                                  ALU.subtract).then_inc(score_sub, 1)

            def normalise_heads(u, b, first):
                N = 2 * u + b
                dve.wait_ge(avt_ps, 4 * u + 2 * b + 2)
                av = AV_T[b].rearrange("q (h c) -> q h c", h=H)
                dve.reciprocal(o_rcp[:, :].rearrange("q (h o) -> q h o", o=1), av[:, :, D:D + 1]).then_inc(rcp_made, 1)
                dve.wait_ge(rcp_made, N + 1)
                if not first:
                    dve.wait_ge(y_ps, N - 1)
                dve.tensor_tensor(o_sb[b][:, :].rearrange("q (h c) -> q h c", h=H), av[:, :, 0:D],
                                  o_rcp[:, :].rearrange("q (h o) -> q h o", o=1).to_broadcast([128, H, D]), ALU.mult).then_inc(o_made, 1)

            def norm1(u, slot, b, first):
                N = 2 * u + b
                dve.wait_ge(y_ps, N + 1)
                if not (first and b == 0) and not first:
                    dve.wait_ge(x1_made, N - 1)
                dve.tensor_tensor(res1[:, b, :], Y[b], x_all[:, bass.ds(N, 1), :].rearrange("t b e -> t (b e)"), ALU.add).then_inc(y_added, 1)
                dve.wait_ge(y_added, N + 1)
                dve.bn_stats(stats1[:, b, :], res1[:, b, :]).then_inc(stats1_made, 1)
                wait_alone(dve, stats1_made, N + 1)
                dve.bn_aggr(mv1[:, b, :], stats1[:, b, :]).then_inc(mv1_made, 1)

            def cross_maximum(u, first):
                s = MIX_B[:, 0:2 * L].rearrange("q (b k) -> q b k", b=2)
                dve.wait_ge(xscore_ps, u + 1)
                dve.tensor_reduce(xtop[:, :], s, AXIS_X, ALU.max).then_inc(xtop_found, 1)
                dve.wait_ge(xtop_found, u + 1)
                dve.tensor_tensor(xs_sb[:, :, :], s, xtop[:, :].rearrange("q (b o) -> q b o", o=1).to_broadcast([128, 2, L]),
                                  ALU.subtract).then_inc(xscore_sub, 1)

            def cross_sum(u):
                dve.wait_ge(xexped, u + 1)
                dve.tensor_reduce(xsum[:, :], xe_sb[:, :, :], AXIS_X, ALU.add).then_inc(xsum_step, 1)
                dve.wait_ge(xsum_step, 2 * u + 1)
                dve.reciprocal(xrcp[:, :], xsum[:, :]).then_inc(xsum_step, 1)

            def norm2(u, slot, first):
                dve.wait_ge(xo_ps, u + 1)
                dve.wait_ge(xsum_step, 2 * u + 2)
                if not first:
                    dve.wait_ge(x2_made, 2 * u)
                for b in range(2):
                    dve.scalar_tensor_tensor(out=res2[:, b, :], in0=MIX_B[:, b * 128:(b + 1) * 128], scalar=xrcp[:, b:b + 1], in1=x1[slot][:, b, :],
                                             op0=ALU.mult, op1=ALU.add).then_inc(res2_made, 1)
                for b in range(2):
                    dve.wait_ge(res2_made, 2 * u + b + 1)
                    dve.bn_stats(stats2[:, b, :], res2[:, b, :]).then_inc(stats2_made, 1)
                for b in range(2):
                    wait_alone(dve, stats2_made, 2 * u + b + 1)
                    dve.bn_aggr(mv2[:, b, :], stats2[:, b, :]).then_inc(mv2_made, 1)

            def keep_logits(u):
                dve.wait_ge(logit_ps, u + 1)
                dve.tensor_copy(logits[:, bass.ds(2 * u, 2), :], LOGITS.rearrange("t (b e) -> t b e", b=2)).then_inc(logit_sb, 1)

            rope_products(0, 0, True)
            dve.wait_ge(x_all_in, 16)

            def pair(u, slot, k, age, has_next):
                first = age == 0
                maximum(u, 0, first)
                if age >= 1:
                    normalise_heads(u - 1, 1, age < 2)
                maximum(u, 1, first)
                if age >= 1:
                    norm1(u - 1, 1 - slot, 1, age < 2)
                if has_next:
                    rope_products(u + 1, 1 - slot, first)
                maximum(u, 2, first)
                if age >= 1:
                    cross_maximum(u - 1, False)
                maximum(u, 3, first)
                if age >= 1:
                    cross_sum(u - 1)
                normalise_heads(u, 0, first)
                if age >= 1:
                    norm2(u - 1, 1 - slot, age < 2)
                norm1(u, slot, 0, first)
                if age >= 2:
                    keep_logits(u - 2)

            pair(0, 0, 0, 0, True)
            pair(1, 1, 0, 1, True)
            with dve.Fori(0, 2) as i:
                pair(2 * i + 2, 0, i + 1, 2, True)
                pair(2 * i + 3, 1, i + 1, 3, True)
            pair(6, 0, 3, 6, True)
            pair(7, 1, 3, 7, False)
            normalise_heads(7, 1, False)
            norm1(7, 1, 1, False)
            cross_maximum(7, False)
            cross_sum(7)
            norm2(7, 1, False)
            keep_logits(6)
            keep_logits(7)

            dve.memset(ones[:, :], 1.0).then_inc(ones_set, 1)
            def step(instruction):
                instruction.then_inc(route_step, 1)
            def spread(a, shape):
                return a.to_broadcast(shape)

            dve.wait_ge(logit_sb, PAIRS)
            step(dve.tensor_reduce(l_top[:, :], logits[:, :, :], AXIS_X, ALU.max))
            dve.wait_ge(route_step, 1)
            step(dve.tensor_tensor(l_less[:, :, :], logits[:, :, :], spread(l_top[:, :].rearrange("t (b o) -> t b o", o=1), [128, B, NE]), ALU.subtract))
            theirs = spread(logits[:, :, :].rearrange("t b (o f) -> t b o f", o=1), [128, B, NE, NE])
            own = spread(logits[:, :, :].rearrange("t b (e o) -> t b e o", o=1), [128, B, NE, NE])
            step(dve.tensor_tensor(tied[:, :, :, :], theirs, own, ALU.is_equal))
            step(dve.tensor_tensor(above[:, :, :, :], theirs, own, ALU.is_gt))
            dve.wait_ge(route_step, 4)
            step(dve.tensor_tensor(tied[:, :, :, :].rearrange("t b e f -> t b (e f)"), tied[:, :, :, :].rearrange("t b e f -> t b (e f)"),
                                   spread(table["lower"].rearrange("t (o c) -> t o c", o=1), [128, B, NE * NE]), ALU.mult))
            dve.wait_ge(route_step, 5)
            step(dve.tensor_tensor(above[:, :, :, :], above[:, :, :, :], tied[:, :, :, :], ALU.add))
            dve.wait_ge(route_step, 6)
            step(dve.tensor_reduce(rank[:, :, :], above[:, :, :, :], AXIS_X, ALU.add))
            dve.wait_ge(route_step, 7)
            step(dve.tensor_scalar(either[:, :, :], rank[:, :, :], 2.0, None, ALU.is_lt))
            step(dve.tensor_scalar(chosen[0][:, :, :], rank[:, :, :], 0.0, None, ALU.is_equal))
            step(dve.tensor_scalar(chosen[1][:, :, :], rank[:, :, :], 1.0, None, ALU.is_equal))
            dve.wait_ge(route_exp, 1)
            step(dve.tensor_reduce(p_sum[:, :], prob[:, :, :], AXIS_X, ALU.add))
            dve.wait_ge(route_step, 11)
            step(dve.reciprocal(l_top[:, :], p_sum[:, :]))
            dve.wait_ge(route_step, 12)
            step(dve.tensor_tensor(prob[:, :, :], prob[:, :, :], spread(l_top[:, :].rearrange("t (b o) -> t b o", o=1), [128, B, NE]), ALU.mult))
            dve.wait_ge(route_step, 13)
            for c in range(2):
                step(dve.tensor_tensor(product[c][:, :, :], chosen[c][:, :, :], prob[:, :, :], ALU.mult))
            for c in range(2):
                dve.wait_ge(route_step, 14 + c)
                step(dve.tensor_reduce(share[:, c, :], product[c][:, :, :], AXIS_X, ALU.add))
            dve.wait_ge(route_step, 17)
            step(dve.tensor_tensor(share_sum[:, :], share[:, 0, :], share[:, 1, :], ALU.add))
            dve.wait_ge(route_step, 18)
            step(dve.reciprocal(p_sum[:, :], share_sum[:, :]))
            dve.wait_ge(route_step, 19)
            step(dve.tensor_tensor(share[:, :, :], share[:, :, :], spread(p_sum[:, :].rearrange("t (o b) -> t o b", o=1), [128, 2, B]), ALU.mult))
            dve.wait_ge(place_ps, 1)
            step(dve.tensor_tensor(more_rows[:, :, :], spread(COUNT.rearrange("t (e o) -> t e o", o=1), [128, NE, EXPERT_TILES]),
                                   spread(table["tile_rows"].rearrange("t (o m) -> t o m", o=1), [128, NE, EXPERT_TILES]), ALU.is_gt))
            dve.wait_ge(route_step, 21)
            step(dve.tensor_reduce(tiles[:, :], more_rows[:, :, :], AXIS_X, ALU.add))
            dve.wait_ge(route_step, 22)
            step(dve.tensor_tensor(tiles_before[:, :, :], spread(tiles[:, :].rearrange("t (o f) -> t o f", o=1), [128, NE, NE]),
                                   table["lower"].rearrange("t (e f) -> t e f", e=NE), ALU.mult))
            dve.wait_ge(route_step, 23)
            step(dve.tensor_reduce(start[:, :], tiles_before[:, :, :], AXIS_X, ALU.add))
            dve.wait_ge(route_step, 24)
            step(dve.tensor_scalar(start_rows[:, :], start[:, :], 128.0, None, ALU.mult))
            step(dve.tensor_tensor(tile_end[:, :], start[:, :], tiles[:, :], ALU.add))
            dve.wait_ge(route_step, 26)
            step(dve.tensor_tensor(place[:, :, :], PLACE.rearrange("t (b e) -> t b e", b=B), spread(start_rows[:, :].rearrange("t (o e) -> t o e", o=1), [128, B, NE]), ALU.add))
            dve.wait_ge(route_step, 27)
            for c in range(2):
                step(dve.tensor_tensor(product[2 + c][:, :, :], chosen[c][:, :, :], place[:, :, :], ALU.mult))
            for c in range(2):
                dve.wait_ge(route_step, 28 + c)
                step(dve.tensor_reduce(dest[:, c, :], product[2 + c][:, :, :], AXIS_X, ALU.add))
            dve.wait_ge(route_step, 31)
            step(dve.tensor_copy(dest_i[:, :, :], dest[:, :, :]))
            dve.wait_ge(route_step, 32)
            step(dve.tensor_scalar(dest_tile_i[:, :, :], dest_i[:, :, :], 7, None, ALU.arith_shift_right))
            step(dve.tensor_scalar(dest_row_i[:, :, :], dest_i[:, :, :], 127, None, ALU.bitwise_and))
            dve.wait_ge(route_step, 34)
            step(dve.tensor_copy(dest_tile[:, :, :], dest_tile_i[:, :, :]))
            step(dve.tensor_copy(dest_row[:, :, :], dest_row_i[:, :, :]))
            dve.wait_ge(route_step, 36)
            for c in range(2):
                for b in range(B):
                    n = c * B + b
                    if n >= 4:
                        dve.wait_ge(hot_used, n - 3)
                    dve.tensor_scalar(row_is[:, n % 4, :], table["iota"], dest_row[:, c, b:b + 1], None, ALU.is_equal).then_inc(hot_made, 1)
                    dve.tensor_scalar(tile_is[:, n % 4, :], table["iota"][:, 0:SLOTS], dest_tile[:, c, b:b + 1], table["token"][:, b:b + 1],
                                      ALU.is_equal, ALU.mult).then_inc(hot_made, 1)
            step(dve.tensor_tensor(past[:, :, :], spread(table["iota"][:, 0:SLOTS].rearrange("t (s o) -> t s o", o=1), [128, SLOTS, NE]),
                                   spread(tile_end[:, :].rearrange("t (o e) -> t o e", o=1), [128, SLOTS, NE]), ALU.is_ge))
            dve.wait_ge(route_step, 37)
            step(dve.tensor_reduce(expert_f[:, :], past[:, :, :], AXIS_X, ALU.add))
            dve.wait_ge(route_step, 38)
            step(dve.tensor_scalar(expert_of[:, :], expert_f[:, :], float(NE - 1), None, ALU.min))
            dve.wait_ge(hot_used, 2 * B)
            step(dve.tensor_copy(taken[:, :, :], TABLE.rearrange("p (c s) -> p c s", c=2)))
            dve.wait_ge(route_step, 40)
            step(dve.tensor_tensor(number[:, :], taken[:, 0, :], taken[:, 1, :], ALU.add))
            step(dve.tensor_scalar(is_second[:, :], taken[:, 1, :], 0.0, float(ROWS), ALU.is_gt, ALU.mult))
            dve.wait_ge(route_step, 42)
            step(dve.tensor_scalar(number_in[:, :], number[:, :], -1.0, 0.0, ALU.add, ALU.max))
            step(dve.tensor_scalar(is_empty[:, :], number[:, :], 0.0, None, ALU.is_equal))
            step(dve.tensor_tensor(number[:, :], number[:, :], is_second[:, :], ALU.add))
            dve.wait_ge(route_step, 45)
            step(dve.tensor_copy(from_row[:, :], number_in[:, :]))
            step(dve.tensor_tensor(is_empty[:, :], is_empty[:, :], table["spare"], ALU.mult))
            dve.wait_ge(route_step, 47)
            step(dve.tensor_tensor(number_out[:, :], number[:, :], is_empty[:, :], ALU.add))
            dve.wait_ge(route_step, 48)
            dve.tensor_scalar(to_row[:, :], number_out[:, :], -1.0, None, ALU.add).then_inc(lists_made, 1)

            def product_of(s, slot, age):
                dve.wait_ge(hid3_ps, s + 1)
                dve.wait_ge(gated_made, s + 1)
                if age >= 2:
                    dve.wait_ge(innert_ps, s - 1)
                dve.tensor_tensor(inner[slot][:, :], gated[slot][:, :], HID3[slot][:, :], ALU.mult).then_inc(inner_made, 1)

            def keep_y(s, slot, k):
                dve.wait_ge(yslot_ps, s + 1)
                if k is not None:
                    dve.wait_ge(scattered[slot], 16 * k)
                dve.tensor_copy(y_sb[slot][:, :], Y_SLOT).then_inc(yslot_sb, 1)

            product_of(0, 0, 0)
            product_of(1, 1, 1)
            keep_y(0, 0, None)
            product_of(2, 0, 2)
            keep_y(1, 1, None)
            with dve.Fori(0, (SLOTS - 3) // 2) as i:
                product_of(2 * i + 3, 1, 3)
                keep_y(2 * i + 2, 0, i + 1)
                product_of(2 * i + 4, 0, 4)
                keep_y(2 * i + 3, 1, i + 1)
            keep_y(SLOTS - 1, 0, (SLOTS - 1) // 2)

            def add_rows(u, slot, k, age):
                dve.wait_ge(rows_in[slot], 48 * (k + 1))
                if age >= 2:
                    dve.wait_ge(out_made, 2 * (u - 1))
                for b in range(2):
                    for c, before in ((0, x2_rows), (1, res3)):
                        if c == 1:
                            dve.wait_ge(weighed, 2 * u + b + 1)
                        dve.scalar_tensor_tensor(out=res3[slot][:, b, :], in0=y_rows[slot][:, c, b, :], scalar=share[:, c, bass.ds(2 * u + b, 1)],
                                                 in1=before[slot][:, b, :], op0=ALU.mult, op1=ALU.add).then_inc((weighed, res3_made)[c], 1)
                for b in range(2):
                    dve.wait_ge(res3_made, 2 * u + b + 1)
                    dve.bn_stats(stats3[slot][:, b, :], res3[slot][:, b, :]).then_inc(stats3_made, 1)
                for b in range(2):
                    wait_alone(dve, stats3_made, 2 * u + b + 1)
                    dve.bn_aggr(mv3[slot][:, b, :], stats3[slot][:, b, :]).then_inc(mv3_made, 1)

            add_rows(0, 0, 0, 0)
            add_rows(1, 1, 0, 1)
            with dve.Fori(0, PAIRS // 2 - 1) as i:
                add_rows(2 * i + 2, 0, i + 1, 2)
                add_rows(2 * i + 3, 1, i + 1, 3)

        @block.gpsimd
        def _(pool):
            pool.memset(mask16[:, :, :], 0.0).then_inc(consts_made, 1)
            pool.wait_ge(consts_made, 1)
            pool.affine_select(out=mask16[:, :, :], in_=mask16[:, :, :], compare_op=ALU.is_ge, fill=MASKED, base=0,
                               pattern=[[0, 2], [-1, L]], channel_multiplier=1).then_inc(consts_made, 1)
            pool.memset(exponent[:, :], -0.5).then_inc(consts_made, 1)
            pool.wait_ge(consts_made, 3)
            pool.wait_ge(const_in, 16)
            pool.tensor_copy(ident16[:, :], ident).then_inc(consts_made, 1)

            def add_parts(n, slot, k):
                wait_alone(pool, rope_parts, 2 * n + 2)
                if k is not None:
                    pool.wait_ge(qk_stored[slot], 16 * k)
                total, cos, sin = [p[slot][:, :] for p in (qk_sb, cos_part, sin_part)]
                pool.tensor_tensor(total.rearrange("c (b w t) -> c w b t", b=2, w=2), cos.rearrange("c (w b t) -> c w b t", b=2, w=2),
                                   sin.rearrange("c (w b t) -> c w b t", b=2, w=2), ALU.add).then_inc(roped, 1)

            def layernorm1(u, b):
                N = 2 * u + b
                wait_alone(pool, mv1_made, N + 1)
                pool.tensor_scalar(var1[:, b:b + 1], mv1[:, b, 1:2], EPS, None, ALU.add).then_inc(pool_step1, 1)
                pool.tensor_scalar(less1[:, b:b + 1], mv1[:, b, 0:1], -1.0, None, ALU.mult).then_inc(pool_step1, 1)
                wait_alone(pool, pool_step1, 3 * N + 2)
                pool.tensor_tensor(rstd1[:, b:b + 1], var1[:, b:b + 1], exponent[:, 0:1], ALU.pow).then_inc(pool_step1, 1)
                wait_alone(pool, pool_step1, 3 * N + 3)
                pool.tensor_tensor(shift1[:, b:b + 1], less1[:, b:b + 1], rstd1[:, b:b + 1], ALU.mult).then_inc(rstd1_made, 1)

            def layernorm2(u):
                wait_alone(pool, mv2_made, 2 * u + 2)
                pool.tensor_scalar(var2[:, :].rearrange("t (b o) -> t b o", o=1), mv2[:, :, 1:2], EPS, None, ALU.add).then_inc(pool_step2, 1)
                pool.tensor_scalar(less2[:, :].rearrange("t (b o) -> t b o", o=1), mv2[:, :, 0:1], -1.0, None, ALU.mult).then_inc(pool_step2, 1)
                wait_alone(pool, pool_step2, 3 * u + 2)
                pool.tensor_tensor(rstd2[:, :], var2[:, :], exponent[:, :], ALU.pow).then_inc(pool_step2, 1)
                wait_alone(pool, pool_step2, 3 * u + 3)
                pool.tensor_tensor(shift2[:, :], less2[:, :], rstd2[:, :], ALU.mult).then_inc(rstd2_made, 1)

            def pair(u, slot, k, age, has_next):
                if age >= 1:
                    layernorm1(u - 1, 1)
                if has_next:
                    add_parts(u + 1, 1 - slot, k + slot if age >= 1 else None)
                if age >= 1:
                    layernorm2(u - 1)
                layernorm1(u, 0)

            add_parts(0, 0, None)
            pair(0, 0, 0, 0, True)
            with pool.Fori(0, 3) as i:
                pair(2 * i + 1, 1, i, 1, True)
                pair(2 * i + 2, 0, i + 1, 2, True)
            pair(7, 1, 3, 7, False)
            layernorm1(7, 1)
            layernorm2(7)

            def gather(s, slot, age):
                if age >= 2:
                    pool.wait_ge(xgt_ps, s - 1)
                pool.tensor_copy(from_now[slot][:, :], from_row[:, bass.ds(s, 1)]).then_inc(from_copied, 1)
                wait_alone(pool, from_copied, s + 1)
                pool.indirect_dma_start(out=xg[slot][:, :], out_offset=None, in_=x2_dram.rearrange("b t e -> (b t) e"),
                                        in_offset=bass.IndirectOffsetOnAxis(ap=from_now[slot][:, :], axis=0)).then_inc(gathered[slot], 16)

            def scatter(s, slot):
                pool.wait_ge(yslot_sb, s + 1)
                pool.tensor_copy(to_now[slot][:, :], to_row[:, bass.ds(s, 1)]).then_inc(to_copied, 1)
                wait_alone(pool, to_copied, s + 1)
                pool.indirect_dma_start(out=y_dram, out_offset=bass.IndirectOffsetOnAxis(ap=to_now[slot][:, :], axis=0),
                                        in_=y_sb[slot][:, :], in_offset=None).then_inc(scattered[slot], 16)

            pool.wait_ge(lists_made, 1)
            pool.wait_ge(x2_stored[0], 16 * PAIRS // 2)
            pool.wait_ge(x2_stored[1], 16 * PAIRS // 2)
            gather(0, 0, 0)
            gather(1, 1, 1)
            gather(2, 0, 2)
            with pool.Fori(0, (SLOTS - 3) // 2) as i:
                gather(2 * i + 3, 1, 3)
                scatter(2 * i, 0)
                gather(2 * i + 4, 0, 4)
                scatter(2 * i + 1, 1)
            scatter(SLOTS - 3, 0)
            scatter(SLOTS - 2, 1)
            scatter(SLOTS - 1, 0)

            def layernorm3(u, slot, age):
                wait_alone(pool, mv3_made, 2 * u + 2)
                if age >= 2:
                    wait_alone(pool, out_made, 2 * (u - 1))
                pool.tensor_scalar(var3[slot][:, :].rearrange("t (b o) -> t b o", o=1), mv3[slot][:, :, 1:2], EPS, None, ALU.add).then_inc(pool_step3, 1)
                pool.tensor_scalar(less3[slot][:, :].rearrange("t (b o) -> t b o", o=1), mv3[slot][:, :, 0:1], -1.0, None, ALU.mult).then_inc(pool_step3, 1)
                wait_alone(pool, pool_step3, 3 * u + 2)
                pool.tensor_tensor(rstd3[slot][:, :], var3[slot][:, :], exponent[:, :], ALU.pow).then_inc(pool_step3, 1)
                wait_alone(pool, pool_step3, 3 * u + 3)
                pool.tensor_tensor(shift3[slot][:, :], less3[slot][:, :], rstd3[slot][:, :], ALU.mult).then_inc(rstd3_made, 1)

            layernorm3(0, 0, 0)
            layernorm3(1, 1, 1)
            with pool.Fori(0, PAIRS // 2 - 1) as i:
                layernorm3(2 * i + 2, 0, 2)
                layernorm3(2 * i + 3, 1, 3)


_INS = ["x", "ctx_1024", "L0_attn_W1", "L0_attn_W2", "L0_attn_W3", "L0_attn_Wo", "L0_xattn_Wq",
        "L0_ffn_gate_w", "L0_ffn_w1s", "L0_ffn_w2s", "L0_ffn_w3s"]


def kernel(**inputs):
    import concourse.bacc as bacc
    from concourse.bass_utils import run_bass_kernel_spmd

    nc = bacc.Bacc("TRN2", target_bir_lowering=False, num_devices=1)
    arrays, args = {}, []
    for name in _INS + ["shape_constants"]:
        a = shape_constants() if name == "shape_constants" else np.ascontiguousarray(inputs[name])
        arrays[f"in_{name}"] = a
        args.append(nc.dram_tensor(f"in_{name}", a.shape, mybir.dt.from_np(a.dtype), kind="ExternalInput").ap())
    args.append(nc.dram_tensor("out", (B, S, E), F32, kind="ExternalOutput").ap())
    build(nc, *args)
    got = run_bass_kernel_spmd(nc, [arrays], core_ids=[0])
    return got.results[0]["out"]
```

```python
from contextlib import ExitStack

import numpy as np
import concourse.bass as bass
from concourse import mybir

F32 = mybir.dt.float32
BF16, F16 = mybir.dt.bfloat16, mybir.dt.float16
I32, U32 = mybir.dt.int32, mybir.dt.uint32
ALU = mybir.AluOpType
ACT = mybir.ActivationFunctionType
AXIS_X = mybir.AxisListType.X

B, S, E = 16, 128, 128
H, D = 8, 16
TL = S // H
L = 77
NE, I = 8, 512
C = I // 128
PAIRS = B // 2
EPS = 1e-5
EITHER_AT = 8
MASKED = -1e30
HEAD_SCALE, CROSS_SCALE = float(H) ** -0.5, float(E) ** -0.5
ROWS = B * S
SLOTS = 2 * ROWS // 128 + NE - 1
EXPERT_TILES = ROWS // 128
Y_ROWS = 2 * ROWS + SLOTS * 128
RING = 4
RUNS = (SLOTS - RING - 1) // RING
LAST_FROM = RING * (RUNS + 1)
COLUMNS = {"cos": TL, "sin": TL, "ident": 128, "before": 128, "same_before": 128, "same": NE, "lower": NE * NE,
           "tile_rows": EXPERT_TILES, "iota": 128, "token": B, "spare": SLOTS}
CONST_COLS = sum(COLUMNS.values())


def shape_constants():
    cos, sin = rope_tables()
    row, col = np.arange(128)[:, None], np.arange(128)[None, :]
    e = np.arange(NE)
    parts = {
        "cos": cos, "sin": sin, "ident": row == col,
        "before": row < col,
        "same_before": (row // NE < col // NE) & (row % NE == col % NE),
        "same": row % NE == e[None, :],
        "lower": np.tile((e[None, :] < e[:, None]).reshape(1, -1), (128, 1)),
        "tile_rows": np.tile(128 * np.arange(EXPERT_TILES)[None, :], (128, 1)),
        "iota": np.tile(col, (128, 1)),
        "token": 128 * np.arange(B)[None, :] + row + 1,
        "spare": 2 * ROWS + 1 + 128 * np.arange(SLOTS)[None, :] + row,
    }
    return np.concatenate([parts[n].astype(np.float32) for n in COLUMNS], axis=1)


def rope_tables():
    inv = (1.0 / np.float32(10000.0) ** (np.arange(0, D, 2, dtype=np.float32) / np.float32(D))).astype(np.float32)
    pos = (np.arange(TL)[None, :] * H + np.arange(H)[:, None]).astype(np.float32)
    ang = pos[:, None, :] * np.repeat(inv, 2)[None, :, None]
    ang = ang.astype(np.float32).reshape(H * D, TL)
    return np.cos(ang), np.sin(ang)


def build(nc, x, ctx_in, w_q, w_k, w_v, w_o, w_x, gate_w, w1s, w2s, w3s, consts, out):
    with ExitStack() as ctx:
        def sb(name, shape, dt=F32):
            return ctx.enter_context(nc.sbuf_tensor(name, shape, dt))

        def sem(name):
            return ctx.enter_context(nc.semaphore(name))

        def two(make, name, *a):
            return [make(f"{name}{n}", *a) for n in range(2)]

        def ring(make, name, *a):
            return [make(f"{name}{n}", *a) for n in range(RING)]

        qk_dram = nc.dram_tensor("qk_dram", (2, H, D, 2 * 2 * S), F32, kind="Internal").ap()
        v_dram = nc.dram_tensor("v_dram", (2, 2, S, E), F32, kind="Internal").ap()
        y_dram = nc.dram_tensor("y_dram", (Y_ROWS, E), F32, kind="Internal").ap()
        x2_dram = nc.dram_tensor("x2_dram", (B, S, E), F32, kind="Internal").ap()

        const = sb("const", [128, CONST_COLS])
        table, at = {}, 0
        for name, width in COLUMNS.items():
            table[name] = const[:, at:at + width]
            at += width
        rope_cos, rope_sin, ident = table["cos"], table["sin"], table["ident"]
        ident16 = sb("ident16", [128, 128], BF16)
        mask16 = sb("mask16", [128, 2, L], BF16)
        exponent = sb("exponent", [128, 2])
        w_nat = sb("w_nat", [128, 5, 128])
        w_proj = sb("w_proj", [128, 5, 128])
        wo_rows = sb("wo_rows", [128, H, TL])
        wo_t = sb("wo_t", [128, 128])
        wx_t = sb("wx_t", [128, 128])
        wx_gram = sb("wx_gram", [128, 128])
        gate = sb("gate", [128, NE])
        c_rows = two(sb, "c_rows", [L, 4, 128])
        c_t = two(sb, "c_t", [128, 4 * L])
        xk_all = sb("xk_all", [L, B, 128])
        xkk_all = sb("xkk_all", [128, B * L])
        x_all = sb("x_all", [128, B, 128])
        xs = two(sb, "xs", [128, 2, 128])
        x_t = two(sb, "x_t", [128, 256])
        cos_part = two(sb, "cos_part", [128, 512])
        sin_part = two(sb, "sin_part", [128, 512])
        qk_sb = two(sb, "qk_sb", [128, 512])
        qk_t = two(sb, "qk_t", [32 + D, H, 2, S])
        q_t = two(sb, "q_t", [32 + D, H, H, TL])
        v_sb = two(sb, "v_sb", [128, 2, 128])
        v_h = two(sb, "v_h", [128, 2, H, 2 * D])
        top, less_top = two(sb, "top", [128, 4]), two(sb, "less_top", [128, 4])
        e_sb = two(sb, "e_sb", [128, 4, 128])
        e_t = two(sb, "e_t", [128, 4, 128])
        av_sb = two(sb, "av_sb", [128, 128])
        o_rcp = sb("o_rcp", [128, H])
        o_sb = two(sb, "o_sb", [128, 128])
        res1 = sb("res1", [128, 2, 128])
        var1, var2 = sb("var1", [128, 2]), sb("var2", [128, 2])
        stats1, mv1, rstd1 = sb("stats1", [128, 2, 6]), sb("mv1", [128, 2, 2]), sb("rstd1", [128, 2])
        x1 = two(sb, "x1", [128, 2, 128])
        x1_t = sb("x1_t", [128, 256])
        xless_top = sb("xless_top", [128, 2])
        xtop, xsum, xrcp = sb("xtop", [128, 2]), sb("xsum", [128, 2]), sb("xrcp", [128, 2])
        xe_sb = sb("xe_sb", [128, 2, L])
        xe_t = sb("xe_t", [L, 256])
        res2 = sb("res2", [128, 2, 128])
        stats2, mv2, rstd2 = sb("stats2", [128, 2, 6]), sb("mv2", [128, 2, 2]), sb("rstd2", [128, 2])
        x2 = two(sb, "x2", [128, 2, 128])
        x2_t = sb("x2_t", [128, 256])
        logits = sb("logits", [128, B, NE])
        ones = sb("ones", [128, 128])
        l_top, l_less, prob, p_sum = sb("l_top", [128, B]), sb("l_less", [128, B, NE]), sb("prob", [128, B, NE]), sb("p_sum", [128, B])
        above, tied, rank = sb("above", [128, B, NE, NE]), sb("tied", [128, B, NE, NE]), sb("rank", [128, B, NE])
        chosen = [sb(name, [128, B, NE]) for name in ("first_choice", "second_choice")]
        either = sb("either", [128, B, NE])
        totals = sb("totals", [128, 128])
        more_rows, tiles, tiles_before = sb("more_rows", [128, NE, EXPERT_TILES]), sb("tiles", [128, NE]), sb("tiles_before", [128, NE, NE])
        start, start_rows, tile_end = sb("start", [128, NE]), sb("start_rows", [128, NE]), sb("tile_end", [128, NE])
        past, expert_f, expert_of = sb("past", [128, SLOTS, NE]), sb("expert_f", [128, SLOTS]), sb("expert_of", [128, SLOTS], I32)
        place, product = sb("place", [128, B, NE]), [sb(f"product{n}", [128, B, NE]) for n in range(4)]
        dest, dest_i = sb("dest", [128, 2, B]), sb("dest_i", [128, 2, B], I32)
        dest_tile_i, dest_row_i = sb("dest_tile_i", [128, 2, B], I32), sb("dest_row_i", [128, 2, B], I32)
        dest_tile, dest_row = sb("dest_tile", [128, 2, B]), sb("dest_row", [128, 2, B])
        share, share_sum = sb("share", [128, 2, B]), sb("share_sum", [128, B])
        row_is = sb("row_is", [128, 4, 128], F16)
        tile_is = sb("tile_is", [128, 4, SLOTS], F16)
        taken, is_second, is_empty = sb("taken", [128, 2, SLOTS]), sb("is_second", [128, SLOTS]), sb("is_empty", [128, SLOTS])
        number, number_in, number_out = sb("number", [128, SLOTS]), sb("number_in", [128, SLOTS]), sb("number_out", [128, SLOTS])
        from_row, to_row = sb("from_row", [128, SLOTS], U32), sb("to_row", [128, SLOTS], U32)
        from_now, to_now = ring(sb, "from_now", [128, 1], U32), two(sb, "to_now", [128, 1], U32)
        w1_sb, w3_sb = sb("w1_sb", [128, NE, I]), sb("w3_sb", [128, NE, I])
        w2_sb = sb("w2_sb", [128, NE, C, 128])
        xg = ring(sb, "xg", [128, 128])
        xg_t = two(sb, "xg_t", [128, 128])
        gated, inner = two(sb, "gated", [128, I]), two(sb, "inner", [128, I])
        inner_t = two(sb, "inner_t", [128, C, 128])
        y_sb = two(sb, "y_sb", [128, 128])
        y_rows = two(sb, "y_rows", [128, 2, 2, 128])
        x2_rows = two(sb, "x2_rows", [128, 2, 128])
        res3 = two(sb, "res3", [128, 2, 128])
        stats3, mv3 = two(sb, "stats3", [128, 2, 6]), two(sb, "mv3", [128, 2, 2])
        less3 = two(sb, "less3", [128, 2])
        var3, rstd3, shift3 = two(sb, "var3", [128, 2]), two(sb, "rstd3", [128, 2]), two(sb, "shift3", [128, 2])
        out_rows = two(sb, "out_rows", [128, 2, 128])

        bank = [ctx.enter_context(nc.psum_tensor(f"bank{n}", [128, 512], F32)) for n in range(8)]
        SCORE = bank[0:2]
        TURN = bank[2:4]
        PROJ, PROJ_ROT, MIX, OUTS = bank[4:8]
        MIX_A, MIX_B = MIX[:, 0:256], MIX[:, 256:512]
        AV = OUTS[:, 0:128]
        AV_T = [PROJ[:, 256:512], PROJ_ROT[:, 256:512]]
        Y = [PROJ[:, 0:128], PROJ_ROT[:, 0:128]]
        LOGITS = PROJ[:, 128:128 + 2 * NE]
        TOTAL, PLACE, COUNT, TABLE = bank[0][:, 0:128], bank[1][:, 0:128], bank[2][:, 0:NE], bank[3][:, 0:2 * SLOTS]
        HID1, HID3, INNER_T, XG_T, Y_SLOT = bank[0:2], bank[2:4], bank[4:6], bank[6][:, 0:128], bank[7][:, 0:128]

        var1_made, var2_made = sem("var1_made"), sem("var2_made")
        const_in, w_in, gate_in = sem("const_in"), sem("w_in"), sem("gate_in")
        consts_made, ones_made, wo_ordered = sem("consts_made"), sem("ones_made"), sem("wo_ordered")
        w_turned, w_copied = sem("w_turned"), sem("w_copied")
        c_in = two(sem, "c_in")
        c_turned, c_copied, c_made, c_kept = sem("c_turned"), sem("c_copied"), sem("c_made"), sem("c_kept")
        x_all_in, x_in = sem("x_all_in"), two(sem, "x_in")
        xt_ps, xt_sb = sem("xt_ps"), sem("xt_sb")
        qk_ps, v_ps, rope_parts, roped, v_rows = sem("qk_ps"), sem("v_ps"), sem("rope_parts"), sem("roped"), sem("v_rows")
        qk_stored, qk_placed, q_ordered = two(sem, "qk_stored"), two(sem, "qk_placed"), sem("q_ordered")
        v_stored, v_placed = two(sem, "v_stored"), two(sem, "v_placed")
        score_ps, top_found, bias_made, exped = sem("score_ps"), sem("top_found"), sem("bias_made"), sem("exped")
        et_ps, et_sb, av_ps, rcp_made, o_made = sem("et_ps"), sem("et_sb"), sem("av_ps"), sem("rcp_made"), sem("o_made")
        av_copied, avt_ps = sem("av_copied"), sem("avt_ps")
        y_ps, y_added, stats1_made, mv1_made, rstd1_made, x1_made = (
            sem("y_ps"), sem("y_added"), sem("stats1_made"), sem("mv1_made"), sem("rstd1_made"), sem("x1_made"))
        x1t_ps, x1t_sb, xscore_ps, xtop_found, xbias_made = sem("x1t_ps"), sem("x1t_sb"), sem("xscore_ps"), sem("xtop_found"), sem("xbias_made")
        xexped, xet_ps, xet_sb, xo_ps, xsum_step = sem("xexped"), sem("xet_ps"), sem("xet_sb"), sem("xo_ps"), sem("xsum_step")
        res2_made, stats2_made, mv2_made, rstd2_made, x2_made = (
            sem("res2_made"), sem("stats2_made"), sem("mv2_made"), sem("rstd2_made"), sem("x2_made"))
        x2t_ps, x2t_sb, logit_ps, logit_sb = sem("x2t_ps"), sem("x2t_sb"), sem("logit_ps"), sem("logit_sb")
        x2_stored = two(sem, "x2_stored")
        route_step, route_exp, total_ps, totals_sb, place_ps = sem("route_step"), sem("route_exp"), sem("total_ps"), sem("totals_sb"), sem("place_ps")
        hot_made, hot_used, table_ps, lists_made, ones_set = sem("hot_made"), sem("hot_used"), sem("table_ps"), sem("lists_made"), sem("ones_set")
        experts_in, from_copied, to_copied = sem("experts_in"), sem("from_copied"), sem("to_copied")
        gathered, scattered = ring(sem, "gathered"), two(sem, "scattered")
        xgt_ps, xgt_sb, hid1_ps, hid3_ps, gated_made, inner_made = (
            sem("xgt_ps"), sem("xgt_sb"), sem("hid1_ps"), sem("hid3_ps"), sem("gated_made"), sem("inner_made"))
        innert_ps, innert_sb, yslot_ps, yslot_sb = sem("innert_ps"), sem("innert_sb"), sem("yslot_ps"), sem("yslot_sb")
        rows_in = two(sem, "rows_in")
        weighed, res3_made, stats3_made, mv3_made, pool_step3, rstd3_made, out_made = (
            sem("weighed"), sem("res3_made"), sem("stats3_made"), sem("mv3_made"), sem("pool_step3"), sem("rstd3_made"), sem("out_made"))
        out_stored = two(sem, "out_stored")

        waits_met = {e.engine: sem(f"waits_met_{n}") for n, e in enumerate((nc.sync, nc.vector, nc.gpsimd))}

        def wait_alone(engine, semaphore, value):
            engine.wait_ge(semaphore, value)
            engine.sem_inc(waits_met[engine.engine], 1)

        block = ctx.enter_context(nc.Block())

        @block.sync
        def _(sp):
            sp.dma_start(const[:, :], consts).then_inc(const_in, 16)
            for n, w in enumerate((w_q, w_k, w_v, w_o, w_x)):
                sp.dma_start(w_nat[:, n, :], w).then_inc(w_in, 16)

            def load_context(u, slot):
                sp.dma_start(c_rows[slot][:, :, :], ctx_in[bass.ds(4 * u, 4)].rearrange("b l e -> l b e")).then_inc(c_in[slot], 16)

            def load_x_all():
                sp.dma_start(x_all[:, :, :], x.rearrange("b t e -> t b e")).then_inc(x_all_in, 16)

            def load_x(n, slot):
                sp.dma_start(xs[slot][:, :, :], x[bass.ds(2 * n, 2)].rearrange("b t e -> t b e")).then_inc(x_in[slot], 16)

            load_context(0, 0)
            load_x(0, 0)
            load_context(1, 1)
            sp.dma_start(gate[:, :], gate_w).then_inc(gate_in, 16)
            load_x(1, 1)
            load_x_all()
            for u in range(2, 4):
                sp.wait_ge(c_turned, u - 1)
                load_context(u, u % 2)

            def rearrange(n, slot, k):
                wait_alone(sp, roped, n + 1)
                if k >= 1:
                    wait_alone(sp, qk_placed[slot], 32 * k)
                sp.dma_start(qk_dram[slot].rearrange("j d t -> (j d) t"), qk_sb[slot][:, :]).then_inc(qk_stored[slot], 16)
                wait_alone(sp, v_rows, n + 1)
                if k >= 1:
                    wait_alone(sp, v_placed[slot], 16 * H * k)
                sp.dma_start(v_dram[slot].rearrange("b t c -> t b c"), v_sb[slot][:, :, :]).then_inc(v_stored[slot], 16)
                wait_alone(sp, qk_stored[slot], 16 * k + 16)
                if k >= 1:
                    wait_alone(sp, score_ps, 4 * (n - 1))
                else:
                    wait_alone(sp, ones_made, 4)
                for b in range(2):
                    sp.dma_start(qk_t[slot][32 * b:32 * b + D, :, :, :].rearrange("d j w t -> d j (w t)"),
                                 qk_dram[slot][:, :, b * 256:(b + 1) * 256].rearrange("j d t -> d j t")).then_inc(qk_placed[slot], 16)
                wait_alone(sp, v_stored[slot], 16 * k + 16)
                if k >= 1:
                    wait_alone(sp, av_ps, 4 * (n - 1))
                for j in range(H):
                    sp.dma_start(v_h[slot][j * TL:(j + 1) * TL, :, :, 0:D],
                                 v_dram[slot][:, :, j * D:(j + 1) * D].rearrange("b (h t) d -> t b h d", h=H)).then_inc(v_placed[slot], 16)

            def store_x2(u, slot):
                wait_alone(sp, x2_made, 2 * u + 2)
                sp.dma_start(x2_dram[bass.ds(2 * u, 2)].rearrange("b t e -> t b e"), x2[slot][:, :, :]).then_inc(x2_stored[slot], 16)

            rearrange(0, 0, 0)
            sp.dma_start(w1_sb[:, :, :], w1s.rearrange("e h i -> h e i")).then_inc(experts_in, 16)
            sp.dma_start(w3_sb[:, :, :], w3s.rearrange("e h i -> h e i")).then_inc(experts_in, 16)
            sp.dma_start(w2_sb[:, :, :, :], w2s.rearrange("e (c p) h -> p e c h", c=C)).then_inc(experts_in, 16)

            def pair(u, slot, k, age, has_next, has_after):
                if has_after:
                    wait_alone(sp, xt_ps, u + 1)
                    load_x(u + 2, slot)
                if has_next:
                    rearrange(u + 1, 1 - slot, k + slot)
                if age >= 2:
                    store_x2(u - 2, slot)

            pair(0, 0, 0, 0, True, True)
            pair(1, 1, 0, 1, True, True)
            with sp.Fori(0, 2) as i:
                pair(2 * i + 2, 0, i + 1, 2, True, True)
                pair(2 * i + 3, 1, i + 1, 3, True, True)
            pair(6, 0, 3, 6, True, False)
            pair(7, 1, 3, 7, False, False)
            store_x2(6, 0)
            store_x2(7, 1)
            sp.wait_ge(x2_stored[0], 16 * 4)
            sp.wait_ge(x2_stored[1], 16 * 4)
            def load_rows(u, slot, k):
                if k is not None:
                    wait_alone(sp, res3_made, 2 * (u - 1))
                for choice in range(2):
                    sp.dma_start(y_rows[slot][:, choice, :, :], y_dram[bass.ds(2 * S * u + choice * ROWS, 2 * S), :].rearrange("(b t) e -> t b e", b=2))\
                      .then_inc(rows_in[slot], 16)
                sp.dma_start(x2_rows[slot][:, :, :], x2_dram[bass.ds(2 * u, 2)].rearrange("b t e -> t b e")).then_inc(rows_in[slot], 16)

            def store_rows(u, slot):
                wait_alone(sp, out_made, 2 * u + 2)
                sp.dma_start(out[bass.ds(2 * u, 2)].rearrange("b t e -> t b e"), out_rows[slot][:, :, :]).then_inc(out_stored[slot], 16)

            sp.wait_ge(scattered[0], 16 * ((SLOTS + 1) // 2))
            sp.wait_ge(scattered[1], 16 * (SLOTS // 2))
            load_rows(0, 0, None)
            load_rows(1, 1, None)
            with sp.Fori(0, PAIRS // 2 - 1) as i:
                for slot in range(2):
                    load_rows(2 * i + 2 + slot, slot, 0)
                    store_rows(2 * i + slot, slot)
            store_rows(PAIRS - 2, 0)
            store_rows(PAIRS - 1, 1)
            sp.wait_ge(out_stored[0], 16 * PAIRS // 2)
            sp.wait_ge(out_stored[1], 16 * PAIRS // 2)

        @block.tensor
        def _(pe):
            pe.wait_ge(const_in, 16)
            pe.wait_ge(w_in, 80)
            for n in range(3):
                mm = pe.transpose(TURN[0][:, n * 128:(n + 1) * 128], w_nat[:, n, :], ident)
            pe.wait_ge(wo_ordered, 1)
            pe.transpose(TURN[1][:, 0:128], wo_rows[:, :, :].rearrange("e j t -> e (j t)"), ident)
            pe.transpose(TURN[1][:, 128:256], w_nat[:, 4, :], ident)
            pe.matmul(TURN[1][:, 256:384], w_nat[:, 4, :], w_nat[:, 4, :], start=True, stop=True).then_inc(w_turned, 1)
            pe.wait_ge(w_copied, 2)

            def context(u, slot, m):
                pe.wait_ge(c_in[slot], 16 * m + 16)
                for b in range(4):
                    mm = pe.transpose(SCORE[slot][:, b * L:(b + 1) * L], c_rows[slot][:, b, :], ident[0:L, 0:L])
                mm.then_inc(c_turned, 1)
                pe.wait_ge(c_copied, u + 1)
                if u >= 1:
                    pe.wait_ge(c_kept, 2 * u)
                for b in range(4):
                    pe.matmul(TURN[0][0:L, b * 128:(b + 1) * 128], c_t[slot][:, b * L:(b + 1) * L], wx_t[:, :], start=True, stop=True)
                pe.matmul(TURN[1][:, 0:4 * L], wx_gram[:, :], c_t[slot][:, :], start=True, stop=True).then_inc(c_made, 1)

            for u in range(4):
                context(u, u % 2, u // 2)
            pe.wait_ge(c_kept, 8)

            def turn_x(n, slot, k, first):
                if first:
                    if n >= 1:
                        pe.wait_ge(v_rows, n)
                else:
                    pe.wait_ge(res2_made, 2 * (n - 2))
                pe.wait_ge(x_in[slot], 16 * k + 16)
                for b in range(2):
                    mm = pe.transpose(MIX_A[:, b * 128:(b + 1) * 128], xs[slot][:, b, :], ident)
                mm.then_inc(xt_ps, 1)

            def project(n, slot, rotated, age):
                pe.wait_ge(xt_sb, n + 1)
                if age >= 1:
                    pe.wait_ge(y_added, 2 * (n - 1) - 1 + rotated)
                bank = (PROJ, PROJ_ROT)[rotated]
                pe.matmul(bank[:, 0:256], w_proj[:, rotated, :], x_t[slot][:, :], start=True, stop=True)
                pe.matmul(bank[:, 256:512], w_proj[:, 2 + rotated, :], x_t[slot][:, :], start=True, stop=True).then_inc(qk_ps, 1)

            def project_v(n, slot):
                pe.wait_ge(xt_sb, n + 1)
                for b in range(2):
                    mm = pe.matmul(MIX_B[:, b * 128:(b + 1) * 128], x_t[slot][:, b * 128:(b + 1) * 128], w_proj[:, 4, :], start=True, stop=True)
                mm.then_inc(v_ps, 1)

            def scores(u, slot, k, g, first):
                G = 4 * u + g
                if g == 0:
                    pe.wait_ge(qk_placed[slot], 32 * k + 32)
                    pe.wait_ge(q_ordered, u + 1)
                if not (first and g < 2):
                    pe.wait_ge(exped, G - 1)
                for h in range(4):
                    head, rows = (g % 2) * 4 + h, slice(32 * (g // 2), 32 * (g // 2) + D)
                    mm = pe.matmul(SCORE[g % 2][:, h * 128:(h + 1) * 128], q_t[slot][rows, head, :, :].rearrange("d j t -> d (j t)"),
                                   qk_t[slot][rows, :, 1, head * TL:(head + 1) * TL], start=True, stop=True)
                mm.then_inc(score_ps, 1)

            def turn_e(u, g, first):
                G = 4 * u + g
                pe.wait_ge(exped, G + 1)
                if not (first and g < 2):
                    pe.wait_ge(et_sb, G - 1)
                for h in range(4):
                    mm = pe.transpose(TURN[g % 2][:, h * 128:(h + 1) * 128], e_sb[g % 2][:, h, :], ident)
                mm.then_inc(et_ps, 1)

            def times_v(u, slot, k, g, first):
                G, b = 4 * u + g, g // 2
                if g == 0:
                    pe.wait_ge(v_placed[slot], 16 * H * (k + 1))
                pe.wait_ge(et_sb, G + 1)
                if not (first and g == 0):
                    pe.wait_ge(av_copied, G)
                for h in range(4):
                    mm = pe.matmul(AV[32 * h:32 * (h + 1), :], v_h[slot][:, b, (g % 2) * 4 + h, :], e_t[g % 2][:, h, :], start=True, stop=True)
                mm.then_inc(av_ps, 1)

            def turn_av(u, g, projected=None, last=False):
                G = 4 * u + g
                if g == 0:
                    pe.wait_ge(rope_parts, 2 * projected)
                    if last:
                        pe.wait_ge(y_added, 2 * u)
                pe.wait_ge(av_copied, G + 1)
                pe.transpose(AV_T[g // 2][:, 128 * (g % 2):128 * (g % 2 + 1)], av_sb[g % 2][:, :], ident).then_inc(avt_ps, 1)

            def mix_rows(u, b):
                pe.wait_ge(o_made, 2 * u + b + 1)
                pe.matmul(Y[b], wo_t[:, :], o_sb[b][:, :], start=True, stop=True).then_inc(y_ps, 1)

            def cross_turn(u, slot, rows_of_v, turned):
                pe.wait_ge(v_rows, rows_of_v)
                if turned is not None:
                    pe.wait_ge(x2t_sb, turned)
                pe.wait_ge(x1_made, 2 * u + 2)
                for b in range(2):
                    mm = pe.transpose(MIX_A[:, b * 128:(b + 1) * 128], x1[slot][:, b, :], ident)
                mm.then_inc(x1t_ps, 1)

            def cross_scores(u):
                pe.wait_ge(x1t_sb, u + 1)
                for b in range(2):
                    to = MIX_B[:, b * L:(b + 1) * L]
                    pe.matmul(to, x1_t[:, b * 128:(b + 1) * 128], xkk_all[:, bass.ds((2 * u + b) * L, L)], start=True, stop=False)
                    mm = pe.matmul(to, ident16[:, :], mask16[:, b, :], start=False, stop=True)
                mm.then_inc(xscore_ps, 1)

            def cross_turn_e(u):
                pe.wait_ge(xexped, u + 1)
                for b in range(2):
                    mm = pe.transpose(MIX_A[0:L, b * 128:(b + 1) * 128], xe_sb[:, b, :], ident)
                mm.then_inc(xet_ps, 1)

            def cross_times_v(u):
                pe.wait_ge(xet_sb, u + 1)
                for b in range(2):
                    mm = pe.matmul(MIX_B[:, b * 128:(b + 1) * 128], xe_t[:, b * 128:(b + 1) * 128],
                                   xk_all[:, bass.ds(2 * u + b, 1), :].rearrange("l b e -> l (b e)"), start=True, stop=True)
                mm.then_inc(xo_ps, 1)

            def turn_x2(u, slot, rows_of_v, last=False):
                pe.wait_ge(v_rows, rows_of_v)
                if last:
                    pe.wait_ge(res2_made, 2 * u + 2)
                pe.wait_ge(x2_made, 2 * u + 2)
                for b in range(2):
                    mm = pe.transpose(MIX_A[:, b * 128:(b + 1) * 128], x2[slot][:, b, :], ident)
                mm.then_inc(x2t_ps, 1)

            def route(u):
                pe.wait_ge(x2t_sb, u + 1)
                for b in range(2):
                    mm = pe.matmul(LOGITS[:, b * NE:(b + 1) * NE], x2_t[:, b * 128:(b + 1) * 128], gate[:, :], start=True, stop=True)
                mm.then_inc(logit_ps, 1)

            turn_x(0, 0, 0, True)
            project(0, 0, 0, 0)
            project(0, 0, 1, 0)
            project_v(0, 0)
            pe.wait_ge(gate_in, 16)

            def pair(u, slot, k, age, has_next):
                first = age == 0
                scores(u, slot, k, 0, first)
                if age >= 1:
                    turn_av(u - 1, 3)
                if has_next:
                    turn_x(u + 1, 1 - slot, k + slot, age < 2)
                scores(u, slot, k, 1, first)
                if has_next:
                    project(u + 1, 1 - slot, 0, age)
                if age >= 1:
                    mix_rows(u - 1, 1)
                if has_next:
                    project_v(u + 1, 1 - slot)
                    project(u + 1, 1 - slot, 1, age)
                turn_e(u, 0, first)
                scores(u, slot, k, 2, first)
                turn_e(u, 1, first)
                if age >= 2:
                    turn_x2(u - 2, slot, u + 2 if has_next else u + 1, not has_next)
                scores(u, slot, k, 3, first)
                times_v(u, slot, k, 0, first)
                if age >= 1:
                    cross_turn(u - 1, 1 - slot, u + 2 if has_next else u + 1, None if age < 2 else u - 1)
                turn_e(u, 2, first)
                if age >= 1:
                    cross_scores(u - 1)
                turn_av(u, 0, u + 2 if has_next else u + 1, not has_next)
                times_v(u, slot, k, 1, first)
                turn_e(u, 3, first)
                if age >= 1:
                    cross_turn_e(u - 1)
                if age >= 2:
                    route(u - 2)
                turn_av(u, 1)
                times_v(u, slot, k, 2, first)
                if age >= 1:
                    cross_times_v(u - 1)
                mix_rows(u, 0)
                turn_av(u, 2)
                times_v(u, slot, k, 3, first)

            pair(0, 0, 0, 0, True)
            pair(1, 1, 0, 1, True)
            with pe.Fori(0, 2) as i:
                pair(2 * i + 2, 0, i + 1, 2, True)
                pair(2 * i + 3, 1, i + 1, 3, True)
            pair(6, 0, 3, 6, True)
            pair(7, 1, 3, 7, False)
            turn_av(7, 3)
            mix_rows(7, 1)
            turn_x2(6, 0, 8, True)
            cross_turn(7, 1, 8, 7)
            cross_scores(7)
            cross_turn_e(7)
            cross_times_v(7)
            pe.wait_ge(y_added, 2 * PAIRS)
            route(6)
            turn_x2(7, 1, 8, True)
            pe.wait_ge(logit_sb, PAIRS - 1)
            route(7)

            pe.wait_ge(ones_set, 1)
            pe.wait_ge(route_step, EITHER_AT)
            chosen_cols = either[:, :, :].rearrange("t b e -> t (b e)")
            pe.matmul(TOTAL, chosen_cols, ones[:, :], start=True, stop=True).then_inc(total_ps, 1)
            pe.matmul(PLACE, table["before"], chosen_cols, start=True, stop=False)
            pe.wait_ge(totals_sb, 1)
            pe.matmul(PLACE, totals[:, :], table["same_before"], start=False, stop=True)
            pe.matmul(COUNT, totals[:, :], table["same"], start=True, stop=True).then_inc(place_ps, 1)
            for choice in range(2):
                for b in range(B):
                    n = choice * B + b
                    pe.wait_ge(hot_made, 2 * n + 2)
                    mm = pe.matmul(TABLE[:, choice * SLOTS:(choice + 1) * SLOTS], row_is[:, n % 4, :], tile_is[:, n % 4, :],
                                   start=(b == 0), stop=(b == B - 1))
                    mm.then_inc(hot_used, 1)

            def turn_rows(s, ring, k):
                pe.wait_ge(gathered[ring], 16 * k + 16)
                pe.transpose(XG_T, xg[ring][:, :], ident).then_inc(xgt_ps, 1)

            def hidden(s, slot, expert, to, w_sb, done):
                mm = pe.matmul(to[slot][:, :], xg_t[slot][:, :], w_sb[:, bass.ds(expert, 1), :].rearrange("h a i -> h (a i)"), start=True, stop=True)
                mm.then_inc(done, 1)

            def down(s, slot, expert, first):
                pe.wait_ge(innert_sb, s + 1)
                if not first:
                    pe.wait_ge(yslot_sb, s)
                for c in range(C):
                    mm = pe.matmul(Y_SLOT, inner_t[slot][:, c, :], w2_sb[:, bass.ds(expert, 1), c, :].rearrange("i a h -> i (a h)"),
                                   start=(c == 0), stop=(c == C - 1))
                mm.then_inc(yslot_ps, 1)

            def turn_inner(s, slot):
                pe.wait_ge(inner_made, s + 1)
                for c in range(C):
                    mm = pe.transpose(INNER_T[slot][:, c * 128:(c + 1) * 128], inner[slot][:, c * 128:(c + 1) * 128], ident)
                mm.then_inc(innert_ps, 1)

            def tile(s, ring, k, age, expert, expert_before, has_next):
                slot = ring % 2
                pe.wait_ge(xgt_sb, s + 1)
                hidden(s, slot, expert, HID1, w1_sb, hid1_ps)
                hidden(s, slot, expert, HID3, w3_sb, hid3_ps)
                if has_next:
                    turn_rows(s + 1, (ring + 1) % RING, k + (ring + 1) // RING)
                if age >= 2:
                    down(s - 2, slot, expert_before, age < 3)
                if age >= 1:
                    turn_inner(s - 1, 1 - slot)

            def tiles_from(s, k, count, age, before, last=False):
                experts = list(before)
                for n in range(count):
                    experts.append(pe.value_load(expert_of[0:1, bass.ds(s + n, 1)], min_val=0, max_val=NE - 1))
                    tile(s + n, n, k, min(age + n, RING), experts[-1], experts[-3], not (last and n == count - 1))
                return experts[-2:]

            pe.wait_ge(lists_made, 1)
            pe.wait_ge(experts_in, 48)
            turn_rows(0, 0, 0)
            held = [pe.alloc_register(f"expert_before{n}") for n in range(2)]

            def hold(experts):
                for register, expert in zip(held, experts):
                    pe.reg_mov(register, expert)

            def experts_held():
                return [pe.snap(bass.RuntimeValue.of_register_unchecked(r)).with_bounds(min_val=0, max_val=NE - 1) for r in held]

            hold(tiles_from(0, 0, RING, 0, [None, None]))
            with pe.Fori(0, RUNS) as i:
                hold(tiles_from(RING * i + RING, i + 1, RING, RING, experts_held()))
            experts = tiles_from(LAST_FROM, RUNS + 1, SLOTS - LAST_FROM, RING, experts_held(), True)
            down(SLOTS - 2, (SLOTS - 2) % 2, experts[0], False)
            turn_inner(SLOTS - 1, (SLOTS - 1) % 2)
            down(SLOTS - 1, (SLOTS - 1) % 2, experts[1], False)

        @block.scalar
        def _(act):
            act.wait_ge(w_turned, 1)
            act.copy(wo_t[:, :], TURN[1][:, 0:128])
            act.copy(wx_t[:, :], TURN[1][:, 128:256])
            act.copy(wx_gram[:, :], TURN[1][:, 256:384]).then_inc(w_copied, 1)

            def context(u, slot):
                act.wait_ge(c_turned, u + 1)
                act.copy(c_t[slot][:, :], SCORE[slot][:, 0:4 * L]).then_inc(c_copied, 1)
                act.wait_ge(c_made, u + 1)
                act.copy(xk_all[:, bass.ds(4 * u, 4), :], TURN[0][0:L, :].rearrange("l (b e) -> l b e", b=4)).then_inc(c_kept, 1)

            for u in range(4):
                context(u, u % 2)

            def copy_x_t(n, slot):
                act.wait_ge(xt_ps, n + 1)
                act.copy(x_t[slot][:, :], MIX_A).then_inc(xt_sb, 1)

            def copy_v(n, slot, k):
                act.wait_ge(v_ps, n + 1)
                if k is not None:
                    act.wait_ge(v_stored[slot], 16 * k)
                act.copy(v_sb[slot][:, :, :], MIX_B.rearrange("t (b c) -> t b c", b=2)).then_inc(v_rows, 1)

            def exp(u, g, first):
                G = 4 * u + g
                act.wait_ge(bias_made, G + 1)
                if not (first and g < 2):
                    act.wait_ge(et_ps, G - 1)
                for h in range(4):
                    last = act.activation(e_sb[g % 2][:, h, :], SCORE[g % 2][:, h * 128:(h + 1) * 128], ACT.Exp,
                                          bias=less_top[g % 2][:, h:h + 1], scale=HEAD_SCALE)
                last.then_inc(exped, 1)

            def copy_e_t(u, g, first):
                G = 4 * u + g
                act.wait_ge(et_ps, G + 1)
                if not (first and g < 2):
                    act.wait_ge(av_ps, G - 1)
                act.copy(e_t[g % 2][:, :, :], TURN[g % 2][:, :].rearrange("k (h q) -> k h q", h=4)).then_inc(et_sb, 1)

            def cross_copy_x1(u):
                act.wait_ge(x1t_ps, u + 1)
                act.copy(x1_t[:, :], MIX_A).then_inc(x1t_sb, 1)

            def cross_exp(u):
                act.wait_ge(xbias_made, u + 1)
                for b in range(2):
                    last = act.activation(xe_sb[:, b, :], MIX_B[:, b * L:(b + 1) * L], ACT.Exp, bias=xless_top[:, b:b + 1], scale=CROSS_SCALE)
                last.then_inc(xexped, 1)

            def cross_copy_e(u):
                act.wait_ge(xet_ps, u + 1)
                act.copy(xe_t[:, :], MIX_A[0:L, :]).then_inc(xet_sb, 1)

            def copy_x2_t(u):
                act.wait_ge(x2t_ps, u + 1)
                act.copy(x2_t[:, :], MIX_A).then_inc(x2t_sb, 1)

            def order_q(n, slot, k):
                act.wait_ge(qk_placed[slot], 32 * k + 32)
                act.copy(q_t[slot][:, :, :, :], qk_t[slot][:, :, 0, :].rearrange("d j (h t) -> d h j t", h=H)).then_inc(q_ordered, 1)

            copy_x_t(0, 0)
            copy_v(0, 0, None)
            order_q(0, 0, 0)

            def copy_av(u, g, first):
                G = 4 * u + g
                act.wait_ge(av_ps, G + 1)
                if not (first and g < 2):
                    act.wait_ge(avt_ps, G - 1)
                act.copy(av_sb[g % 2][:, :], AV).then_inc(av_copied, 1)

            def pair(u, slot, k, age, has_next):
                first = age == 0
                if has_next:
                    copy_x_t(u + 1, 1 - slot)
                exp(u, 0, first)
                exp(u, 1, first)
                if has_next:
                    copy_v(u + 1, 1 - slot, None if first else k + slot)
                copy_e_t(u, 0, first)
                copy_e_t(u, 1, first)
                if age >= 2:
                    copy_x2_t(u - 2)
                exp(u, 2, first)
                copy_av(u, 0, first)
                if age >= 1:
                    cross_copy_x1(u - 1)
                exp(u, 3, first)
                copy_e_t(u, 2, first)
                if age >= 1:
                    cross_exp(u - 1)
                copy_av(u, 1, first)
                copy_e_t(u, 3, first)
                if age >= 1:
                    cross_copy_e(u - 1)
                copy_av(u, 2, first)
                if has_next:
                    order_q(u + 1, 1 - slot, k + slot)
                copy_av(u, 3, first)

            pair(0, 0, 0, 0, True)
            pair(1, 1, 0, 1, True)
            with act.Fori(0, 2) as i:
                pair(2 * i + 2, 0, i + 1, 2, True)
                pair(2 * i + 3, 1, i + 1, 3, True)
            pair(6, 0, 3, 6, True)
            pair(7, 1, 3, 7, False)
            copy_x2_t(6)
            cross_copy_x1(7)
            cross_exp(7)
            cross_copy_e(7)
            copy_x2_t(7)

            act.wait_ge(route_step, 2)
            act.activation(prob[:, :, :], l_less[:, :, :], ACT.Exp).then_inc(route_exp, 1)
            act.wait_ge(total_ps, 1)
            act.copy(totals[:, :], TOTAL).then_inc(totals_sb, 1)

            def copy_rows(s, slot):
                act.wait_ge(xgt_ps, s + 1)
                act.copy(xg_t[slot][:, :], XG_T).then_inc(xgt_sb, 1)

            def copy_inner(s, slot, age):
                act.wait_ge(innert_ps, s + 1)
                if age >= 2:
                    act.wait_ge(yslot_ps, s - 1)
                act.copy(inner_t[slot][:, :, :], INNER_T[slot][:, :].rearrange("i (c t) -> i c t", c=C)).then_inc(innert_sb, 1)

            def tile(s, slot, age, has_next):
                act.wait_ge(hid1_ps, s + 1)
                if age >= 2:
                    act.wait_ge(inner_made, s - 1)
                act.activation(gated[slot][:, :], HID1[slot][:, :], ACT.Silu).then_inc(gated_made, 1)
                if has_next:
                    copy_rows(s + 1, 1 - slot)
                if age >= 1:
                    copy_inner(s - 1, 1 - slot, age - 1)

            copy_rows(0, 0)
            for s in range(4):
                tile(s, s % 2, s, True)
            with act.Fori(0, (SLOTS - 5) // 2) as i:
                tile(2 * i + 4, 0, 4, True)
                tile(2 * i + 5, 1, 5, True)
            tile(SLOTS - 1, 0, 4, False)
            copy_inner(SLOTS - 1, 0, 4)

            def normalise3(u, slot, stored):
                act.wait_ge(rstd3_made, u + 1)
                if stored is not None:
                    act.wait_ge(out_stored[slot], stored)
                for b in range(2):
                    act.activation(out_rows[slot][:, b, :], res3[slot][:, b, :], ACT.Identity, bias=shift3[slot][:, b:b + 1],
                                   scale=rstd3[slot][:, b:b + 1]).then_inc(out_made, 1)

            normalise3(0, 0, None)
            normalise3(1, 1, None)
            with act.Fori(0, PAIRS // 2 - 1) as i:
                for slot in range(2):
                    normalise3(2 * i + 2 + slot, slot, 16 * (i + 1))

        @block.vector
        def _(dve):
            dve.wait_ge(w_in, 80)
            dve.tensor_copy(wo_rows[:, :, :], w_nat[:, 3, :].rearrange("e (t j) -> e j t", j=H)).then_inc(wo_ordered, 1)
            dve.wait_ge(w_turned, 1)
            for w, n in ((0, 0), (2, 1), (4, 2)):
                dve.tensor_copy(w_proj[:, w, :], TURN[0][:, n * 128:(n + 1) * 128])
            for w, n in ((1, 0), (3, 1)):
                pairs_of = w_proj[:, w, :].rearrange("e (i two) -> e i two", two=2)
                turned = TURN[0][:, n * 128:(n + 1) * 128].rearrange("e (i two) -> e i two", two=2)
                dve.tensor_scalar(pairs_of[:, :, 0:1], turned[:, :, 1:2], -1.0, None, ALU.mult)
                last = dve.tensor_copy(pairs_of[:, :, 1:2], turned[:, :, 0:1])
            last.then_inc(w_copied, 1)
            for slot in range(2):
                dve.memset(v_h[slot][:, :, :, D + 1:], 0.0)
                dve.memset(v_h[slot][:, :, :, D:D + 1], 1.0).then_inc(ones_made, 1)
                dve.memset(qk_t[slot][:, :, :, :], 0.0).then_inc(ones_made, 1)
            for u in range(4):
                dve.wait_ge(c_made, u + 1)
                dve.tensor_copy(xkk_all[:, 4 * L * u:4 * L * (u + 1)], TURN[1][:, 0:4 * L]).then_inc(c_kept, 1)

            def rope(n, slot, k):
                for m, (part, ps, table) in enumerate(((cos_part, PROJ, rope_cos), (sin_part, PROJ_ROT, rope_sin))):
                    dve.wait_ge(qk_ps, 2 * n + 1 + m)
                    dve.tensor_tensor(part[slot][:, :].rearrange("c (h t) -> c h t", t=TL), ps[:, :].rearrange("c (h t) -> c h t", t=TL),
                                      table.rearrange("c (o t) -> c o t", o=1).to_broadcast([128, 512 // TL, TL]), ALU.mult).then_inc(rope_parts, 1)
                dve.wait_ge(rope_parts, 2 * n + 2)
                if k is not None:
                    dve.wait_ge(qk_stored[slot], 16 * k)
                total, cos, sin = [p[slot][:, :] for p in (qk_sb, cos_part, sin_part)]
                dve.tensor_tensor(total.rearrange("c (b w t) -> c w b t", b=2, w=2), cos.rearrange("c (w b t) -> c w b t", b=2, w=2),
                                  sin.rearrange("c (w b t) -> c w b t", b=2, w=2), ALU.add).then_inc(roped, 1)

            def maximum(u, g, first):
                G = 4 * u + g
                s = SCORE[g % 2][:, :].rearrange("q (h k) -> q h k", h=4)
                dve.wait_ge(score_ps, G + 1)
                dve.tensor_reduce(top[g % 2][:, :], s, AXIS_X, ALU.max).then_inc(top_found, 1)
                dve.wait_ge(top_found, G + 1)
                dve.tensor_scalar(less_top[g % 2][:, :], top[g % 2][:, :], -HEAD_SCALE, None, ALU.mult).then_inc(bias_made, 1)

            def keep_logits(u):
                dve.wait_ge(logit_ps, u + 1)
                dve.tensor_copy(logits[:, bass.ds(2 * u, 2), :], LOGITS.rearrange("t (b e) -> t b e", b=2)).then_inc(logit_sb, 1)

            def normalise_heads(u, b, first, routed=None):
                N = 2 * u + b
                dve.wait_ge(avt_ps, 4 * u + 2 * b + 2)
                if routed is not None:
                    keep_logits(routed)
                av = AV_T[b].rearrange("q (h c) -> q h c", h=H)
                dve.reciprocal(o_rcp[:, :].rearrange("q (h o) -> q h o", o=1), av[:, :, D:D + 1]).then_inc(rcp_made, 1)
                dve.wait_ge(rcp_made, N + 1)
                if not first:
                    dve.wait_ge(y_ps, N - 1)
                dve.tensor_tensor(o_sb[b][:, :].rearrange("q (h c) -> q h c", h=H), av[:, :, 0:D],
                                  o_rcp[:, :].rearrange("q (h o) -> q h o", o=1).to_broadcast([128, H, D]), ALU.mult).then_inc(o_made, 1)

            def norm1(u, slot, b, first):
                N = 2 * u + b
                dve.wait_ge(y_ps, N + 1)
                dve.tensor_tensor(res1[:, b, :], Y[b], x_all[:, bass.ds(N, 1), :].rearrange("t b e -> t (b e)"), ALU.add).then_inc(y_added, 1)
                dve.wait_ge(y_added, N + 1)
                dve.bn_stats(stats1[:, b, :], res1[:, b, :]).then_inc(stats1_made, 1)
                wait_alone(dve, stats1_made, N + 1)
                dve.bn_aggr(mv1[:, b, :], stats1[:, b, :]).then_inc(mv1_made, 1)
                dve.wait_ge(mv1_made, N + 1)
                dve.tensor_scalar(var1[:, b:b + 1], mv1[:, b, 1:2], EPS, None, ALU.add).then_inc(var1_made, 1)

            def apply1(u, slot, b, first):
                dve.wait_ge(rstd1_made, 2 * u + b + 1)
                if not first:
                    dve.wait_ge(x1t_ps, u - 1)
                dve.tensor_scalar(x1[slot][:, b, :], res1[:, b, :], mv1[:, b, 0:1], rstd1[:, b:b + 1], ALU.subtract, ALU.mult).then_inc(x1_made, 1)

            def cross_maximum(u, first):
                s = MIX_B[:, 0:2 * L].rearrange("q (b k) -> q b k", b=2)
                dve.wait_ge(xscore_ps, u + 1)
                dve.tensor_reduce(xtop[:, :], s, AXIS_X, ALU.max).then_inc(xtop_found, 1)
                dve.wait_ge(xtop_found, u + 1)
                dve.tensor_scalar(xless_top[:, :], xtop[:, :], -CROSS_SCALE, None, ALU.mult).then_inc(xbias_made, 1)

            def cross_sum(u):
                dve.wait_ge(xexped, u + 1)
                dve.tensor_reduce(xsum[:, :], xe_sb[:, :, :], AXIS_X, ALU.add).then_inc(xsum_step, 1)
                dve.wait_ge(xsum_step, 2 * u + 1)
                dve.reciprocal(xrcp[:, :], xsum[:, :]).then_inc(xsum_step, 1)

            def norm2(u, slot):
                dve.wait_ge(xo_ps, u + 1)
                dve.wait_ge(xsum_step, 2 * u + 2)
                dve.wait_ge(x1_made, 2 * u + 2)
                for b in range(2):
                    dve.scalar_tensor_tensor(out=res2[:, b, :], in0=MIX_B[:, b * 128:(b + 1) * 128], scalar=xrcp[:, b:b + 1], in1=x1[slot][:, b, :],
                                             op0=ALU.mult, op1=ALU.add).then_inc(res2_made, 1)
                for b in range(2):
                    dve.wait_ge(res2_made, 2 * u + b + 1)
                    dve.bn_stats(stats2[:, b, :], res2[:, b, :]).then_inc(stats2_made, 1)
                for b in range(2):
                    wait_alone(dve, stats2_made, 2 * u + b + 1)
                    dve.bn_aggr(mv2[:, b, :], stats2[:, b, :]).then_inc(mv2_made, 1)
                dve.wait_ge(mv2_made, 2 * u + 2)
                dve.tensor_scalar(var2[:, :].rearrange("t (b o) -> t b o", o=1), mv2[:, :, 1:2], EPS, None, ALU.add).then_inc(var2_made, 1)

            def apply2(u, slot, k, first):
                dve.wait_ge(rstd2_made, u + 1)
                if not first:
                    dve.wait_ge(x2_stored[slot], 16 * k)
                    dve.wait_ge(x2t_ps, u - 1)
                for b in range(2):
                    dve.tensor_scalar(x2[slot][:, b, :], res2[:, b, :], mv2[:, b, 0:1], rstd2[:, b:b + 1], ALU.subtract, ALU.mult).then_inc(x2_made, 1)

            rope(0, 0, None)
            dve.wait_ge(x_all_in, 16)

            def pair(u, slot, k, age, has_next):
                first = age == 0
                maximum(u, 0, first)
                if age >= 1:
                    normalise_heads(u - 1, 1, age < 2)
                maximum(u, 1, first)
                if age >= 1:
                    norm1(u - 1, 1 - slot, 1, age < 2)
                if has_next:
                    rope(u + 1, 1 - slot, k + slot if age >= 1 else None)
                if age >= 2:
                    apply2(u - 2, slot, k - 1, age < 4)
                maximum(u, 2, first)
                if age >= 1:
                    apply1(u - 1, 1 - slot, 0, age < 3)
                    apply1(u - 1, 1 - slot, 1, age < 3)
                maximum(u, 3, first)
                if age >= 1:
                    cross_maximum(u - 1, False)
                    cross_sum(u - 1)
                normalise_heads(u, 0, first, u - 2 if age >= 2 else None)
                if age >= 1:
                    norm2(u - 1, 1 - slot)
                norm1(u, slot, 0, first)

            for u in range(4):
                pair(u, u % 2, u // 2, u, True)
            with dve.Fori(0, 1) as i:
                pair(2 * i + 4, 0, i + 2, 4, True)
                pair(2 * i + 5, 1, i + 2, 5, True)
            pair(6, 0, 3, 6, True)
            pair(7, 1, 3, 7, False)
            normalise_heads(7, 1, False)
            norm1(7, 1, 1, False)
            apply1(7, 1, 0, False)
            apply1(7, 1, 1, False)
            apply2(6, 0, 3, False)
            cross_maximum(7, False)
            cross_sum(7)
            norm2(7, 1)
            keep_logits(6)
            apply2(7, 1, 3, False)
            keep_logits(7)

            dve.memset(ones[:, :], 1.0).then_inc(ones_set, 1)
            def step(instruction):
                instruction.then_inc(route_step, 1)
            def spread(a, shape):
                return a.to_broadcast(shape)

            dve.wait_ge(logit_sb, PAIRS)
            step(dve.tensor_reduce(l_top[:, :], logits[:, :, :], AXIS_X, ALU.max))
            dve.wait_ge(route_step, 1)
            step(dve.tensor_tensor(l_less[:, :, :], logits[:, :, :], spread(l_top[:, :].rearrange("t (b o) -> t b o", o=1), [128, B, NE]), ALU.subtract))
            theirs = spread(logits[:, :, :].rearrange("t b (o f) -> t b o f", o=1), [128, B, NE, NE])
            own = spread(logits[:, :, :].rearrange("t b (e o) -> t b e o", o=1), [128, B, NE, NE])
            step(dve.tensor_tensor(tied[:, :, :, :], theirs, own, ALU.is_equal))
            step(dve.tensor_tensor(above[:, :, :, :], theirs, own, ALU.is_gt))
            dve.wait_ge(route_step, 4)
            step(dve.tensor_tensor(tied[:, :, :, :].rearrange("t b e f -> t b (e f)"), tied[:, :, :, :].rearrange("t b e f -> t b (e f)"),
                                   spread(table["lower"].rearrange("t (o c) -> t o c", o=1), [128, B, NE * NE]), ALU.mult))
            dve.wait_ge(route_step, 5)
            step(dve.tensor_tensor(above[:, :, :, :], above[:, :, :, :], tied[:, :, :, :], ALU.add))
            dve.wait_ge(route_step, 6)
            step(dve.tensor_reduce(rank[:, :, :], above[:, :, :, :], AXIS_X, ALU.add))
            dve.wait_ge(route_step, 7)
            step(dve.tensor_scalar(either[:, :, :], rank[:, :, :], 2.0, None, ALU.is_lt))
            step(dve.tensor_scalar(chosen[0][:, :, :], rank[:, :, :], 0.0, None, ALU.is_equal))
            step(dve.tensor_scalar(chosen[1][:, :, :], rank[:, :, :], 1.0, None, ALU.is_equal))
            dve.wait_ge(route_exp, 1)
            step(dve.tensor_reduce(p_sum[:, :], prob[:, :, :], AXIS_X, ALU.add))
            dve.wait_ge(route_step, 11)
            step(dve.reciprocal(l_top[:, :], p_sum[:, :]))
            dve.wait_ge(route_step, 12)
            step(dve.tensor_tensor(prob[:, :, :], prob[:, :, :], spread(l_top[:, :].rearrange("t (b o) -> t b o", o=1), [128, B, NE]), ALU.mult))
            dve.wait_ge(route_step, 13)
            for c in range(2):
                step(dve.tensor_tensor(product[c][:, :, :], chosen[c][:, :, :], prob[:, :, :], ALU.mult))
            for c in range(2):
                dve.wait_ge(route_step, 14 + c)
                step(dve.tensor_reduce(share[:, c, :], product[c][:, :, :], AXIS_X, ALU.add))
            dve.wait_ge(route_step, 17)
            step(dve.tensor_tensor(share_sum[:, :], share[:, 0, :], share[:, 1, :], ALU.add))
            dve.wait_ge(route_step, 18)
            step(dve.reciprocal(p_sum[:, :], share_sum[:, :]))
            dve.wait_ge(route_step, 19)
            step(dve.tensor_tensor(share[:, :, :], share[:, :, :], spread(p_sum[:, :].rearrange("t (o b) -> t o b", o=1), [128, 2, B]), ALU.mult))
            dve.wait_ge(place_ps, 1)
            step(dve.tensor_tensor(more_rows[:, :, :], spread(COUNT.rearrange("t (e o) -> t e o", o=1), [128, NE, EXPERT_TILES]),
                                   spread(table["tile_rows"].rearrange("t (o m) -> t o m", o=1), [128, NE, EXPERT_TILES]), ALU.is_gt))
            dve.wait_ge(route_step, 21)
            step(dve.tensor_reduce(tiles[:, :], more_rows[:, :, :], AXIS_X, ALU.add))
            dve.wait_ge(route_step, 22)
            step(dve.tensor_tensor(tiles_before[:, :, :], spread(tiles[:, :].rearrange("t (o f) -> t o f", o=1), [128, NE, NE]),
                                   table["lower"].rearrange("t (e f) -> t e f", e=NE), ALU.mult))
            dve.wait_ge(route_step, 23)
            step(dve.tensor_reduce(start[:, :], tiles_before[:, :, :], AXIS_X, ALU.add))
            dve.wait_ge(route_step, 24)
            step(dve.tensor_scalar(start_rows[:, :], start[:, :], 128.0, None, ALU.mult))
            step(dve.tensor_tensor(tile_end[:, :], start[:, :], tiles[:, :], ALU.add))
            dve.wait_ge(route_step, 26)
            step(dve.tensor_tensor(place[:, :, :], PLACE.rearrange("t (b e) -> t b e", b=B), spread(start_rows[:, :].rearrange("t (o e) -> t o e", o=1), [128, B, NE]), ALU.add))
            dve.wait_ge(route_step, 27)
            for c in range(2):
                step(dve.tensor_tensor(product[2 + c][:, :, :], chosen[c][:, :, :], place[:, :, :], ALU.mult))
            for c in range(2):
                dve.wait_ge(route_step, 28 + c)
                step(dve.tensor_reduce(dest[:, c, :], product[2 + c][:, :, :], AXIS_X, ALU.add))
            dve.wait_ge(route_step, 31)
            step(dve.tensor_copy(dest_i[:, :, :], dest[:, :, :]))
            dve.wait_ge(route_step, 32)
            step(dve.tensor_scalar(dest_tile_i[:, :, :], dest_i[:, :, :], 7, None, ALU.arith_shift_right))
            step(dve.tensor_scalar(dest_row_i[:, :, :], dest_i[:, :, :], 127, None, ALU.bitwise_and))
            dve.wait_ge(route_step, 34)
            step(dve.tensor_copy(dest_tile[:, :, :], dest_tile_i[:, :, :]))
            step(dve.tensor_copy(dest_row[:, :, :], dest_row_i[:, :, :]))
            dve.wait_ge(route_step, 36)
            for c in range(2):
                for b in range(B):
                    n = c * B + b
                    if n >= 4:
                        dve.wait_ge(hot_used, n - 3)
                    dve.tensor_scalar(row_is[:, n % 4, :], table["iota"], dest_row[:, c, b:b + 1], None, ALU.is_equal).then_inc(hot_made, 1)
                    dve.tensor_scalar(tile_is[:, n % 4, :], table["iota"][:, 0:SLOTS], dest_tile[:, c, b:b + 1], table["token"][:, b:b + 1],
                                      ALU.is_equal, ALU.mult).then_inc(hot_made, 1)
            step(dve.tensor_tensor(past[:, :, :], spread(table["iota"][:, 0:SLOTS].rearrange("t (s o) -> t s o", o=1), [128, SLOTS, NE]),
                                   spread(tile_end[:, :].rearrange("t (o e) -> t o e", o=1), [128, SLOTS, NE]), ALU.is_ge))
            dve.wait_ge(route_step, 37)
            step(dve.tensor_reduce(expert_f[:, :], past[:, :, :], AXIS_X, ALU.add))
            dve.wait_ge(route_step, 38)
            step(dve.tensor_scalar(expert_of[:, :], expert_f[:, :], float(NE - 1), None, ALU.min))
            dve.wait_ge(hot_used, 2 * B)
            step(dve.tensor_copy(taken[:, :, :], TABLE.rearrange("p (c s) -> p c s", c=2)))
            dve.wait_ge(route_step, 40)
            step(dve.tensor_tensor(number[:, :], taken[:, 0, :], taken[:, 1, :], ALU.add))
            step(dve.tensor_scalar(is_second[:, :], taken[:, 1, :], 0.0, float(ROWS), ALU.is_gt, ALU.mult))
            dve.wait_ge(route_step, 42)
            step(dve.tensor_scalar(number_in[:, :], number[:, :], -1.0, 0.0, ALU.add, ALU.max))
            step(dve.tensor_scalar(is_empty[:, :], number[:, :], 0.0, None, ALU.is_equal))
            step(dve.tensor_tensor(number[:, :], number[:, :], is_second[:, :], ALU.add))
            dve.wait_ge(route_step, 45)
            step(dve.tensor_copy(from_row[:, :], number_in[:, :]))
            step(dve.tensor_tensor(is_empty[:, :], is_empty[:, :], table["spare"], ALU.mult))
            dve.wait_ge(route_step, 47)
            step(dve.tensor_tensor(number_out[:, :], number[:, :], is_empty[:, :], ALU.add))
            dve.wait_ge(route_step, 48)
            dve.tensor_scalar(to_row[:, :], number_out[:, :], -1.0, None, ALU.add).then_inc(lists_made, 1)

            def product_of(s, slot, age):
                dve.wait_ge(hid3_ps, s + 1)
                dve.wait_ge(gated_made, s + 1)
                if age >= 2:
                    dve.wait_ge(innert_ps, s - 1)
                dve.tensor_tensor(inner[slot][:, :], gated[slot][:, :], HID3[slot][:, :], ALU.mult).then_inc(inner_made, 1)

            def keep_y(s, slot, k):
                dve.wait_ge(yslot_ps, s + 1)
                if k is not None:
                    dve.wait_ge(scattered[slot], 16 * k)
                dve.tensor_copy(y_sb[slot][:, :], Y_SLOT).then_inc(yslot_sb, 1)

            def tile(s, slot, k, age):
                product_of(s, slot, age)
                if age >= 2:
                    keep_y(s - 2, slot, None if age < 4 else k - 1)

            for s in range(4):
                tile(s, s % 2, s // 2, s)
            with dve.Fori(0, (SLOTS - 5) // 2) as i:
                tile(2 * i + 4, 0, i + 2, 4)
                tile(2 * i + 5, 1, i + 2, 5)
            tile(SLOTS - 1, 0, (SLOTS - 1) // 2, 4)
            keep_y(SLOTS - 2, 1, (SLOTS - 2) // 2)
            keep_y(SLOTS - 1, 0, (SLOTS - 1) // 2)

            def add_rows(u, slot, k, age):
                dve.wait_ge(rows_in[slot], 48 * (k + 1))
                if age >= 2:
                    dve.wait_ge(out_made, 2 * (u - 1))
                for b in range(2):
                    for c, before in ((0, x2_rows), (1, res3)):
                        if c == 1:
                            dve.wait_ge(weighed, 2 * u + b + 1)
                        dve.scalar_tensor_tensor(out=res3[slot][:, b, :], in0=y_rows[slot][:, c, b, :], scalar=share[:, c, bass.ds(2 * u + b, 1)],
                                                 in1=before[slot][:, b, :], op0=ALU.mult, op1=ALU.add).then_inc((weighed, res3_made)[c], 1)
                for b in range(2):
                    dve.wait_ge(res3_made, 2 * u + b + 1)
                    dve.bn_stats(stats3[slot][:, b, :], res3[slot][:, b, :]).then_inc(stats3_made, 1)
                for b in range(2):
                    wait_alone(dve, stats3_made, 2 * u + b + 1)
                    dve.bn_aggr(mv3[slot][:, b, :], stats3[slot][:, b, :]).then_inc(mv3_made, 1)

            add_rows(0, 0, 0, 0)
            add_rows(1, 1, 0, 1)
            with dve.Fori(0, PAIRS // 2 - 1) as i:
                add_rows(2 * i + 2, 0, i + 1, 2)
                add_rows(2 * i + 3, 1, i + 1, 3)

        @block.gpsimd
        def _(pool):
            pool.memset(mask16[:, :, :], 0.0).then_inc(consts_made, 1)
            pool.wait_ge(consts_made, 1)
            pool.affine_select(out=mask16[:, :, :], in_=mask16[:, :, :], compare_op=ALU.is_ge, fill=MASKED, base=0,
                               pattern=[[0, 2], [-1, L]], channel_multiplier=1).then_inc(consts_made, 1)
            pool.memset(exponent[:, :], -0.5).then_inc(consts_made, 1)
            pool.wait_ge(consts_made, 3)
            pool.wait_ge(const_in, 16)
            pool.tensor_copy(ident16[:, :], ident).then_inc(consts_made, 1)

            def root1(u, b):
                pool.wait_ge(var1_made, 2 * u + b + 1)
                pool.tensor_tensor(rstd1[:, b:b + 1], var1[:, b:b + 1], exponent[:, 0:1], ALU.pow).then_inc(rstd1_made, 1)

            def root2(u):
                pool.wait_ge(var2_made, u + 1)
                pool.tensor_tensor(rstd2[:, :], var2[:, :], exponent[:, :], ALU.pow).then_inc(rstd2_made, 1)

            def pair(u, slot, k, age, has_next):
                if age >= 1:
                    root1(u - 1, 1)
                if age >= 1:
                    root2(u - 1)
                root1(u, 0)

            pair(0, 0, 0, 0, True)
            with pool.Fori(0, 3) as i:
                pair(2 * i + 1, 1, i, 1, True)
                pair(2 * i + 2, 0, i + 1, 2, True)
            pair(7, 1, 3, 7, False)
            root1(7, 1)
            root2(7)

            def gather(s, at, age):
                if age >= RING:
                    pool.wait_ge(xgt_ps, s - RING + 1)
                pool.tensor_copy(from_now[at][:, :], from_row[:, bass.ds(s, 1)]).then_inc(from_copied, 1)
                wait_alone(pool, from_copied, s + 1)
                pool.indirect_dma_start(out=xg[at][:, :], out_offset=None, in_=x2_dram.rearrange("b t e -> (b t) e"),
                                        in_offset=bass.IndirectOffsetOnAxis(ap=from_now[at][:, :], axis=0)).then_inc(gathered[at], 16)

            def scatter(s, slot):
                pool.wait_ge(yslot_sb, s + 1)
                pool.tensor_copy(to_now[slot][:, :], to_row[:, bass.ds(s, 1)]).then_inc(to_copied, 1)
                wait_alone(pool, to_copied, s + 1)
                pool.indirect_dma_start(out=y_dram, out_offset=bass.IndirectOffsetOnAxis(ap=to_now[slot][:, :], axis=0),
                                        in_=y_sb[slot][:, :], in_offset=None).then_inc(scattered[slot], 16)

            pool.wait_ge(lists_made, 1)
            pool.wait_ge(x2_stored[0], 16 * PAIRS // 2)
            pool.wait_ge(x2_stored[1], 16 * PAIRS // 2)
            for s in range(RING):
                gather(s, s, s)
            with pool.Fori(0, RUNS) as i:
                for at in range(RING):
                    gather(RING * i + RING + at, at, RING)
                    scatter(RING * i + at, at % 2)
            for s in range(LAST_FROM, SLOTS):
                gather(s, s % RING, RING)
                scatter(s - RING, s % 2)
            for s in range(SLOTS - RING, SLOTS):
                scatter(s, s % 2)

            def layernorm3(u, slot, age):
                wait_alone(pool, mv3_made, 2 * u + 2)
                if age >= 2:
                    wait_alone(pool, out_made, 2 * (u - 1))
                pool.tensor_scalar(var3[slot][:, :].rearrange("t (b o) -> t b o", o=1), mv3[slot][:, :, 1:2], EPS, None, ALU.add).then_inc(pool_step3, 1)
                pool.tensor_scalar(less3[slot][:, :].rearrange("t (b o) -> t b o", o=1), mv3[slot][:, :, 0:1], -1.0, None, ALU.mult).then_inc(pool_step3, 1)
                wait_alone(pool, pool_step3, 3 * u + 2)
                pool.tensor_tensor(rstd3[slot][:, :], var3[slot][:, :], exponent[:, :], ALU.pow).then_inc(pool_step3, 1)
                wait_alone(pool, pool_step3, 3 * u + 3)
                pool.tensor_tensor(shift3[slot][:, :], less3[slot][:, :], rstd3[slot][:, :], ALU.mult).then_inc(rstd3_made, 1)

            layernorm3(0, 0, 0)
            layernorm3(1, 1, 1)
            with pool.Fori(0, PAIRS // 2 - 1) as i:
                layernorm3(2 * i + 2, 0, 2)
                layernorm3(2 * i + 3, 1, 3)


_INS = ["x", "ctx_1024", "L0_attn_W1", "L0_attn_W2", "L0_attn_W3", "L0_attn_Wo", "L0_xattn_Wq",
        "L0_ffn_gate_w", "L0_ffn_w1s", "L0_ffn_w2s", "L0_ffn_w3s"]


def kernel(**inputs):
    import concourse.bacc as bacc
    from concourse.bass_utils import run_bass_kernel_spmd

    nc = bacc.Bacc("TRN2", target_bir_lowering=False, num_devices=1)
    arrays, args = {}, []
    for name in _INS + ["shape_constants"]:
        a = shape_constants() if name == "shape_constants" else np.ascontiguousarray(inputs[name])
        arrays[f"in_{name}"] = a
        args.append(nc.dram_tensor(f"in_{name}", a.shape, mybir.dt.from_np(a.dtype), kind="ExternalInput").ap())
    args.append(nc.dram_tensor("out", (B, S, E), F32, kind="ExternalOutput").ap())
    build(nc, *args)
    got = run_bass_kernel_spmd(nc, [arrays], core_ids=[0])
    return got.results[0]["out"]
```

```python
from contextlib import ExitStack

import numpy as np
import concourse.bass as bass
from concourse import mybir

F32 = mybir.dt.float32
BF16, F16 = mybir.dt.bfloat16, mybir.dt.float16
I32, U32 = mybir.dt.int32, mybir.dt.uint32
ALU = mybir.AluOpType
ACT = mybir.ActivationFunctionType
AXIS_X = mybir.AxisListType.X

B, S, E = 16, 128, 128
H, D = 8, 16
TL = S // H
L = 77
NE, I = 8, 512
C = I // 128
PAIRS = B // 2
QUARTERS = 4
EPS = 1e-5
EITHER_AT = 4
MASKED = 1e30
HEAD_SCALE, CROSS_SCALE = float(H) ** -0.5, float(E) ** -0.5
ROWS = B * S
SLOTS = 2 * ROWS // 128 + NE - 1
EXPERT_TILES = ROWS // 128
Y_ROWS = 2 * ROWS + SLOTS * 128
RING = 4
RUNS = (SLOTS - RING - 1) // RING
LAST_FROM = RING * (RUNS + 1)
COLUMNS = {"cos": TL, "sin": TL, "ident": 128, "before": 128, "same_before": 128, "same": NE, "lower": NE * NE,
           "tile_rows": EXPERT_TILES, "iota": 128, "token": B, "spare": SLOTS}
CONST_COLS = sum(COLUMNS.values())


def shape_constants():
    cos, sin = rope_tables()
    row, col = np.arange(128)[:, None], np.arange(128)[None, :]
    e = np.arange(NE)
    parts = {
        "cos": cos, "sin": sin, "ident": row == col,
        "before": row < col,
        "same_before": (row // NE < col // NE) & (row % NE == col % NE),
        "same": row % NE == e[None, :],
        "lower": np.tile((e[None, :] < e[:, None]).reshape(1, -1), (128, 1)),
        "tile_rows": np.tile(128 * np.arange(EXPERT_TILES)[None, :], (128, 1)),
        "iota": np.tile(col, (128, 1)),
        "token": 128 * np.arange(B)[None, :] + row + 1,
        "spare": 2 * ROWS + 1 + 128 * np.arange(SLOTS)[None, :] + row,
    }
    return np.concatenate([parts[n].astype(np.float32) for n in COLUMNS], axis=1)


def rope_tables():
    inv = (1.0 / np.float32(10000.0) ** (np.arange(0, D, 2, dtype=np.float32) / np.float32(D))).astype(np.float32)
    pos = (np.arange(TL)[None, :] * H + np.arange(H)[:, None]).astype(np.float32)
    ang = pos[:, None, :] * np.repeat(inv, 2)[None, :, None]
    ang = ang.astype(np.float32).reshape(H * D, TL)
    return np.cos(ang), np.sin(ang)


def build(nc, x, ctx_in, w_q, w_k, w_v, w_o, w_x, gate_w, w1s, w2s, w3s, consts, out):
    with ExitStack() as ctx:
        def sb(name, shape, dt=F32):
            return ctx.enter_context(nc.sbuf_tensor(name, shape, dt))

        def sem(name):
            return ctx.enter_context(nc.semaphore(name))

        def two(make, name, *a):
            return [make(f"{name}{n}", *a) for n in range(2)]

        def ring(make, name, *a):
            return [make(f"{name}{n}", *a) for n in range(RING)]

        qk_dram = nc.dram_tensor("qk_dram", (2, H, D, 2 * 2 * S), F32, kind="Internal").ap()
        v_dram = nc.dram_tensor("v_dram", (2, 2, S, E), F32, kind="Internal").ap()
        y_dram = nc.dram_tensor("y_dram", (Y_ROWS, E), F32, kind="Internal").ap()
        x2_dram = nc.dram_tensor("x2_dram", (B, S, E), F32, kind="Internal").ap()

        const = sb("const", [128, CONST_COLS])
        table, at = {}, 0
        for name, width in COLUMNS.items():
            table[name] = const[:, at:at + width]
            at += width
        rope_cos, rope_sin, ident = table["cos"], table["sin"], table["ident"]
        ident16 = sb("ident16", [128, 128], BF16)
        mask16 = sb("mask16", [128, 2, L], BF16)
        exponent = sb("exponent", [128, 2])
        w_nat = sb("w_nat", [128, 5, 128])
        w_proj = sb("w_proj", [128, 5, 128])
        wo_rows = sb("wo_rows", [128, H, TL])
        wo_t = sb("wo_t", [128, 128])
        wx_t = sb("wx_t", [128, 128])
        wx_gram = sb("wx_gram", [128, 128])
        gate = sb("gate", [128, NE])
        c_rows = sb("c_rows", [L, B, 128])
        c_t = two(sb, "c_t", [128, 4 * L])
        xk_all = sb("xk_all", [L, B, 128])
        xkk_all = sb("xkk_all", [128, B * L])
        x_all = sb("x_all", [128, B, 128])
        xs = two(sb, "xs", [128, 2, 128])
        x_t = two(sb, "x_t", [128, 256])
        cos_part = two(sb, "cos_part", [128, 512])
        sin_part = two(sb, "sin_part", [128, 512])
        qk_sb = two(sb, "qk_sb", [128, 512])
        qk_t = two(sb, "qk_t", [32 + D, H, 2, S])
        q_t = two(sb, "q_t", [32 + D, H, H, TL])
        v_sb = two(sb, "v_sb", [128, 2, 128])
        v_h = two(sb, "v_h", [128, 2, H, 2 * D])
        least_score = two(sb, "least_score", [128, 4])
        e_sb = two(sb, "e_sb", [128, 4, 128])
        e_t = two(sb, "e_t", [128, 4, 128])
        av_sb = two(sb, "av_sb", [128, 128])
        o_rcp = sb("o_rcp", [128, H])
        o_sb = two(sb, "o_sb", [128, 128])
        res1 = sb("res1", [128, 2, 128])
        var1, var2 = sb("var1", [128, 2]), sb("var2", [128, 2])
        stats1, mv1, rstd1 = sb("stats1", [128, 2, 6]), sb("mv1", [128, 2, 2]), sb("rstd1", [128, 2])
        x1 = two(sb, "x1", [128, 2, 128])
        x1_t = sb("x1_t", [128, 256])
        xleast, xsum, xrcp = sb("xleast", [128, 2]), sb("xsum", [128, 2]), sb("xrcp", [128, 2])
        xe_sb = sb("xe_sb", [128, 2, L])
        xe_t = sb("xe_t", [L, 256])
        res2 = sb("res2", [128, 2, 128])
        stats2, mv2, rstd2 = sb("stats2", [128, 2, 6]), sb("mv2", [128, 2, 2]), sb("rstd2", [128, 2])
        x2 = two(sb, "x2", [128, 2, 128])
        x2_t = sb("x2_t", [128, 256])
        logits = sb("logits", [128, B, NE])
        ones = sb("ones", [128, 128])
        l_top, l_less, prob, p_sum = sb("l_top", [128, B]), sb("l_less", [128, B, NE]), sb("prob", [128, B, NE]), sb("p_sum", [128, B])
        above, tied, rank = sb("above", [128, B, NE, NE]), sb("tied", [128, B, NE, NE]), sb("rank", [128, B, NE])
        chosen = [sb(name, [128, B, NE]) for name in ("first_choice", "second_choice")]
        either = sb("either", [128, B, NE])
        totals = sb("totals", [128, 128])
        more_rows, tiles, tiles_before = sb("more_rows", [128, NE, EXPERT_TILES]), sb("tiles", [128, NE]), sb("tiles_before", [128, NE, NE])
        start, start_rows, tile_end = sb("start", [128, NE]), sb("start_rows", [128, NE]), sb("tile_end", [128, NE])
        past, expert_f, expert_of = sb("past", [128, SLOTS, NE]), sb("expert_f", [128, SLOTS]), sb("expert_of", [128, SLOTS], I32)
        place, product = sb("place", [128, B, NE]), [sb(f"product{n}", [128, B, NE]) for n in range(4)]
        dest, dest_i = sb("dest", [128, 2, B]), sb("dest_i", [128, 2, B], I32)
        dest_tile_i, dest_row_i = sb("dest_tile_i", [128, 2, B], I32), sb("dest_row_i", [128, 2, B], I32)
        dest_tile, dest_row = sb("dest_tile", [128, 2, B], F16), sb("dest_row", [128, 2, B], F16)
        share, share_sum = sb("share", [128, 2, B]), sb("share_sum", [128, B])
        counting, token16 = sb("counting", [128, 128, B], F16), sb("token16", [128, B], F16)
        row_is = sb("row_is", [128, 2, 128, B], F16)
        tile_is = sb("tile_is", [128, 2, SLOTS, B], F16)
        taken, is_second, is_empty = sb("taken", [128, 2, SLOTS]), sb("is_second", [128, SLOTS]), sb("is_empty", [128, SLOTS])
        number, number_in, number_out = sb("number", [128, SLOTS]), sb("number_in", [128, SLOTS]), sb("number_out", [128, SLOTS])
        from_row, to_row = sb("from_row", [128, SLOTS], U32), sb("to_row", [128, SLOTS], U32)
        from_now, to_now = ring(sb, "from_now", [128, 1], U32), two(sb, "to_now", [128, 1], U32)
        w1_sb, w3_sb = sb("w1_sb", [128, NE, I]), sb("w3_sb", [128, NE, I])
        w2_sb = sb("w2_sb", [128, NE, C, 128])
        xg = ring(sb, "xg", [128, 128])
        xg_t = two(sb, "xg_t", [128, 128])
        gated, inner = two(sb, "gated", [128, I]), two(sb, "inner", [128, I])
        w_now = [t[:, :, :, :].rearrange("t b e f -> t (b e f)").rearrange("h (w i) -> h w i", w=2) for t in (above, tied)]
        y_sb = two(sb, "y_sb", [128, 128])
        y_rows = w1_sb[:, :, :].rearrange("h e i -> h (e i)").rearrange("t (c b e) -> t c b e", c=2, b=B)
        out_rows = w3_sb[:, 0:NE // 2, :].rearrange("h e i -> h (e i)").rearrange("t (b e) -> t b e", b=B)
        stats3, mv3 = two(sb, "stats3", [128, 2, 6]), two(sb, "mv3", [128, 2, 2])
        var3, less3, rstd3, shift3 = [sb(name, [128, B]) for name in ("var3", "less3", "rstd3", "shift3")]

        bank = [ctx.enter_context(nc.psum_tensor(f"bank{n}", [128, 512], F32)) for n in range(8)]
        SCORE = bank[0:2]
        TURN = bank[2:4]
        PROJ, PROJ_ROT, MIX, OUTS = bank[4:8]
        MIX_A, MIX_B = MIX[:, 0:256], MIX[:, 256:512]
        AV = OUTS[:, 0:128]
        AV_T = [PROJ[:, 256:512], PROJ_ROT[:, 256:512]]
        Y = [PROJ[:, 0:128], PROJ_ROT[:, 0:128]]
        LOGITS = PROJ[:, 128:128 + 2 * NE]
        TOTAL, PLACE, COUNT, TABLE = bank[0][:, 0:128], bank[1][:, 0:128], bank[2][:, 0:NE], bank[3][:, 0:2 * SLOTS]
        HID1, HID3, XG_T, Y_SLOT = bank[0:2], bank[2:4], bank[6][:, 0:128], bank[7][:, 0:128]

        var1_made, var2_made = sem("var1_made"), sem("var2_made")
        const_in, w_in, gate_in = sem("const_in"), sem("w_in"), sem("gate_in")
        consts_made, ones_made, wo_ordered = sem("consts_made"), sem("ones_made"), sem("wo_ordered")
        w_turned, w_copied = sem("w_turned"), sem("w_copied")
        c_in = two(sem, "c_in")
        c_turned, c_copied, c_made, c_kept = sem("c_turned"), sem("c_copied"), sem("c_made"), sem("c_kept")
        x_all_in, x_in = sem("x_all_in"), two(sem, "x_in")
        xt_ps, xt_sb = sem("xt_ps"), sem("xt_sb")
        qk_ps, v_ps, rope_parts, roped, v_rows = sem("qk_ps"), sem("v_ps"), sem("rope_parts"), sem("roped"), sem("v_rows")
        qk_stored, qk_placed, q_ordered = two(sem, "qk_stored"), two(sem, "qk_placed"), sem("q_ordered")
        v_stored, v_placed = two(sem, "v_stored"), two(sem, "v_placed")
        score_ps, least_found, exped = sem("score_ps"), sem("least_found"), sem("exped")
        et_ps, et_sb, av_ps, rcp_made, o_made = sem("et_ps"), sem("et_sb"), sem("av_ps"), sem("rcp_made"), sem("o_made")
        av_copied, avt_ps = sem("av_copied"), sem("avt_ps")
        y_ps, y_added, stats1_made, mv1_made, rstd1_made, x1_made = (
            sem("y_ps"), sem("y_added"), sem("stats1_made"), sem("mv1_made"), sem("rstd1_made"), sem("x1_made"))
        x1t_ps, x1t_sb, xscore_ps, xleast_found = sem("x1t_ps"), sem("x1t_sb"), sem("xscore_ps"), sem("xleast_found")
        xexped, xet_ps, xet_sb, xo_ps, xsum_step = sem("xexped"), sem("xet_ps"), sem("xet_sb"), sem("xo_ps"), sem("xsum_step")
        res2_made, stats2_made, mv2_made, rstd2_made, x2_made = (
            sem("res2_made"), sem("stats2_made"), sem("mv2_made"), sem("rstd2_made"), sem("x2_made"))
        x2t_ps, x2t_sb, logit_ps, logit_sb = sem("x2t_ps"), sem("x2t_sb"), sem("logit_ps"), sem("logit_sb")
        x2_stored = two(sem, "x2_stored")
        route_step, route_exp, total_ps, totals_sb, place_ps = sem("route_step"), sem("route_exp"), sem("total_ps"), sem("totals_sb"), sem("place_ps")
        hot_made, table_ps, lists_made, ones_set = sem("hot_made"), sem("table_ps"), sem("lists_made"), sem("ones_set")
        counting_made = sem("counting_made")
        ranks_made, joined = sem("ranks_made"), sem("joined")
        from_made, experts_made, compared_made, pool_step = sem("from_made"), sem("experts_made"), sem("compared_made"), sem("pool_step")
        experts_in, from_copied, to_copied = sem("experts_in"), sem("from_copied"), sem("to_copied")
        gathered, scattered = ring(sem, "gathered"), two(sem, "scattered")
        xgt_ps, xgt_sb, hid1_ps, hid3_ps, gated_made, inner_made = (
            sem("xgt_ps"), sem("xgt_sb"), sem("hid1_ps"), sem("hid3_ps"), sem("gated_made"), sem("inner_made"))
        w_set, yslot_ps, yslot_sb = sem("w_set"), sem("yslot_ps"), sem("yslot_sb")
        x2_back, rows_in = sem("x2_back"), [sem(f"rows_in{q}") for q in range(QUARTERS)]
        weighed, res3_made, stats3_made, mv3_made, var3_made, rstd3_made, shift3_made, out_made, out_stored = [
            sem(name) for name in ("weighed", "res3_made", "stats3_made", "mv3_made", "var3_made", "rstd3_made", "shift3_made", "out_made", "out_stored")]

        def compared(logits_of):
            shape = [128, 2, NE, NE]
            return (logits_of.rearrange("t b (o f) -> t b o f", o=1).to_broadcast(shape), logits_of.rearrange("t b (e o) -> t b e o", o=1).to_broadcast(shape))

        waits_met = {e.engine: sem(f"waits_met_{n}") for n, e in enumerate((nc.sync, nc.vector, nc.gpsimd))}

        def wait_alone(engine, semaphore, value):
            engine.wait_ge(semaphore, value)
            engine.sem_inc(waits_met[engine.engine], 1)

        block = ctx.enter_context(nc.Block())

        @block.sync
        def _(sp):
            sp.dma_start(const[:, :], consts).then_inc(const_in, 16)
            for n, w in enumerate((w_q, w_k, w_v, w_o, w_x)):
                sp.dma_start(w_nat[:, n, :], w).then_inc(w_in, 16)

            def load_x_all():
                sp.dma_start(x_all[:, :, :], x.rearrange("b t e -> t b e")).then_inc(x_all_in, 16)

            def load_x(n, slot):
                sp.dma_start(xs[slot][:, :, :], x[bass.ds(2 * n, 2)].rearrange("b t e -> t b e")).then_inc(x_in[slot], 16)

            load_x(0, 0)
            for part, rows in enumerate((slice(0, 4), slice(4, B))):
                sp.dma_start(c_rows[:, rows, :], ctx_in[rows].rearrange("b l e -> l b e")).then_inc(c_in[part], 16)
            load_x(1, 1)
            load_x_all()
            sp.dma_start(gate[:, :], gate_w).then_inc(gate_in, 16)

            def load_expert(e):
                for to, w in ((w1_sb, w1s), (w3_sb, w3s)):
                    sp.dma_start(to[:, bass.ds(e, 1), :], w[bass.ds(e, 1)].rearrange("e h i -> h e i")).then_inc(experts_in, 16)
                sp.dma_start(w2_sb[:, bass.ds(e, 1), :, :], w2s[bass.ds(e, 1)].rearrange("e (c p) h -> p e c h", c=C)).then_inc(experts_in, 16)

            def rearrange(n, slot, k):
                wait_alone(sp, roped, n + 1)
                if k >= 1:
                    wait_alone(sp, qk_placed[slot], 32 * k)
                sp.dma_start(qk_dram[slot].rearrange("j d t -> (j d) t"), qk_sb[slot][:, :]).then_inc(qk_stored[slot], 16)
                wait_alone(sp, v_rows, n + 1)
                if k >= 1:
                    wait_alone(sp, v_placed[slot], 16 * H * k)
                sp.dma_start(v_dram[slot].rearrange("b t c -> t b c"), v_sb[slot][:, :, :]).then_inc(v_stored[slot], 16)
                wait_alone(sp, qk_stored[slot], 16 * k + 16)
                if k >= 1:
                    wait_alone(sp, score_ps, 4 * (n - 1))
                else:
                    wait_alone(sp, ones_made, 4)
                for b in range(2):
                    sp.dma_start(qk_t[slot][32 * b:32 * b + D, :, :, :].rearrange("d j w t -> d j (w t)"),
                                 qk_dram[slot][:, :, b * 256:(b + 1) * 256].rearrange("j d t -> d j t")).then_inc(qk_placed[slot], 16)
                wait_alone(sp, v_stored[slot], 16 * k + 16)
                if k >= 1:
                    wait_alone(sp, av_ps, 4 * (n - 1))
                for j in range(H):
                    sp.dma_start(v_h[slot][j * TL:(j + 1) * TL, :, :, 0:D],
                                 v_dram[slot][:, :, j * D:(j + 1) * D].rearrange("b (h t) d -> t b h d", h=H)).then_inc(v_placed[slot], 16)

            def store_x2(u, slot):
                wait_alone(sp, x2_made, 2 * u + 2)
                sp.dma_start(x2_dram[bass.ds(2 * u, 2)].rearrange("b t e -> t b e"), x2[slot][:, :, :]).then_inc(x2_stored[slot], 16)

            rearrange(0, 0, 0)

            def pair(u, slot, k, age, has_next, has_after):
                if has_after:
                    wait_alone(sp, xt_ps, u + 1)
                    load_x(u + 2, slot)
                if has_next:
                    rearrange(u + 1, 1 - slot, k + slot)
                if age >= 2:
                    store_x2(u - 2, slot)
                load_expert(u)

            pair(0, 0, 0, 0, True, True)
            pair(1, 1, 0, 1, True, True)
            with sp.Fori(0, 2) as i:
                pair(2 * i + 2, 0, i + 1, 2, True, True)
                pair(2 * i + 3, 1, i + 1, 3, True, True)
            pair(6, 0, 3, 6, True, False)
            pair(7, 1, 3, 7, False, False)
            store_x2(6, 0)
            store_x2(7, 1)
            sp.wait_ge(x2_stored[0], 16 * 4)
            sp.wait_ge(x2_stored[1], 16 * 4)
            sp.wait_ge(y_added, 2 * PAIRS)
            sp.dma_start(x_all[:, :, :], x2_dram.rearrange("b t e -> t b e")).then_inc(x2_back, 16)

            def store_rows(u):
                sp.wait_ge(out_made, 2 * u + 2)
                sp.dma_start(out[2 * u:2 * u + 2].rearrange("b t e -> t b e"), out_rows[:, 2 * u:2 * u + 2, :]).then_inc(out_stored, 16)

            sp.wait_ge(scattered[0], 16 * ((SLOTS + 1) // 2))
            sp.wait_ge(scattered[1], 16 * (SLOTS // 2))
            for q in range(QUARTERS):
                rows = slice(q * B // QUARTERS, (q + 1) * B // QUARTERS)
                for choice in range(2):
                    sp.dma_start(y_rows[:, choice, rows, :], y_dram[choice * ROWS:(choice + 1) * ROWS, :].rearrange("(b t) e -> t b e", b=B)[:, rows, :])\
                      .then_inc(rows_in[q], 16)
            for u in range(PAIRS):
                store_rows(u)
            sp.wait_ge(out_stored, 16 * PAIRS)

        @block.tensor
        def _(pe):
            pe.wait_ge(const_in, 16)
            pe.wait_ge(w_in, 80)
            for n in range(3):
                mm = pe.transpose(TURN[0][:, n * 128:(n + 1) * 128], w_nat[:, n, :], ident)
            pe.wait_ge(wo_ordered, 1)
            pe.transpose(TURN[1][:, 0:128], wo_rows[:, :, :].rearrange("e j t -> e (j t)"), ident)
            pe.transpose(TURN[1][:, 128:256], w_nat[:, 4, :], ident)
            pe.matmul(TURN[1][:, 256:384], w_nat[:, 4, :], w_nat[:, 4, :], start=True, stop=True).then_inc(w_turned, 1)
            pe.wait_ge(w_copied, 2)

            def turn_context(u, slot):
                pe.wait_ge(c_in[min(u, 1)], 16)
                for b in range(4):
                    mm = pe.transpose(SCORE[slot][:, b * L:(b + 1) * L], c_rows[:, 4 * u + b, :], ident[0:L, 0:L])
                mm.then_inc(c_turned, 1)

            def context_keys(u, slot):
                pe.wait_ge(c_copied, u + 1)
                if u >= 1:
                    pe.wait_ge(c_kept, 2 * u)
                for b in range(4):
                    pe.matmul(TURN[0][0:L, b * 128:(b + 1) * 128], c_t[slot][:, b * L:(b + 1) * L], wx_t[:, :], start=True, stop=True)
                pe.matmul(TURN[1][:, 0:4 * L], wx_gram[:, :], c_t[slot][:, :], start=True, stop=True).then_inc(c_made, 1)

            def turn_x(n, slot, k, first):
                if first:
                    if n >= 1:
                        pe.wait_ge(v_rows, n)
                else:
                    pe.wait_ge(res2_made, 2 * (n - 2))
                pe.wait_ge(x_in[slot], 16 * k + 16)
                for b in range(2):
                    mm = pe.transpose(MIX_A[:, b * 128:(b + 1) * 128], xs[slot][:, b, :], ident)
                mm.then_inc(xt_ps, 1)

            def project(n, slot, rotated, age):
                pe.wait_ge(xt_sb, n + 1)
                if age >= 1:
                    pe.wait_ge(y_added, 2 * (n - 1) - 1 + rotated)
                bank = (PROJ, PROJ_ROT)[rotated]
                pe.matmul(bank[:, 0:256], w_proj[:, rotated, :], x_t[slot][:, :], start=True, stop=True)
                pe.matmul(bank[:, 256:512], w_proj[:, 2 + rotated, :], x_t[slot][:, :], start=True, stop=True).then_inc(qk_ps, 1)

            def project_v(n, slot):
                pe.wait_ge(xt_sb, n + 1)
                for b in range(2):
                    mm = pe.matmul(MIX_B[:, b * 128:(b + 1) * 128], x_t[slot][:, b * 128:(b + 1) * 128], w_proj[:, 4, :], start=True, stop=True)
                mm.then_inc(v_ps, 1)

            def scores(u, slot, k, g, first):
                G = 4 * u + g
                if g == 0:
                    pe.wait_ge(qk_placed[slot], 32 * k + 32)
                    pe.wait_ge(q_ordered, u + 1)
                if not (first and g < 2):
                    pe.wait_ge(exped, G - 1)
                for h in range(4):
                    head, rows = (g % 2) * 4 + h, slice(32 * (g // 2), 32 * (g // 2) + D)
                    mm = pe.matmul(SCORE[g % 2][:, h * 128:(h + 1) * 128], q_t[slot][rows, head, :, :].rearrange("d j t -> d (j t)"),
                                   qk_t[slot][rows, :, 1, head * TL:(head + 1) * TL], start=True, stop=True)
                mm.then_inc(score_ps, 1)

            def turn_e(u, g, first):
                G = 4 * u + g
                pe.wait_ge(exped, G + 1)
                if not (first and g < 2):
                    pe.wait_ge(et_sb, G - 1)
                for h in range(4):
                    mm = pe.transpose(TURN[g % 2][:, h * 128:(h + 1) * 128], e_sb[g % 2][:, h, :], ident)
                mm.then_inc(et_ps, 1)

            def times_v(u, slot, k, g, first):
                G, b = 4 * u + g, g // 2
                if g == 0:
                    pe.wait_ge(v_placed[slot], 16 * H * (k + 1))
                pe.wait_ge(et_sb, G + 1)
                if not (first and g == 0):
                    pe.wait_ge(av_copied, G)
                for h in range(4):
                    mm = pe.matmul(AV[32 * h:32 * (h + 1), :], v_h[slot][:, b, (g % 2) * 4 + h, :], e_t[g % 2][:, h, :], start=True, stop=True)
                mm.then_inc(av_ps, 1)

            def turn_av(u, g, projected=None, last=False):
                G = 4 * u + g
                if g == 0:
                    pe.wait_ge(rope_parts, 2 * projected)
                    if last:
                        pe.wait_ge(y_added, 2 * u)
                pe.wait_ge(av_copied, G + 1)
                pe.transpose(AV_T[g // 2][:, 128 * (g % 2):128 * (g % 2 + 1)], av_sb[g % 2][:, :], ident).then_inc(avt_ps, 1)

            def mix_rows(u, b):
                pe.wait_ge(o_made, 2 * u + b + 1)
                pe.matmul(Y[b], wo_t[:, :], o_sb[b][:, :], start=True, stop=True).then_inc(y_ps, 1)

            def cross_turn(u, slot, rows_of_v, turned):
                pe.wait_ge(v_rows, rows_of_v)
                if turned is not None:
                    pe.wait_ge(x2t_sb, turned)
                pe.wait_ge(x1_made, 2 * u + 2)
                for b in range(2):
                    mm = pe.transpose(MIX_A[:, b * 128:(b + 1) * 128], x1[slot][:, b, :], ident)
                mm.then_inc(x1t_ps, 1)

            def cross_scores(u):
                pe.wait_ge(x1t_sb, u + 1)
                for b in range(2):
                    to = MIX_B[:, b * L:(b + 1) * L]
                    pe.matmul(to, x1_t[:, b * 128:(b + 1) * 128], xkk_all[:, bass.ds((2 * u + b) * L, L)], start=True, stop=False)
                    mm = pe.matmul(to, ident16[:, :], mask16[:, b, :], start=False, stop=True)
                mm.then_inc(xscore_ps, 1)

            def cross_turn_e(u):
                pe.wait_ge(xexped, u + 1)
                for b in range(2):
                    mm = pe.transpose(MIX_A[0:L, b * 128:(b + 1) * 128], xe_sb[:, b, :], ident)
                mm.then_inc(xet_ps, 1)

            def cross_times_v(u):
                pe.wait_ge(xet_sb, u + 1)
                for b in range(2):
                    mm = pe.matmul(MIX_B[:, b * 128:(b + 1) * 128], xe_t[:, b * 128:(b + 1) * 128],
                                   xk_all[:, bass.ds(2 * u + b, 1), :].rearrange("l b e -> l (b e)"), start=True, stop=True)
                mm.then_inc(xo_ps, 1)

            def turn_x2(u, slot, rows_of_v, last=False, to=MIX_A):
                pe.wait_ge(v_rows, rows_of_v)
                if last:
                    pe.wait_ge(res2_made, 2 * u + 2)
                pe.wait_ge(x2_made, 2 * u + 2)
                for b in range(2):
                    mm = pe.transpose(to[:, b * 128:(b + 1) * 128], x2[slot][:, b, :], ident)
                mm.then_inc(x2t_ps, 1)

            def route(u):
                pe.wait_ge(x2t_sb, u + 1)
                for b in range(2):
                    mm = pe.matmul(LOGITS[:, b * NE:(b + 1) * NE], x2_t[:, b * 128:(b + 1) * 128], gate[:, :], start=True, stop=True)
                mm.then_inc(logit_ps, 1)

            turn_x(0, 0, 0, True)
            project(0, 0, 0, 0)
            project(0, 0, 1, 0)
            project_v(0, 0)
            turn_context(0, 0)
            for u in range(4):
                if u < 3:
                    turn_context(u + 1, (u + 1) % 2)
                context_keys(u, u % 2)
            pe.wait_ge(c_kept, 8)
            pe.wait_ge(gate_in, 16)

            def pair(u, slot, k, age, has_next):
                first = age == 0
                scores(u, slot, k, 0, first)
                if age >= 1:
                    turn_av(u - 1, 3)
                if has_next:
                    turn_x(u + 1, 1 - slot, k + slot, age < 2)
                scores(u, slot, k, 1, first)
                if has_next:
                    project(u + 1, 1 - slot, 0, age)
                if age >= 1:
                    mix_rows(u - 1, 1)
                if has_next:
                    project_v(u + 1, 1 - slot)
                if has_next:
                    project(u + 1, 1 - slot, 1, age)
                turn_e(u, 0, first)
                scores(u, slot, k, 2, first)
                turn_e(u, 1, first)
                if age >= 2:
                    turn_x2(u - 2, slot, u + 2 if has_next else u + 1, not has_next)
                scores(u, slot, k, 3, first)
                times_v(u, slot, k, 0, first)
                if age >= 1:
                    cross_turn(u - 1, 1 - slot, u + 2 if has_next else u + 1, None if age < 2 else u - 1)
                turn_e(u, 2, first)
                if age >= 1:
                    cross_scores(u - 1)
                turn_av(u, 0, u + 2 if has_next else u + 1, not has_next)
                times_v(u, slot, k, 1, first)
                turn_e(u, 3, first)
                if age >= 1:
                    cross_turn_e(u - 1)
                if age >= 2:
                    route(u - 2)
                turn_av(u, 1)
                times_v(u, slot, k, 2, first)
                if age >= 1:
                    cross_times_v(u - 1)
                mix_rows(u, 0)
                turn_av(u, 2)
                times_v(u, slot, k, 3, first)

            pair(0, 0, 0, 0, True)
            pair(1, 1, 0, 1, True)
            with pe.Fori(0, 2) as i:
                pair(2 * i + 2, 0, i + 1, 2, True)
                pair(2 * i + 3, 1, i + 1, 3, True)
            pair(6, 0, 3, 6, True)
            pair(7, 1, 3, 7, False)
            turn_av(7, 3)
            mix_rows(7, 1)
            cross_turn(7, 1, 8, 6)
            turn_x2(6, 0, 8, to=TURN[0])
            cross_scores(7)
            pe.wait_ge(y_added, 2 * PAIRS)
            route(6)
            cross_turn_e(7)
            cross_times_v(7)
            turn_x2(7, 1, 8, to=TURN[0])
            pe.wait_ge(logit_sb, PAIRS - 1)
            route(7)

            pe.wait_ge(ones_set, 1)
            pe.wait_ge(route_step, EITHER_AT)
            chosen_cols = either[:, :, :].rearrange("t b e -> t (b e)")
            pe.matmul(TOTAL, chosen_cols, ones[:, :], start=True, stop=True).then_inc(total_ps, 1)
            pe.matmul(PLACE, table["before"], chosen_cols, start=True, stop=False)
            pe.wait_ge(totals_sb, 1)
            pe.matmul(PLACE, totals[:, :], table["same_before"], start=False, stop=True)
            pe.matmul(COUNT, totals[:, :], table["same"], start=True, stop=True).then_inc(place_ps, 1)
            for choice in range(2):
                pe.wait_ge(hot_made, 3 * choice + 3)
                for b in range(B):
                    mm = pe.matmul(TABLE[:, choice * SLOTS:(choice + 1) * SLOTS], row_is[:, choice, :, b], tile_is[:, choice, :, b],
                                   start=(b == 0), stop=(b == B - 1))
                mm.then_inc(table_ps, 1)

            def turn_rows(s, ring, k):
                pe.wait_ge(gathered[ring], 16 * k + 16)
                pe.transpose(XG_T, xg[ring][:, :], ident).then_inc(xgt_ps, 1)

            def hidden(slot, to, which, done):
                for c in range(C):
                    cols = slice(c * 128, (c + 1) * 128)
                    mm = pe.matmul(to[slot][:, cols], w_now[slot][:, which, cols], xg_t[slot][:, :], start=True, stop=True)
                mm.then_inc(done, 1)

            def down(s, slot, first):
                expert = pe.value_load(expert_of[0:1, bass.ds(s, 1)], min_val=0, max_val=NE - 1)
                pe.wait_ge(inner_made, s + 1)
                if not first:
                    pe.wait_ge(yslot_sb, s)
                for c in range(C):
                    mm = pe.matmul(Y_SLOT, inner[slot][:, c * 128:(c + 1) * 128], w2_sb[:, bass.ds(expert, 1), c, :].rearrange("i a h -> i (a h)"),
                                   start=(c == 0), stop=(c == C - 1))
                mm.then_inc(yslot_ps, 1)

            def tile(s, ring, k, age, has_next=True):
                slot = ring % 2
                pe.wait_ge(w_set, s + 1)
                pe.wait_ge(xgt_sb, s + 1)
                hidden(slot, HID1, 0, hid1_ps)
                hidden(slot, HID3, 1, hid3_ps)
                if has_next:
                    turn_rows(s + 1, (ring + 1) % RING, k + (ring + 1) // RING)
                if age >= 1:
                    down(s - 1, 1 - slot, age < 2)

            pe.wait_ge(experts_made, 1)
            pe.wait_ge(experts_in, 16 * 3 * NE)
            turn_rows(0, 0, 0)
            for s in range(RING):
                tile(s, s, 0, s)
            with pe.Fori(0, RUNS) as i:
                for at in range(RING):
                    tile(RING * i + RING + at, at, i + 1, RING)
            for s in range(LAST_FROM, SLOTS):
                tile(s, s % RING, s // RING, RING, s < SLOTS - 1)
            down(SLOTS - 1, (SLOTS - 1) % 2, False)

        @block.scalar
        def _(act):
            act.wait_ge(w_turned, 1)
            act.copy(wo_t[:, :], TURN[1][:, 0:128])
            act.copy(wx_t[:, :], TURN[1][:, 128:256])
            act.activation(wx_gram[:, :], TURN[1][:, 256:384], ACT.Identity, scale=-CROSS_SCALE).then_inc(w_copied, 1)

            def copy_context(u, slot):
                act.wait_ge(c_turned, u + 1)
                act.copy(c_t[slot][:, :], SCORE[slot][:, 0:4 * L]).then_inc(c_copied, 1)

            def keep_keys(u):
                act.wait_ge(c_made, u + 1)
                act.copy(xk_all[:, bass.ds(4 * u, 4), :], TURN[0][0:L, :].rearrange("l (b e) -> l b e", b=4)).then_inc(c_kept, 1)

            def copy_x_t(n, slot):
                act.wait_ge(xt_ps, n + 1)
                act.copy(x_t[slot][:, :], MIX_A).then_inc(xt_sb, 1)

            def copy_v(n, slot, k):
                act.wait_ge(v_ps, n + 1)
                if k is not None:
                    act.wait_ge(v_stored[slot], 16 * k)
                act.copy(v_sb[slot][:, :, :], MIX_B.rearrange("t (b c) -> t b c", b=2)).then_inc(v_rows, 1)

            def exp(u, g, first):
                G = 4 * u + g
                act.wait_ge(least_found, G + 1)
                if not (first and g < 2):
                    act.wait_ge(et_ps, G - 1)
                for h in range(4):
                    last = act.activation(e_sb[g % 2][:, h, :], SCORE[g % 2][:, h * 128:(h + 1) * 128], ACT.Exp,
                                          bias=least_score[g % 2][:, h:h + 1], scale=-1.0)
                last.then_inc(exped, 1)

            def copy_e_t(u, g, first):
                G = 4 * u + g
                act.wait_ge(et_ps, G + 1)
                if not (first and g < 2):
                    act.wait_ge(av_ps, G - 1)
                act.copy(e_t[g % 2][:, :, :], TURN[g % 2][:, :].rearrange("k (h q) -> k h q", h=4)).then_inc(et_sb, 1)

            def cross_copy_x1(u):
                act.wait_ge(x1t_ps, u + 1)
                act.copy(x1_t[:, :], MIX_A).then_inc(x1t_sb, 1)

            def cross_exp(u):
                act.wait_ge(xleast_found, u + 1)
                for b in range(2):
                    last = act.activation(xe_sb[:, b, :], MIX_B[:, b * L:(b + 1) * L], ACT.Exp, bias=xleast[:, b:b + 1], scale=-1.0)
                last.then_inc(xexped, 1)

            def cross_copy_e(u):
                act.wait_ge(xet_ps, u + 1)
                act.copy(xe_t[:, :], MIX_A[0:L, :]).then_inc(xet_sb, 1)

            def copy_x2_t(u, turned=MIX_A):
                act.wait_ge(x2t_ps, u + 1)
                act.copy(x2_t[:, :], turned).then_inc(x2t_sb, 1)

            copy_x_t(0, 0)
            copy_v(0, 0, None)
            copy_context(0, 0)
            for u in range(4):
                if u < 3:
                    copy_context(u + 1, (u + 1) % 2)
                keep_keys(u)

            def copy_av(u, g, first):
                G = 4 * u + g
                act.wait_ge(av_ps, G + 1)
                if not (first and g < 2):
                    act.wait_ge(avt_ps, G - 1)
                act.copy(av_sb[g % 2][:, :], AV).then_inc(av_copied, 1)

            def pair(u, slot, k, age, has_next):
                first = age == 0
                if has_next:
                    copy_x_t(u + 1, 1 - slot)
                exp(u, 0, first)
                exp(u, 1, first)
                if has_next:
                    copy_v(u + 1, 1 - slot, None if first else k + slot)
                copy_e_t(u, 0, first)
                copy_e_t(u, 1, first)
                if age >= 2:
                    copy_x2_t(u - 2)
                exp(u, 2, first)
                copy_av(u, 0, first)
                if age >= 1:
                    cross_copy_x1(u - 1)
                exp(u, 3, first)
                copy_e_t(u, 2, first)
                if age >= 1:
                    cross_exp(u - 1)
                copy_av(u, 1, first)
                copy_e_t(u, 3, first)
                if age >= 1:
                    cross_copy_e(u - 1)
                copy_av(u, 2, first)
                copy_av(u, 3, first)

            pair(0, 0, 0, 0, True)
            pair(1, 1, 0, 1, True)
            with act.Fori(0, 2) as i:
                pair(2 * i + 2, 0, i + 1, 2, True)
                pair(2 * i + 3, 1, i + 1, 3, True)
            pair(6, 0, 3, 6, True)
            pair(7, 1, 3, 7, False)
            cross_copy_x1(7)
            copy_x2_t(6, TURN[0][:, 0:256])
            cross_exp(7)
            cross_copy_e(7)
            copy_x2_t(7, TURN[0][:, 0:256])

            act.wait_ge(total_ps, 1)
            act.copy(totals[:, :], TOTAL).then_inc(totals_sb, 1)

            def copy_rows(s, slot):
                act.wait_ge(xgt_ps, s + 1)
                act.copy(xg_t[slot][:, :], XG_T).then_inc(xgt_sb, 1)

            def tile(s, slot, age, has_next=True):
                act.wait_ge(hid1_ps, s + 1)
                if age >= 2:
                    act.wait_ge(inner_made, s - 1)
                act.activation(gated[slot][:, :], HID1[slot][:, :], ACT.Silu).then_inc(gated_made, 1)
                if has_next:
                    copy_rows(s + 1, 1 - slot)

            copy_rows(0, 0)
            act.wait_ge(route_step, 33)
            act.activation(prob[:, :, :], l_less[:, :, :], ACT.Exp).then_inc(route_exp, 1)
            for s in range(RING):
                tile(s, s % 2, s)
            with act.Fori(0, RING * RUNS // 2) as i:
                for slot in range(2):
                    tile(2 * i + RING + slot, slot, RING)
            for s in range(LAST_FROM, SLOTS):
                tile(s, s % 2, RING, s < SLOTS - 1)

            with act.Fori(0, PAIRS) as u:
                act.wait_ge(shift3_made, u + 1)
                for b in range(2):
                    act.activation(out_rows[:, bass.ds(2 * u + b, 1), :].rearrange("t b e -> t (b e)"), x_all[:, bass.ds(2 * u + b, 1), :].rearrange("t b e -> t (b e)"),
                                   ACT.Identity, bias=shift3[:, bass.ds(2 * u + b, 1)], scale=rstd3[:, bass.ds(2 * u + b, 1)]).then_inc(out_made, 1)

        @block.vector
        def _(dve):
            dve.wait_ge(w_in, 80)
            dve.tensor_copy(wo_rows[:, :, :], w_nat[:, 3, :].rearrange("e (t j) -> e j t", j=H)).then_inc(wo_ordered, 1)
            dve.wait_ge(w_turned, 1)
            for w, n in ((2, 1), (4, 2)):
                dve.tensor_copy(w_proj[:, w, :], TURN[0][:, n * 128:(n + 1) * 128])
            dve.tensor_scalar(w_proj[:, 0, :], TURN[0][:, 0:128], -HEAD_SCALE, None, ALU.mult)
            for w, n, factor in ((1, 0, -HEAD_SCALE), (3, 1, 1.0)):
                pairs_of = w_proj[:, w, :].rearrange("e (i two) -> e i two", two=2)
                turned = TURN[0][:, n * 128:(n + 1) * 128].rearrange("e (i two) -> e i two", two=2)
                dve.tensor_scalar(pairs_of[:, :, 0:1], turned[:, :, 1:2], -factor, None, ALU.mult)
                last = dve.tensor_scalar(pairs_of[:, :, 1:2], turned[:, :, 0:1], factor, None, ALU.mult)
            last.then_inc(w_copied, 1)
            def rope_part(n, slot, m):
                part, ps, angles = ((cos_part, PROJ, rope_cos), (sin_part, PROJ_ROT, rope_sin))[m]
                dve.wait_ge(qk_ps, 2 * n + 1 + m)
                dve.tensor_tensor(part[slot][:, :].rearrange("c (h t) -> c h t", t=TL), ps[:, :].rearrange("c (h t) -> c h t", t=TL),
                                  angles.rearrange("c (o t) -> c o t", o=1).to_broadcast([128, 512 // TL, TL]), ALU.mult).then_inc(rope_parts, 1)

            def rope_sum(n, slot, k):
                dve.wait_ge(rope_parts, 2 * n + 2)
                if k is not None:
                    dve.wait_ge(qk_stored[slot], 16 * k)
                total, cos, sin = [p[slot][:, :] for p in (qk_sb, cos_part, sin_part)]
                dve.tensor_tensor(total.rearrange("c (b w t) -> c w b t", b=2, w=2), cos.rearrange("c (w b t) -> c w b t", b=2, w=2),
                                  sin.rearrange("c (w b t) -> c w b t", b=2, w=2), ALU.add).then_inc(roped, 1)

            def order_q(n, slot, k):
                dve.wait_ge(qk_placed[slot], 32 * k + 32)
                dve.tensor_copy(q_t[slot][:, :, :, :], qk_t[slot][:, :, 0, :].rearrange("d j (h t) -> d h j t", h=H)).then_inc(q_ordered, 1)

            def least(u, g):
                G = 4 * u + g
                dve.wait_ge(score_ps, G + 1)
                dve.tensor_reduce(least_score[g % 2][:, :], SCORE[g % 2][:, :].rearrange("q (h k) -> q h k", h=4), AXIS_X, ALU.min).then_inc(least_found, 1)

            def keep_logits(u):
                dve.wait_ge(logit_ps, u + 1)
                dve.tensor_copy(logits[:, bass.ds(2 * u, 2), :], LOGITS.rearrange("t (b e) -> t b e", b=2)).then_inc(logit_sb, 1)

            def compare(u):
                rows = bass.ds(2 * u, 2)
                theirs, own = compared(logits[:, rows, :])
                dve.wait_ge(logit_sb, u + 1)
                dve.tensor_tensor(tied[:, rows, :, :], theirs, own, ALU.is_equal).then_inc(compared_made, 1)
                dve.tensor_tensor(above[:, rows, :, :], theirs, own, ALU.is_gt).then_inc(compared_made, 1)

            def normalise_heads(u, b, first, routed=None):
                N = 2 * u + b
                dve.wait_ge(avt_ps, 4 * u + 2 * b + 2)
                if routed is not None:
                    keep_logits(routed)
                av = AV_T[b].rearrange("q (h c) -> q h c", h=H)
                dve.reciprocal(o_rcp[:, :].rearrange("q (h o) -> q h o", o=1), av[:, :, D:D + 1]).then_inc(rcp_made, 1)
                dve.wait_ge(rcp_made, N + 1)
                if not first:
                    dve.wait_ge(y_ps, N - 1)
                dve.tensor_tensor(o_sb[b][:, :].rearrange("q (h c) -> q h c", h=H), av[:, :, 0:D],
                                  o_rcp[:, :].rearrange("q (h o) -> q h o", o=1).to_broadcast([128, H, D]), ALU.mult).then_inc(o_made, 1)

            def add1(u, b):
                N = 2 * u + b
                dve.wait_ge(y_ps, N + 1)
                dve.tensor_tensor(res1[:, b, :], Y[b], x_all[:, bass.ds(N, 1), :].rearrange("t b e -> t (b e)"), ALU.add).then_inc(y_added, 1)

            def count1(u, b):
                dve.wait_ge(y_added, 2 * u + b + 1)
                dve.bn_stats(stats1[:, b, :], res1[:, b, :]).then_inc(stats1_made, 1)

            def mean1(u, b):
                wait_alone(dve, stats1_made, 2 * u + b + 1)
                dve.bn_aggr(mv1[:, b, :], stats1[:, b, :]).then_inc(mv1_made, 1)

            def variance1(u, b):
                dve.wait_ge(mv1_made, 2 * u + b + 1)
                dve.tensor_scalar(var1[:, b:b + 1], mv1[:, b, 1:2], EPS, None, ALU.add).then_inc(var1_made, 1)

            def apply1(u, slot, b, first):
                dve.wait_ge(rstd1_made, 2 * u + b + 1)
                if not first:
                    dve.wait_ge(x1t_ps, u - 1)
                dve.tensor_scalar(x1[slot][:, b, :], res1[:, b, :], mv1[:, b, 0:1], rstd1[:, b:b + 1], ALU.subtract, ALU.mult).then_inc(x1_made, 1)

            def cross_least(u):
                dve.wait_ge(xscore_ps, u + 1)
                dve.tensor_reduce(xleast[:, :], MIX_B[:, 0:2 * L].rearrange("q (b k) -> q b k", b=2), AXIS_X, ALU.min).then_inc(xleast_found, 1)

            def cross_sum(u):
                dve.wait_ge(xexped, u + 1)
                dve.tensor_reduce(xsum[:, :], xe_sb[:, :, :], AXIS_X, ALU.add).then_inc(xsum_step, 1)
                dve.wait_ge(xsum_step, 2 * u + 1)
                dve.reciprocal(xrcp[:, :], xsum[:, :]).then_inc(xsum_step, 1)

            def add2(u, slot):
                dve.wait_ge(xo_ps, u + 1)
                dve.wait_ge(xsum_step, 2 * u + 2)
                dve.wait_ge(x1_made, 2 * u + 2)
                for b in range(2):
                    dve.scalar_tensor_tensor(out=res2[:, b, :], in0=MIX_B[:, b * 128:(b + 1) * 128], scalar=xrcp[:, b:b + 1], in1=x1[slot][:, b, :],
                                             op0=ALU.mult, op1=ALU.add).then_inc(res2_made, 1)

            def count2(u):
                for b in range(2):
                    dve.wait_ge(res2_made, 2 * u + b + 1)
                    dve.bn_stats(stats2[:, b, :], res2[:, b, :]).then_inc(stats2_made, 1)

            def mean2(u):
                wait_alone(dve, stats2_made, 2 * u + 2)
                for b in range(2):
                    dve.bn_aggr(mv2[:, b, :], stats2[:, b, :]).then_inc(mv2_made, 1)

            def variance2(u):
                dve.wait_ge(mv2_made, 2 * u + 2)
                dve.tensor_scalar(var2[:, :].rearrange("t (b o) -> t b o", o=1), mv2[:, :, 1:2], EPS, None, ALU.add).then_inc(var2_made, 1)

            def apply2(u, slot, k, first):
                dve.wait_ge(rstd2_made, u + 1)
                if not first:
                    dve.wait_ge(x2_stored[slot], 16 * k)
                    dve.wait_ge(x2t_ps, u - 1)
                for b in range(2):
                    dve.tensor_scalar(x2[slot][:, b, :], res2[:, b, :], mv2[:, b, 0:1], rstd2[:, b:b + 1], ALU.subtract, ALU.mult).then_inc(x2_made, 1)

            rope_part(0, 0, 0)
            rope_part(0, 0, 1)
            rope_sum(0, 0, None)
            for u in range(4):
                dve.wait_ge(c_made, u + 1)
                dve.tensor_copy(xkk_all[:, 4 * L * u:4 * L * (u + 1)], TURN[1][:, 0:4 * L]).then_inc(c_kept, 1)
            order_q(0, 0, 0)
            dve.wait_ge(x_all_in, 16)

            def pair(u, slot, k, age, has_next):
                first = age == 0
                least(u, 0)
                if age >= 1:
                    normalise_heads(u - 1, 1, age < 2)
                least(u, 1)
                if age >= 1:
                    add1(u - 1, 1)
                if age >= 2:
                    apply2(u - 2, slot, k - 1, age < 4)
                if age >= 1:
                    count1(u - 1, 1)
                if has_next:
                    rope_part(u + 1, 1 - slot, 0)
                if age >= 1:
                    mean1(u - 1, 1)
                if has_next:
                    rope_part(u + 1, 1 - slot, 1)
                if age >= 1:
                    variance1(u - 1, 1)
                if has_next:
                    rope_sum(u + 1, 1 - slot, k + slot if age >= 1 else None)
                least(u, 2)
                if age >= 1:
                    apply1(u - 1, 1 - slot, 0, age < 3)
                    apply1(u - 1, 1 - slot, 1, age < 3)
                least(u, 3)
                if age >= 1:
                    cross_least(u - 1)
                    cross_sum(u - 1)
                normalise_heads(u, 0, first, u - 2 if age >= 2 else None)
                if has_next:
                    order_q(u + 1, 1 - slot, k + slot)
                if age >= 1:
                    add2(u - 1, 1 - slot)
                add1(u, 0)
                if age >= 1:
                    count2(u - 1)
                count1(u, 0)
                if age >= 1:
                    mean2(u - 1)
                mean1(u, 0)
                if age >= 1:
                    variance2(u - 1)
                variance1(u, 0)
                if age >= 2:
                    compare(u - 2)

            def norm1(u, b):
                add1(u, b)
                count1(u, b)
                mean1(u, b)
                variance1(u, b)

            def norm2(u, slot):
                add2(u, slot)
                count2(u)
                mean2(u)
                variance2(u)

            for u in range(4):
                pair(u, u % 2, u // 2, u, True)
            with dve.Fori(0, 1) as i:
                pair(2 * i + 4, 0, i + 2, 4, True)
                pair(2 * i + 5, 1, i + 2, 5, True)
            pair(6, 0, 3, 6, True)
            pair(7, 1, 3, 7, False)
            normalise_heads(7, 1, False)
            norm1(7, 1)
            apply1(7, 1, 0, False)
            apply1(7, 1, 1, False)
            apply2(6, 0, 3, False)
            cross_least(7)
            keep_logits(6)
            compare(6)
            cross_sum(7)
            norm2(7, 1)
            dve.wait_ge(joined, PAIRS - 1)
            dve.tensor_reduce(rank[:, 0:B - 2, :], above[:, 0:B - 2, :, :], AXIS_X, ALU.add).then_inc(ranks_made, 1)
            apply2(7, 1, 3, False)
            keep_logits(7)

            def step(instruction):
                instruction.then_inc(route_step, 1)
            def spread(a, shape):
                return a.to_broadcast(shape)

            last_pair = slice(2 * PAIRS - 2, 2 * PAIRS)
            compare(PAIRS - 1)
            dve.wait_ge(counting_made, 2)
            dve.wait_ge(compared_made, 2 * PAIRS)
            tied_rows = tied[:, last_pair, :, :].rearrange("t b e f -> t b (e f)")
            step(dve.tensor_tensor(tied_rows, tied_rows, spread(table["lower"].rearrange("t (o c) -> t o c", o=1), [128, 2, NE * NE]), ALU.mult))
            dve.wait_ge(route_step, 1)
            step(dve.tensor_tensor(above[:, last_pair, :, :], above[:, last_pair, :, :], tied[:, last_pair, :, :], ALU.add))
            dve.wait_ge(route_step, 2)
            step(dve.tensor_reduce(rank[:, last_pair, :], above[:, last_pair, :, :], AXIS_X, ALU.add))
            dve.wait_ge(ranks_made, 1)
            dve.wait_ge(route_step, 3)
            step(dve.tensor_scalar(either[:, :, :], rank[:, :, :], 2.0, None, ALU.is_lt))
            step(dve.tensor_scalar(chosen[0][:, :, :], rank[:, :, :], 0.0, None, ALU.is_equal))
            step(dve.tensor_scalar(chosen[1][:, :, :], rank[:, :, :], 1.0, None, ALU.is_equal))
            dve.wait_ge(place_ps, 1)
            step(dve.tensor_tensor(more_rows[:, :, :], spread(COUNT.rearrange("t (e o) -> t e o", o=1), [128, NE, EXPERT_TILES]),
                                   spread(table["tile_rows"].rearrange("t (o m) -> t o m", o=1), [128, NE, EXPERT_TILES]), ALU.is_gt))
            dve.wait_ge(route_step, 7)
            step(dve.tensor_reduce(tiles[:, :], more_rows[:, :, :], AXIS_X, ALU.add))
            dve.wait_ge(route_step, 8)
            step(dve.tensor_tensor(tiles_before[:, :, :], spread(tiles[:, :].rearrange("t (o f) -> t o f", o=1), [128, NE, NE]),
                                   table["lower"].rearrange("t (e f) -> t e f", e=NE), ALU.mult))
            dve.wait_ge(route_step, 9)
            step(dve.tensor_reduce(start[:, :], tiles_before[:, :, :], AXIS_X, ALU.add))
            dve.wait_ge(route_step, 10)
            step(dve.tensor_scalar(start_rows[:, :], start[:, :], 128.0, None, ALU.mult))
            dve.wait_ge(route_step, 11)
            step(dve.tensor_tensor(place[:, :, :], PLACE.rearrange("t (b e) -> t b e", b=B), spread(start_rows[:, :].rearrange("t (o e) -> t o e", o=1), [128, B, NE]), ALU.add))
            dve.wait_ge(route_step, 12)
            for c in range(2):
                step(dve.tensor_tensor(product[c][:, :, :], chosen[c][:, :, :], place[:, :, :], ALU.mult))
            for c in range(2):
                dve.wait_ge(route_step, 13 + c)
                step(dve.tensor_reduce(dest[:, c, :], product[c][:, :, :], AXIS_X, ALU.add))
            dve.wait_ge(route_step, 16)
            step(dve.tensor_copy(dest_i[:, :, :], dest[:, :, :]))
            dve.wait_ge(route_step, 17)
            step(dve.tensor_scalar(dest_tile_i[:, :, :], dest_i[:, :, :], 7, None, ALU.arith_shift_right))
            step(dve.tensor_scalar(dest_row_i[:, :, :], dest_i[:, :, :], 127, None, ALU.bitwise_and))
            dve.wait_ge(route_step, 18)
            step(dve.tensor_copy(dest_tile[:, :, :], dest_tile_i[:, :, :]))
            dve.wait_ge(route_step, 19)
            step(dve.tensor_copy(dest_row[:, :, :], dest_row_i[:, :, :]))
            dve.wait_ge(route_step, 21)
            def of_batches(a, count):
                return a.rearrange("t (o b) -> t o b", o=1).to_broadcast([128, count, B])

            for c in range(2):
                dve.tensor_tensor(tile_is[:, c, :, :], counting[:, 0:SLOTS, :], of_batches(dest_tile[:, c, :], SLOTS), ALU.is_equal).then_inc(hot_made, 1)
                dve.tensor_tensor(row_is[:, c, :, :], counting[:, :, :], of_batches(dest_row[:, c, :], 128), ALU.is_equal).then_inc(hot_made, 1)
                dve.wait_ge(hot_made, 3 * c + 1)
                dve.tensor_tensor(tile_is[:, c, :, :], tile_is[:, c, :, :], of_batches(token16[:, :], SLOTS), ALU.mult).then_inc(hot_made, 1)
            dve.wait_ge(table_ps, 2)
            step(dve.tensor_copy(taken[:, :, :], TABLE.rearrange("p (c s) -> p c s", c=2)))
            dve.wait_ge(route_step, 22)
            step(dve.tensor_tensor(number[:, :], taken[:, 0, :], taken[:, 1, :], ALU.add))
            dve.wait_ge(route_step, 23)
            dve.tensor_scalar(from_row[:, :], number[:, :], -1.0, 0.0, ALU.add, ALU.max).then_inc(from_made, 1)
            step(dve.tensor_tensor(tile_end[:, :], start[:, :], tiles[:, :], ALU.add))
            dve.wait_ge(route_step, 24)
            step(dve.tensor_tensor(past[:, :, :], spread(table["iota"][:, 0:SLOTS].rearrange("t (s o) -> t s o", o=1), [128, SLOTS, NE]),
                                   spread(tile_end[:, :].rearrange("t (o e) -> t o e", o=1), [128, SLOTS, NE]), ALU.is_ge))
            dve.wait_ge(route_step, 25)
            step(dve.tensor_reduce(expert_f[:, :], past[:, :, :], AXIS_X, ALU.add))
            dve.wait_ge(route_step, 26)
            dve.tensor_scalar(expert_of[:, :], expert_f[:, :], float(NE - 1), None, ALU.min).then_inc(experts_made, 1)

            def set_weights(s, slot):
                expert = dve.value_load(expert_of[0:1, bass.ds(s, 1)], min_val=0, max_val=NE - 1)
                for which, w_sb in enumerate((w1_sb, w3_sb)):
                    last = dve.tensor_copy(w_now[slot][:, which, :], w_sb[:, bass.ds(expert, 1), :].rearrange("h a i -> h (a i)"))
                last.then_inc(w_set, 1)

            dve.wait_ge(experts_made, 1)
            dve.wait_ge(experts_in, 16 * 3 * NE)
            set_weights(0, 0)
            set_weights(1, 1)
            step(dve.tensor_scalar(is_second[:, :], taken[:, 1, :], 0.0, float(ROWS), ALU.is_gt, ALU.mult))
            step(dve.tensor_scalar(is_empty[:, :], number[:, :], 0.0, None, ALU.is_equal))
            dve.wait_ge(route_step, 27)
            step(dve.tensor_tensor(number_in[:, :], number[:, :], is_second[:, :], ALU.add))
            dve.wait_ge(route_step, 28)
            step(dve.tensor_tensor(is_empty[:, :], is_empty[:, :], table["spare"], ALU.mult))
            dve.wait_ge(route_step, 30)
            step(dve.tensor_tensor(number_out[:, :], number_in[:, :], is_empty[:, :], ALU.add))
            dve.wait_ge(route_step, 31)
            dve.tensor_scalar(to_row[:, :], number_out[:, :], -1.0, None, ALU.add).then_inc(lists_made, 1)

            step(dve.tensor_reduce(l_top[:, :], logits[:, :, :], AXIS_X, ALU.max))
            dve.wait_ge(route_step, 32)
            step(dve.tensor_tensor(l_less[:, :, :], logits[:, :, :], spread(l_top[:, :].rearrange("t (b o) -> t b o", o=1), [128, B, NE]), ALU.subtract))

            dve.wait_ge(route_exp, 1)
            step(dve.tensor_reduce(p_sum[:, :], prob[:, :, :], AXIS_X, ALU.add))
            dve.wait_ge(route_step, 34)
            step(dve.reciprocal(l_top[:, :], p_sum[:, :]))
            dve.wait_ge(route_step, 35)
            step(dve.tensor_tensor(prob[:, :, :], prob[:, :, :], spread(l_top[:, :].rearrange("t (b o) -> t b o", o=1), [128, B, NE]), ALU.mult))
            dve.wait_ge(route_step, 36)
            for c in range(2):
                step(dve.tensor_tensor(product[c][:, :, :], chosen[c][:, :, :], prob[:, :, :], ALU.mult))
            for c in range(2):
                dve.wait_ge(route_step, 37 + c)
                step(dve.tensor_reduce(share[:, c, :], product[c][:, :, :], AXIS_X, ALU.add))
            dve.wait_ge(route_step, 40)
            step(dve.tensor_tensor(share_sum[:, :], share[:, 0, :], share[:, 1, :], ALU.add))
            dve.wait_ge(route_step, 41)
            step(dve.reciprocal(p_sum[:, :], share_sum[:, :]))
            dve.wait_ge(route_step, 42)
            step(dve.tensor_tensor(share[:, :, :], share[:, :, :], spread(p_sum[:, :].rearrange("t (o b) -> t o b", o=1), [128, 2, B]), ALU.mult))

            def product_of(s, slot):
                dve.wait_ge(hid3_ps, s + 1)
                dve.wait_ge(gated_made, s + 1)
                dve.tensor_tensor(inner[slot][:, :], gated[slot][:, :], HID3[slot][:, :], ALU.mult).then_inc(inner_made, 1)

            def keep_y(s, slot, k):
                dve.wait_ge(yslot_ps, s + 1)
                if k is not None:
                    dve.wait_ge(scattered[slot], 16 * k)
                dve.tensor_copy(y_sb[slot][:, :], Y_SLOT).then_inc(yslot_sb, 1)

            def tile(s, slot, k, age, has_after=True):
                product_of(s, slot)
                if has_after:
                    set_weights(s + 2, slot)
                if age >= 1:
                    keep_y(s - 1, 1 - slot, None if age < 3 else k - 1 + slot)

            for s in range(RING):
                tile(s, s % 2, s // 2, s)
            with dve.Fori(0, RING * RUNS // 2) as i:
                for slot in range(2):
                    tile(2 * i + RING + slot, slot, i + 2, RING)
            for s in range(LAST_FROM, SLOTS):
                tile(s, s % 2, s // 2, RING, s + 2 < SLOTS)
            keep_y(SLOTS - 1, (SLOTS - 1) % 2, (SLOTS - 1) // 2)

            def weigh(u, choice):
                for b in range(2 * u, 2 * u + 2):
                    if choice == 1:
                        dve.wait_ge(weighed, b + 1)
                    dve.scalar_tensor_tensor(out=x_all[:, b, :], in0=y_rows[:, choice, b, :], scalar=share[:, choice, b:b + 1], in1=x_all[:, b, :],
                                             op0=ALU.mult, op1=ALU.add).then_inc((weighed, res3_made)[choice], 1)

            def count3(u):
                for b in range(2):
                    dve.wait_ge(res3_made, 2 * u + b + 1)
                    dve.bn_stats(stats3[u % 2][:, b, :], x_all[:, 2 * u + b, :]).then_inc(stats3_made, 1)

            def mean3(u):
                for b in range(2):
                    dve.wait_ge(stats3_made, 2 * u + b + 1)
                    dve.bn_aggr(mv3[u % 2][:, b, :], stats3[u % 2][:, b, :]).then_inc(mv3_made, 1)

            def variance3(u):
                dve.wait_ge(mv3_made, 2 * u + 2)
                dve.tensor_scalar(var3[:, 2 * u:2 * u + 2].rearrange("t (b o) -> t b o", o=1), mv3[u % 2][:, :, 1:2], EPS, None, ALU.add)
                dve.tensor_scalar(less3[:, 2 * u:2 * u + 2].rearrange("t (b o) -> t b o", o=1), mv3[u % 2][:, :, 0:1], -1.0, None, ALU.mult).then_inc(var3_made, 1)

            dve.wait_ge(x2_back, 16)
            for u in range(PAIRS + 1):
                if u < PAIRS:
                    if u % (PAIRS // QUARTERS) == 0:
                        dve.wait_ge(rows_in[u * QUARTERS // PAIRS], 32)
                    weigh(u, 0)
                if u >= 1:
                    mean3(u - 1)
                if u < PAIRS:
                    weigh(u, 1)
                if u >= 1:
                    variance3(u - 1)
                if u < PAIRS:
                    count3(u)

        @block.gpsimd
        def _(pool):
            for slot in range(2):
                pool.memset(qk_t[slot][:, :, :, :], 0.0).then_inc(ones_made, 1)
                pool.memset(v_h[slot][:, :, :, D + 1:], 0.0)
                pool.memset(v_h[slot][:, :, :, D:D + 1], 1.0).then_inc(ones_made, 1)
            pool.memset(mask16[:, :, :], 0.0).then_inc(consts_made, 1)
            pool.wait_ge(consts_made, 1)
            pool.affine_select(out=mask16[:, :, :], in_=mask16[:, :, :], compare_op=ALU.is_ge, fill=MASKED, base=0,
                               pattern=[[0, 2], [-1, L]], channel_multiplier=1).then_inc(consts_made, 1)
            pool.memset(ones[:, :], 1.0).then_inc(ones_set, 1)
            pool.memset(exponent[:, :], -0.5).then_inc(consts_made, 1)
            pool.wait_ge(consts_made, 3)
            pool.wait_ge(const_in, 16)
            pool.tensor_copy(ident16[:, :], ident).then_inc(consts_made, 1)
            pool.tensor_copy(counting[:, :, :], table["iota"].rearrange("t (c o) -> t c o", o=1).to_broadcast([128, 128, B])).then_inc(counting_made, 1)
            pool.tensor_copy(token16[:, :], table["token"]).then_inc(counting_made, 1)

            def root1(u, b):
                pool.wait_ge(var1_made, 2 * u + b + 1)
                pool.tensor_tensor(rstd1[:, b:b + 1], var1[:, b:b + 1], exponent[:, 0:1], ALU.pow).then_inc(rstd1_made, 1)

            def root2(u):
                pool.wait_ge(var2_made, u + 1)
                pool.tensor_tensor(rstd2[:, :], var2[:, :], exponent[:, :], ALU.pow).then_inc(rstd2_made, 1)

            def join(u):
                rows = bass.ds(2 * u, 2)
                tied_rows = tied[:, rows, :, :].rearrange("t b e f -> t b (e f)")
                wait_alone(pool, compared_made, 2 * u + 2)
                pool.tensor_tensor(tied_rows, tied_rows, table["lower"].rearrange("t (o c) -> t o c", o=1).to_broadcast([128, 2, NE * NE]), ALU.mult).then_inc(pool_step, 1)
                wait_alone(pool, pool_step, u + 1)
                pool.tensor_tensor(above[:, rows, :, :], above[:, rows, :, :], tied[:, rows, :, :], ALU.add).then_inc(joined, 1)

            def pair(u, age):
                if age >= 1:
                    root1(u - 1, 1)
                    root2(u - 1)
                root1(u, 0)
                if age >= 3:
                    join(u - 3)

            for u in range(4):
                pair(u, u)
            with pool.Fori(4, PAIRS) as u:
                pair(u, 4)
            root1(7, 1)
            join(5)
            join(6)
            root2(7)

            def gather(s, at, age):
                if age >= RING:
                    pool.wait_ge(xgt_ps, s - RING + 1)
                pool.tensor_copy(from_now[at][:, :], from_row[:, bass.ds(s, 1)]).then_inc(from_copied, 1)
                wait_alone(pool, from_copied, s + 1)
                pool.indirect_dma_start(out=xg[at][:, :], out_offset=None, in_=x2_dram.rearrange("b t e -> (b t) e"),
                                        in_offset=bass.IndirectOffsetOnAxis(ap=from_now[at][:, :], axis=0)).then_inc(gathered[at], 16)

            def scatter(s, slot):
                pool.wait_ge(yslot_sb, s + 1)
                pool.tensor_copy(to_now[slot][:, :], to_row[:, bass.ds(s, 1)]).then_inc(to_copied, 1)
                wait_alone(pool, to_copied, s + 1)
                pool.indirect_dma_start(out=y_dram, out_offset=bass.IndirectOffsetOnAxis(ap=to_now[slot][:, :], axis=0),
                                        in_=y_sb[slot][:, :], in_offset=None).then_inc(scattered[slot], 16)

            pool.wait_ge(from_made, 1)
            pool.wait_ge(x2_stored[0], 16 * PAIRS // 2)
            pool.wait_ge(x2_stored[1], 16 * PAIRS // 2)
            for s in range(RING):
                gather(s, s, s)
            pool.wait_ge(lists_made, 1)
            with pool.Fori(0, RUNS) as i:
                for at in range(RING):
                    gather(RING * i + RING + at, at, RING)
                    scatter(RING * i + at, at % 2)
            for s in range(LAST_FROM, SLOTS):
                gather(s, s % RING, RING)
                scatter(s - RING, s % 2)
            for s in range(SLOTS - RING, SLOTS):
                scatter(s, s % 2)

            with pool.Fori(0, PAIRS) as u:
                pair_cols = bass.ds(2 * u, 2)
                pool.wait_ge(var3_made, u + 1)
                pool.tensor_tensor(rstd3[:, pair_cols], var3[:, pair_cols], exponent[:, :], ALU.pow).then_inc(rstd3_made, 1)
                wait_alone(pool, rstd3_made, u + 1)
                pool.tensor_tensor(shift3[:, pair_cols], less3[:, pair_cols], rstd3[:, pair_cols], ALU.mult).then_inc(shift3_made, 1)


_INS = ["x", "ctx_1024", "L0_attn_W1", "L0_attn_W2", "L0_attn_W3", "L0_attn_Wo", "L0_xattn_Wq",
        "L0_ffn_gate_w", "L0_ffn_w1s", "L0_ffn_w2s", "L0_ffn_w3s"]


def kernel(**inputs):
    import concourse.bacc as bacc
    from concourse.bass_utils import run_bass_kernel_spmd

    nc = bacc.Bacc("TRN2", target_bir_lowering=False, num_devices=1)
    arrays, args = {}, []
    for name in _INS + ["shape_constants"]:
        a = shape_constants() if name == "shape_constants" else np.ascontiguousarray(inputs[name])
        arrays[f"in_{name}"] = a
        args.append(nc.dram_tensor(f"in_{name}", a.shape, mybir.dt.from_np(a.dtype), kind="ExternalInput").ap())
    args.append(nc.dram_tensor("out", (B, S, E), F32, kind="ExternalOutput").ap())
    build(nc, *args)
    got = run_bass_kernel_spmd(nc, [arrays], core_ids=[0])
    return got.results[0]["out"]
```
